# Optimizing a Trainium2 kernel written in Bass

```python
import numpy as np
import jax
import jax.numpy as jnp

def _softmax(x, axis=-1):
    return jax.nn.softmax(x, axis=axis)

def _gelu(x):
    return jax.nn.gelu(x, approximate=True)

def _silu(x):
    return jax.nn.silu(x)

def _sigmoid(x):
    return jax.nn.sigmoid(x)

def _layernorm(x, axis=-1, eps=1e-05):
    m = jnp.mean(x, axis=axis, keepdims=True)
    v = jnp.var(x, axis=axis, keepdims=True)
    return (x - m) / jnp.sqrt(v + eps)

def _scatter_add(tgt, idx, src, axis=0):
    return tgt.at[idx].add(src)

def _segment_sum(src, seg, n):
    return jax.ops.segment_sum(src, seg, n)
kernel_name = 'mk_metaformer_d4_conv_nchw256_r4_f77283'

def setup_inputs(seed: int=0):
    np.random.seed(seed)
    _w = jnp.asarray

    def _rec_inputs():
        import jax
        import jax.numpy as jnp
        _gk = jax.random.key(seed)
        x = -0.0003929 + 0.9999 * jax.random.normal(jax.random.fold_in(_gk, 1), (16, 64, 16, 16), jnp.float32)
        return x
    x = _rec_inputs()

    def _L0_conv_setup():
        import jax, jax.numpy as jnp
        import numpy as np
        B, C_IN, H, W = (16, 64, 16, 16)
        D_LAT = 64
        K = 1024
        key = jax.random.key(seed)
        k1, k2, k3, k4 = jax.random.split(key, 4)
        z = jax.random.normal(k1, (B, C_IN, H, W), dtype=jnp.float32)
        proj_w = jax.random.normal(k2, (D_LAT, C_IN), dtype=jnp.float32) / np.sqrt(C_IN)
        proj_b = jax.random.normal(k3, (D_LAT,), dtype=jnp.float32) * 0.01
        emb = (jax.random.uniform(k4, (K, D_LAT), dtype=jnp.float32) * 2.0 - 1.0) / K
        return {'z': z, 'proj_w': proj_w, 'proj_b': proj_b, 'emb': emb}
    _L0_conv_all = _L0_conv_setup()
    _L0_conv_in = {k: v for k, v in _L0_conv_all.items() if k in ('proj_w', 'proj_b', 'emb')}
    del _L0_conv_all

    def _L0_ffn_setup():
        import jax, jax.numpy as jnp
        import numpy as np
        B, T, D, H, E = (16, 1024, 64, 128, 8)
        key = jax.random.key(seed)
        ks = jax.random.split(key, 5)
        x = jax.random.normal(ks[0], (B, T, D), dtype=jnp.float32)
        gate_w = jax.random.normal(ks[1], (D, E), dtype=jnp.float32) * 0.02
        gate_b = jnp.zeros((E,), dtype=jnp.float32)
        W1 = jax.random.normal(ks[2], (E, D, H), dtype=jnp.float32) * 0.02
        b1 = jnp.zeros((E, H), dtype=jnp.float32)
        W2 = jax.random.normal(ks[3], (E, H, D), dtype=jnp.float32) * 0.02
        b2 = jnp.zeros((E, D), dtype=jnp.float32)
        return {'x': x, 'gate_w': gate_w, 'gate_b': gate_b, 'W1': W1, 'b1': b1, 'W2': W2, 'b2': b2}
    _L0_ffn_all = _L0_ffn_setup()
    _L0_ffn_in = {k: v for k, v in _L0_ffn_all.items() if k in ('gate_w', 'gate_b', 'W1', 'b1', 'W2', 'b2')}
    del _L0_ffn_all

    def _L1_conv_setup():
        import jax, jax.numpy as jnp
        import numpy as np
        from jax import lax
        DIM = 64
        NUM_HEADS = 8
        HEAD_DIM = DIM // NUM_HEADS
        SCALE = HEAD_DIM ** (-0.5)
        KERNEL_SIZES = [5, 7, 9]
        DILATIONS = [1, 2, 3]
        HEADS_PER_RANGE = [4, 3, 1]
        B, H, W = (2, 16, 16)

        def _unfold(x, ksz, dil, h, hd):
            b, _, hh, ww = x.shape
            p = ksz // 2 * dil
            patches = lax.conv_general_dilated_patches(x, (ksz, ksz), (1, 1), [(p, p), (p, p)], rhs_dilation=(dil, dil))
            return patches.reshape(b, h, hd, ksz * ksz, hh * ww)

        def _forward(x, qkv_params, proj_w, proj_b):
            b, c, hh, ww = x.shape
            hw = hh * ww
            outs = []
            hs = 0
            for i in range(len(KERNEL_SIZES)):
                w_i, b_i = qkv_params[i]
                qkv = jnp.einsum('bchw,oc->bohw', x, w_i) + b_i[None, :, None, None]
                q, k, v = jnp.split(qkv, 3, axis=1)
                h_i = HEADS_PER_RANGE[i]
                he = hs + h_i
                q_r = q.reshape(b, NUM_HEADS, HEAD_DIM, hh, ww)[:, hs:he]
                k_r = k.reshape(b, NUM_HEADS, HEAD_DIM, hh, ww)[:, hs:he]
                v_r = v.reshape(b, NUM_HEADS, HEAD_DIM, hh, ww)[:, hs:he]
                ksz, dil = (KERNEL_SIZES[i], DILATIONS[i])
                k_nb = _unfold(k_r.reshape(b, h_i * HEAD_DIM, hh, ww), ksz, dil, h_i, HEAD_DIM)
                v_nb = _unfold(v_r.reshape(b, h_i * HEAD_DIM, hh, ww), ksz, dil, h_i, HEAD_DIM)
                q_flat = q_r.reshape(b, h_i, HEAD_DIM, hw) * SCALE
                logits = jnp.einsum('bhdp,bhdlp->bhlp', q_flat, k_nb)
                attn = jax.nn.softmax(logits, axis=2)
                out_i = jnp.einsum('bhlp,bhdlp->bhdp', attn, v_nb)
                outs.append(out_i)
                hs = he
            out = jnp.concatenate(outs, axis=1).reshape(b, c, hh, ww)
            out = jnp.einsum('bchw,oc->bohw', out, proj_w) + proj_b[None, :, None, None]
            return out
        key = jax.random.key(seed)
        ks = jax.random.split(key, 9)
        d = {'x': jax.random.normal(ks[0], (B, DIM, H, W), jnp.float32)}
        for i in range(3):
            d[f'qkv_w{i}'] = jax.random.normal(ks[1 + 2 * i], (3 * DIM, DIM), jnp.float32) * 0.02
            d[f'qkv_b{i}'] = jnp.zeros((3 * DIM,), jnp.float32)
        d['proj_w'] = jax.random.normal(ks[7], (DIM, DIM), jnp.float32) * 0.02
        d['proj_b'] = jnp.zeros((DIM,), jnp.float32)
        return d
    _L1_conv_all = _L1_conv_setup()
    _L1_conv_in = {k: v for k, v in _L1_conv_all.items() if k in ('qkv_w0', 'qkv_b0', 'qkv_w1', 'qkv_b1', 'qkv_w2', 'qkv_b2', 'proj_w', 'proj_b')}
    del _L1_conv_all

    def _L1_ffn_setup():
        import jax, jax.numpy as jnp
        import numpy as np
        NUM_EXPERTS = 8
        TOP_K = 2
        B, S, D = (8, 2048, 64)

        def _moe(tokens, router_w, w1, b1, w2, b2):
            N = tokens.shape[0]
            E = router_w.shape[0]
            logits = tokens.astype(jnp.float32) @ router_w.astype(jnp.float32).T
            probs = jax.nn.softmax(logits, axis=-1)
            rw, re = jax.lax.top_k(probs, TOP_K)
            if TOP_K > 1:
                rw = rw / jnp.maximum(rw.sum(-1, keepdims=True), 1e-12)
            rw = rw.astype(tokens.dtype)
            combine = jnp.zeros((N, E), tokens.dtype).at[jnp.arange(N)[:, None], re].set(rw)
            out = tokens
            for e in range(E):
                h = jax.nn.gelu(tokens @ w1[e] + b1[e], approximate=False)
                y = h @ w2[e] + b2[e]
                out = out + combine[:, e:e + 1] * y
            return out
        key = jax.random.key(seed)
        ks = jax.random.split(key, 4)
        scale = 1.0 / np.sqrt(D).astype(np.float32)
        return {'input_embeddings': jax.random.normal(ks[0], (B, S, D), jnp.float32), 'router_w': jax.random.normal(ks[1], (NUM_EXPERTS, D), jnp.float32) * scale, 'w1': jax.random.normal(ks[2], (NUM_EXPERTS, D, D), jnp.float32) * scale, 'b1': jnp.zeros((NUM_EXPERTS, D), jnp.float32), 'w2': jax.random.normal(ks[3], (NUM_EXPERTS, D, D), jnp.float32) * scale, 'b2': jnp.zeros((NUM_EXPERTS, D), jnp.float32)}
    _L1_ffn_all = _L1_ffn_setup()
    _L1_ffn_in = {k: v for k, v in _L1_ffn_all.items() if k in ('router_w', 'w1', 'b1', 'w2', 'b2')}
    del _L1_ffn_all

    def _L2_conv_setup():
        import jax, jax.numpy as jnp
        import numpy as np
        EPS = 1e-08
        key = jax.random.key(seed)
        k1, k2, k3 = jax.random.split(key, 3)
        b, c, h, w = (4, 64, 16, 16)
        x = jax.random.normal(k1, (b, c, h, w), dtype=jnp.float32)
        W = jax.random.normal(k2, (64, 64), dtype=jnp.float32) * (1.0 / np.sqrt(64))
        bias = jax.random.normal(k3, (64,), dtype=jnp.float32) * 0.01
        return {'x': x, 'W': W, 'bias': bias}
    _L2_conv_all = _L2_conv_setup()
    _L2_conv_in = {k: v for k, v in _L2_conv_all.items() if k in ('W', 'bias')}
    del _L2_conv_all

    def _L2_ffn_setup():
        import jax, jax.numpy as jnp
        import numpy as np
        D_MODEL = 64
        N_EXPERTS = 16
        HIDDEN = 128
        SCALE = 0.02
        key = jax.random.key(seed)
        ks = jax.random.split(key, 5)
        x = jax.random.normal(ks[0], (4, 2048, D_MODEL), dtype=jnp.float32)
        gate_w = jax.random.normal(ks[1], (D_MODEL, N_EXPERTS), dtype=jnp.float32) * SCALE
        gate_b = jnp.zeros((N_EXPERTS,), dtype=jnp.float32)
        w1 = jax.random.normal(ks[2], (N_EXPERTS, D_MODEL, HIDDEN), dtype=jnp.float32) * SCALE
        w2 = jax.random.normal(ks[3], (N_EXPERTS, D_MODEL, HIDDEN), dtype=jnp.float32) * SCALE
        w3 = jax.random.normal(ks[4], (N_EXPERTS, HIDDEN, D_MODEL), dtype=jnp.float32) * SCALE
        return {'x': x, 'gate_w': gate_w, 'gate_b': gate_b, 'w1': w1, 'w2': w2, 'w3': w3}
    _L2_ffn_all = _L2_ffn_setup()
    _L2_ffn_in = {k: v for k, v in _L2_ffn_all.items() if k in ('gate_w', 'gate_b', 'w1', 'w2', 'w3')}
    del _L2_ffn_all

    def _L3_conv_setup():
        import jax, jax.numpy as jnp
        import numpy as np
        SHARPNESS = 2
        BN_EPS = 1e-05
        key = jax.random.key(seed)
        k1, k2, k3 = jax.random.split(key, 3)
        b, c, h, w = (32, 64, 48, 48)
        x = jax.random.normal(k1, (b, c, h, w), dtype=jnp.float32)
        conv_w = jax.random.normal(k2, (c, c), dtype=jnp.float32) * (1.0 / np.sqrt(c))
        conv_b = jax.random.normal(k3, (c,), dtype=jnp.float32) * 0.01
        bn_gamma = jnp.ones((c,), dtype=jnp.float32)
        bn_beta = jnp.zeros((c,), dtype=jnp.float32)
        return {'x': x, 'conv_w': conv_w, 'conv_b': conv_b, 'bn_gamma': bn_gamma, 'bn_beta': bn_beta}
    _L3_conv_all = _L3_conv_setup()
    _L3_conv_in = {k: v for k, v in _L3_conv_all.items() if k in ('conv_w', 'conv_b', 'bn_gamma', 'bn_beta')}
    del _L3_conv_all

    def _L3_ffn_setup():
        import jax, jax.numpy as jnp
        import numpy as np
        B, T, D, H, E = (16, 1024, 64, 128, 8)
        key = jax.random.key(seed)
        ks = jax.random.split(key, 5)
        x = jax.random.normal(ks[0], (B, T, D), dtype=jnp.float32)
        gate_w = jax.random.normal(ks[1], (D, E), dtype=jnp.float32) * 0.02
        gate_b = jnp.zeros((E,), dtype=jnp.float32)
        W1 = jax.random.normal(ks[2], (E, D, H), dtype=jnp.float32) * 0.02
        b1 = jnp.zeros((E, H), dtype=jnp.float32)
        W2 = jax.random.normal(ks[3], (E, H, D), dtype=jnp.float32) * 0.02
        b2 = jnp.zeros((E, D), dtype=jnp.float32)
        return {'x': x, 'gate_w': gate_w, 'gate_b': gate_b, 'W1': W1, 'b1': b1, 'W2': W2, 'b2': b2}
    _L3_ffn_all = _L3_ffn_setup()
    _L3_ffn_in = {k: v for k, v in _L3_ffn_all.items() if k in ('gate_w', 'gate_b', 'W1', 'b1', 'W2', 'b2')}
    del _L3_ffn_all
    return {'x': x, 'L0_conv_proj_w': _L0_conv_in['proj_w'], 'L0_conv_proj_b': _L0_conv_in['proj_b'], 'L0_conv_emb': _L0_conv_in['emb'], 'L0_ffn_gate_w': _L0_ffn_in['gate_w'], 'L0_ffn_gate_b': _L0_ffn_in['gate_b'], 'L0_ffn_W1': _L0_ffn_in['W1'], 'L0_ffn_b1': _L0_ffn_in['b1'], 'L0_ffn_W2': _L0_ffn_in['W2'], 'L0_ffn_b2': _L0_ffn_in['b2'], 'L1_conv_qkv_w0': _L1_conv_in['qkv_w0'], 'L1_conv_qkv_b0': _L1_conv_in['qkv_b0'], 'L1_conv_qkv_w1': _L1_conv_in['qkv_w1'], 'L1_conv_qkv_b1': _L1_conv_in['qkv_b1'], 'L1_conv_qkv_w2': _L1_conv_in['qkv_w2'], 'L1_conv_qkv_b2': _L1_conv_in['qkv_b2'], 'L1_conv_proj_w': _L1_conv_in['proj_w'], 'L1_conv_proj_b': _L1_conv_in['proj_b'], 'L1_ffn_router_w': _L1_ffn_in['router_w'], 'L1_ffn_w1': _L1_ffn_in['w1'], 'L1_ffn_b1': _L1_ffn_in['b1'], 'L1_ffn_w2': _L1_ffn_in['w2'], 'L1_ffn_b2': _L1_ffn_in['b2'], 'L2_conv_W': _L2_conv_in['W'], 'L2_conv_bias': _L2_conv_in['bias'], 'L2_ffn_gate_w': _L2_ffn_in['gate_w'], 'L2_ffn_gate_b': _L2_ffn_in['gate_b'], 'L2_ffn_w1': _L2_ffn_in['w1'], 'L2_ffn_w2': _L2_ffn_in['w2'], 'L2_ffn_w3': _L2_ffn_in['w3'], 'L3_conv_conv_w': _L3_conv_in['conv_w'], 'L3_conv_conv_b': _L3_conv_in['conv_b'], 'L3_conv_bn_gamma': _L3_conv_in['bn_gamma'], 'L3_conv_bn_beta': _L3_conv_in['bn_beta'], 'L3_ffn_gate_w': _L3_ffn_in['gate_w'], 'L3_ffn_gate_b': _L3_ffn_in['gate_b'], 'L3_ffn_W1': _L3_ffn_in['W1'], 'L3_ffn_b1': _L3_ffn_in['b1'], 'L3_ffn_W2': _L3_ffn_in['W2'], 'L3_ffn_b2': _L3_ffn_in['b2']}

def reference(x, L0_conv_proj_w, L0_conv_proj_b, L0_conv_emb, L0_ffn_gate_w, L0_ffn_gate_b, L0_ffn_W1, L0_ffn_b1, L0_ffn_W2, L0_ffn_b2, L1_conv_qkv_w0, L1_conv_qkv_b0, L1_conv_qkv_w1, L1_conv_qkv_b1, L1_conv_qkv_w2, L1_conv_qkv_b2, L1_conv_proj_w, L1_conv_proj_b, L1_ffn_router_w, L1_ffn_w1, L1_ffn_b1, L1_ffn_w2, L1_ffn_b2, L2_conv_W, L2_conv_bias, L2_ffn_gate_w, L2_ffn_gate_b, L2_ffn_w1, L2_ffn_w2, L2_ffn_w3, L3_conv_conv_w, L3_conv_conv_b, L3_conv_bn_gamma, L3_conv_bn_beta, L3_ffn_gate_w, L3_ffn_gate_b, L3_ffn_W1, L3_ffn_b1, L3_ffn_W2, L3_ffn_b2):
    import jax
    import jax.numpy as jnp

    def _L0_conv_ref(z, proj_w, proj_b, emb):
        import jax, jax.numpy as jnp
        import numpy as np
        B, C_IN, H, W = (16, 64, 16, 16)
        D_LAT = 64
        K = 1024
        zp = jnp.einsum('bchw,oc->bohw', z, proj_w) + proj_b[None, :, None, None]
        zt = jnp.transpose(zp, (0, 2, 3, 1))
        zf = zt.reshape(-1, D_LAT)
        dist = (zf * zf).sum(-1, keepdims=True) - 2.0 * (zf @ emb.T) + (emb * emb).sum(-1)[None, :]
        idx = jnp.argmin(dist, axis=1)
        z_q = emb[idx].reshape(zt.shape)
        rep = zt + jax.lax.stop_gradient(z_q - zt)
        return jnp.transpose(rep, (0, 3, 1, 2))

    def _L0_ffn_ref(x, gate_w, gate_b, W1, b1, W2, b2):
        import jax, jax.numpy as jnp
        import numpy as np
        B, T, D, H, E = (16, 1024, 64, 128, 8)
        Bb, Tt, Dd = x.shape
        Ee = gate_w.shape[1]
        xf = x.reshape(-1, Dd)
        N = xf.shape[0]
        logits = xf @ gate_w + gate_b
        probs = jax.nn.softmax(logits, axis=-1)
        top2_vals, top2_idx = jax.lax.top_k(probs, 2)
        cw = jnp.zeros((N, Ee), dtype=xf.dtype).at[jnp.arange(N)[:, None], top2_idx].add(top2_vals)

        def step(acc, params):
            w1, bb1, w2, bb2, we = params
            h = jax.nn.gelu(xf @ w1 + bb1, approximate=False)
            y = h @ w2 + bb2
            return (acc + we[:, None] * y, None)
        out, _ = jax.lax.scan(step, jnp.zeros_like(xf), (W1, b1, W2, b2, cw.T))
        return out.reshape(Bb, Tt, Dd)

    def _L1_conv_ref(x, qkv_w0, qkv_b0, qkv_w1, qkv_b1, qkv_w2, qkv_b2, proj_w, proj_b):
        import jax, jax.numpy as jnp
        import numpy as np
        from jax import lax
        DIM = 64
        NUM_HEADS = 8
        HEAD_DIM = DIM // NUM_HEADS
        SCALE = HEAD_DIM ** (-0.5)
        KERNEL_SIZES = [5, 7, 9]
        DILATIONS = [1, 2, 3]
        HEADS_PER_RANGE = [4, 3, 1]
        B, H, W = (2, 16, 16)

        def _unfold(x, ksz, dil, h, hd):
            b, _, hh, ww = x.shape
            p = ksz // 2 * dil
            patches = lax.conv_general_dilated_patches(x, (ksz, ksz), (1, 1), [(p, p), (p, p)], rhs_dilation=(dil, dil))
            return patches.reshape(b, h, hd, ksz * ksz, hh * ww)

        def _forward(x, qkv_params, proj_w, proj_b):
            b, c, hh, ww = x.shape
            hw = hh * ww
            outs = []
            hs = 0
            for i in range(len(KERNEL_SIZES)):
                w_i, b_i = qkv_params[i]
                qkv = jnp.einsum('bchw,oc->bohw', x, w_i) + b_i[None, :, None, None]
                q, k, v = jnp.split(qkv, 3, axis=1)
                h_i = HEADS_PER_RANGE[i]
                he = hs + h_i
                q_r = q.reshape(b, NUM_HEADS, HEAD_DIM, hh, ww)[:, hs:he]
                k_r = k.reshape(b, NUM_HEADS, HEAD_DIM, hh, ww)[:, hs:he]
                v_r = v.reshape(b, NUM_HEADS, HEAD_DIM, hh, ww)[:, hs:he]
                ksz, dil = (KERNEL_SIZES[i], DILATIONS[i])
                k_nb = _unfold(k_r.reshape(b, h_i * HEAD_DIM, hh, ww), ksz, dil, h_i, HEAD_DIM)
                v_nb = _unfold(v_r.reshape(b, h_i * HEAD_DIM, hh, ww), ksz, dil, h_i, HEAD_DIM)
                q_flat = q_r.reshape(b, h_i, HEAD_DIM, hw) * SCALE
                logits = jnp.einsum('bhdp,bhdlp->bhlp', q_flat, k_nb)
                attn = jax.nn.softmax(logits, axis=2)
                out_i = jnp.einsum('bhlp,bhdlp->bhdp', attn, v_nb)
                outs.append(out_i)
                hs = he
            out = jnp.concatenate(outs, axis=1).reshape(b, c, hh, ww)
            out = jnp.einsum('bchw,oc->bohw', out, proj_w) + proj_b[None, :, None, None]
            return out
        qkv_params = [(qkv_w0, qkv_b0), (qkv_w1, qkv_b1), (qkv_w2, qkv_b2)]
        return _forward(x, qkv_params, proj_w, proj_b)

    def _L1_ffn_ref(input_embeddings, router_w, w1, b1, w2, b2):
        import jax, jax.numpy as jnp
        import numpy as np
        NUM_EXPERTS = 8
        TOP_K = 2
        B, S, D = (8, 2048, 64)

        def _moe(tokens, router_w, w1, b1, w2, b2):
            N = tokens.shape[0]
            E = router_w.shape[0]
            logits = tokens.astype(jnp.float32) @ router_w.astype(jnp.float32).T
            probs = jax.nn.softmax(logits, axis=-1)
            rw, re = jax.lax.top_k(probs, TOP_K)
            if TOP_K > 1:
                rw = rw / jnp.maximum(rw.sum(-1, keepdims=True), 1e-12)
            rw = rw.astype(tokens.dtype)
            combine = jnp.zeros((N, E), tokens.dtype).at[jnp.arange(N)[:, None], re].set(rw)
            out = tokens
            for e in range(E):
                h = jax.nn.gelu(tokens @ w1[e] + b1[e], approximate=False)
                y = h @ w2[e] + b2[e]
                out = out + combine[:, e:e + 1] * y
            return out
        b, s, d = input_embeddings.shape
        tokens = input_embeddings.reshape(b * s, d)
        return _moe(tokens, router_w, w1, b1, w2, b2).reshape(b, s, d)

    def _L2_conv_ref(x, W, bias):
        import jax, jax.numpy as jnp
        import numpy as np
        EPS = 1e-08
        b, c, h, w = x.shape
        p = h * w
        xf = x.reshape(b, c, p)
        dots = jnp.einsum('bcp,bcq->bpq', xf, xf)
        norms = jnp.sqrt(jnp.sum(xf * xf, axis=1))
        denom = jnp.maximum(norms[:, :, None] * norms[:, None, :], EPS)
        sim = jnp.square(jax.nn.relu(dots / denom))
        tx = jnp.einsum('oc,bcq->boq', W, xf) + bias[None, :, None]
        out = jnp.einsum('bpq,boq->bop', sim, tx)
        return out.reshape(b, -1, h, w)

    def _L2_ffn_ref(x, gate_w, gate_b, w1, w2, w3):
        import jax, jax.numpy as jnp
        import numpy as np
        D_MODEL = 64
        N_EXPERTS = 16
        HIDDEN = 128
        SCALE = 0.02
        n_experts = w1.shape[0]
        logits = jnp.einsum('bsd,de->bse', x, gate_w) + gate_b
        probs = jax.nn.softmax(logits, axis=-1)
        top_probs, top_idx = jax.lax.top_k(probs, 2)
        top_probs = top_probs / jnp.sum(top_probs, axis=-1, keepdims=True)
        dispatch = jnp.sum(jax.nn.one_hot(top_idx, n_experts, dtype=x.dtype) * top_probs[..., None], axis=-2)
        h1 = jnp.einsum('bsd,edh->bseh', x, w1)
        h2 = jnp.einsum('bsd,edh->bseh', x, w2)
        hidden = jax.nn.silu(h1) * h2
        expert_out = jnp.einsum('bseh,eho->bseo', hidden, w3)
        return jnp.einsum('bseo,bse->bso', expert_out, dispatch)

    def _L3_conv_ref(x, conv_w, conv_b, bn_gamma, bn_beta):
        import jax, jax.numpy as jnp
        import numpy as np
        SHARPNESS = 2
        BN_EPS = 1e-05
        b, c, h, w = x.shape
        hw = h * w
        x_norm = jnp.linalg.norm(x.reshape(b, -1), axis=1).reshape(b, 1, 1)
        x_1 = x.reshape(b, hw, c) / x_norm
        x_2 = x.reshape(b, c, hw) / x_norm
        cos = jnp.einsum('bnc,bcm->bnm', x_1, x_2)
        s = jnp.maximum(cos, 0.0) ** SHARPNESS
        t = jnp.einsum('oc,bchw->bohw', conv_w, x) + conv_b[None, :, None, None]
        mean = t.mean(axis=(0, 2, 3))
        var = t.var(axis=(0, 2, 3))
        t = (t - mean[None, :, None, None]) * jax.lax.rsqrt(var + BN_EPS)[None, :, None, None]
        t = t * bn_gamma[None, :, None, None] + bn_beta[None, :, None, None]
        t = jnp.maximum(t, 0.0)
        tr = t.reshape(b, hw, c)
        y = jnp.einsum('bnm,bmc->bnc', s, tr)
        return y.reshape(b, c, h, w)

    def _L3_ffn_ref(x, gate_w, gate_b, W1, b1, W2, b2):
        import jax, jax.numpy as jnp
        import numpy as np
        B, T, D, H, E = (16, 1024, 64, 128, 8)
        Bb, Tt, Dd = x.shape
        Ee = gate_w.shape[1]
        xf = x.reshape(-1, Dd)
        N = xf.shape[0]
        logits = xf @ gate_w + gate_b
        probs = jax.nn.softmax(logits, axis=-1)
        top2_vals, top2_idx = jax.lax.top_k(probs, 2)
        cw = jnp.zeros((N, Ee), dtype=xf.dtype).at[jnp.arange(N)[:, None], top2_idx].add(top2_vals)

        def step(acc, params):
            w1, bb1, w2, bb2, we = params
            h = jax.nn.gelu(xf @ w1 + bb1, approximate=False)
            y = h @ w2 + bb2
            return (acc + we[:, None] * y, None)
        out, _ = jax.lax.scan(step, jnp.zeros_like(xf), (W1, b1, W2, b2, cw.T))
        return out.reshape(Bb, Tt, Dd)

    def _gn(v, G=32, eps=1e-05):
        B_, C_, H_, W_ = v.shape
        g = v.reshape(B_, G, C_ // G, H_, W_)
        m = jnp.mean(g, axis=(2, 3, 4), keepdims=True)
        s = jnp.var(g, axis=(2, 3, 4), keepdims=True)
        return ((g - m) / jnp.sqrt(s + eps)).reshape(v.shape)

    def _ln_c(v, eps=1e-06):
        m = jnp.mean(v, axis=1, keepdims=True)
        s = jnp.var(v, axis=1, keepdims=True)
        return (v - m) / jnp.sqrt(s + eps)

    def _ln_t(v, eps=1e-05):
        m = jnp.mean(v, axis=-1, keepdims=True)
        s = jnp.var(v, axis=-1, keepdims=True)
        return (v - m) / jnp.sqrt(s + eps)

    def _to_tokens(v):
        B_, C_, H_, W_ = v.shape
        return v.reshape(B_, C_, H_ * W_).transpose(0, 2, 1)

    def _from_tokens(t, like):
        B_, C_, H_, W_ = like.shape
        return t.transpose(0, 2, 1).reshape(B_, C_, H_, W_)
    x = x + _L0_conv_ref(_ln_c(x), L0_conv_proj_w, L0_conv_proj_b, L0_conv_emb)
    t = _to_tokens(x)
    t = t + _L0_ffn_ref(_ln_t(t), L0_ffn_gate_w, L0_ffn_gate_b, L0_ffn_W1, L0_ffn_b1, L0_ffn_W2, L0_ffn_b2)
    x = _from_tokens(t, x)
    x = x + _L1_conv_ref(_ln_c(x), L1_conv_qkv_w0, L1_conv_qkv_b0, L1_conv_qkv_w1, L1_conv_qkv_b1, L1_conv_qkv_w2, L1_conv_qkv_b2, L1_conv_proj_w, L1_conv_proj_b)
    t = _to_tokens(x)
    t = t + _L1_ffn_ref(_ln_t(t), L1_ffn_router_w, L1_ffn_w1, L1_ffn_b1, L1_ffn_w2, L1_ffn_b2)
    x = _from_tokens(t, x)
    x = x + _L2_conv_ref(_ln_c(x), L2_conv_W, L2_conv_bias)
    t = _to_tokens(x)
    t = t + _L2_ffn_ref(_ln_t(t), L2_ffn_gate_w, L2_ffn_gate_b, L2_ffn_w1, L2_ffn_w2, L2_ffn_w3)
    x = _from_tokens(t, x)
    x = x + _L3_conv_ref(_ln_c(x), L3_conv_conv_w, L3_conv_conv_b, L3_conv_bn_gamma, L3_conv_bn_beta)
    t = _to_tokens(x)
    t = t + _L3_ffn_ref(_ln_t(t), L3_ffn_gate_w, L3_ffn_gate_b, L3_ffn_W1, L3_ffn_b1, L3_ffn_W2, L3_ffn_b2)
    x = _from_tokens(t, x)
    return x

_drawn_inputs = setup_inputs


def setup_inputs(seed=0):
    import zlib

    import numpy as np

    out = dict(_drawn_inputs(seed))
    spreads = {'L0_ffn_gate_b': (0.0, 0.1),
     'L0_ffn_b1': (0.0, 0.8),
     'L0_ffn_b2': (0.0, 0.1),
     'L1_conv_qkv_b0': (0.0, 0.322),
     'L1_conv_qkv_b1': (0.0, 0.37),
     'L1_conv_qkv_b2': (0.0, 0.8),
     'L1_conv_proj_b': (0.0, 0.1),
     'L1_ffn_b1': (0.0, 0.29),
     'L1_ffn_b2': (0.0, 0.1),
     'L2_ffn_gate_b': (0.0, 0.8),
     'L3_conv_bn_gamma': (1.0, 0.6),
     'L3_conv_bn_beta': (0.0, 2.0),
     'L3_ffn_gate_b': (0.0, 0.8),
     'L3_ffn_b1': (0.0, 0.8),
     'L3_ffn_b2': (0.0, 0.8)}
    factors = {'L0_conv_proj_w': 8.0,
     'L0_conv_proj_b': 200.0,
     'L0_conv_emb': 8.0,
     'L0_ffn_W1': 5.109,
     'L0_ffn_W2': 4.325,
     'L1_conv_qkv_w0': 5.826,
     'L1_conv_qkv_w1': 8.0,
     'L1_conv_qkv_w2': 8.0,
     'L2_conv_bias': 4.53,
     'L2_ffn_gate_w': 8.0,
     'L2_ffn_w1': 8.0,
     'L2_ffn_w2': 8.0,
     'L2_ffn_w3': 8.0,
     'L3_conv_conv_w': 200.0,
     'L3_ffn_gate_w': 8.0,
     'L3_ffn_W1': 8.0,
     'L3_ffn_W2': 8.0}
    for name, (base, spread) in spreads.items():
        noise = np.random.default_rng([zlib.crc32(name.encode()), seed]).standard_normal(out[name].shape)
        drawn = base * np.exp(spread * noise) if base else spread * noise
        out[name] = jnp.asarray(drawn.astype(out[name].dtype))
    for name, factor in factors.items():
        out[name] = (out[name] * factor).astype(out[name].dtype)
    return out
```

```python
from collections import namedtuple
from contextlib import ExitStack, contextmanager

import numpy as np

import concourse.bass as bass
from concourse import mybir

F32 = mybir.dt.float32
BF16 = mybir.dt.bfloat16
U32 = mybir.dt.uint32
ALU = mybir.AluOpType
ACT = mybir.ActivationFunctionType
AX = mybir.AxisListType.X

P = 128
C = 64
IMAGES = 16
SIDE = 16
PLACES = SIDE * SIDE
TILES = IMAGES * PLACES // P
CODES = 1024
PAIRS = IMAGES // 2
PT = TILES // PAIRS
SUPERS = 4
ST = TILES // SUPERS
SPAN = ST * P
HALF = SPAN // 2

HEADS, HD = 8, 8
SCALE = HD ** -0.5
NEG = -1e30

RANGES = [(5, 1, (0, 1, 2, 3)), (7, 2, (4, 5, 6)), (9, 3, (7,))]

FFN = [
    dict(E=8, H=128, gated=False, renorm=False, floor=None, gate_b=True, b1=True, b2=True, keep=False),
    dict(E=8, H=64, gated=False, renorm=True, floor=1e-12, gate_b=False, b1=True, b2=True, keep=True),
    dict(E=16, H=128, gated=True, renorm=True, floor=None, gate_b=True, b1=False, b2=False, keep=False),
    dict(E=8, H=128, gated=False, renorm=False, floor=None, gate_b=True, b1=True, b2=True, keep=False),
]


def weight_columns():
    at, where = 0, []
    for f in FFN:
        w = dict(up=at)
        at += f["E"] * f["H"]
        if f["gated"]:
            w["up2"] = at
            at += f["E"] * f["H"]
        w["gate"] = at
        at += f["E"]
        where.append(w)
    return where, at


WHERE, WCOLS = weight_columns()
SPLIT_TURNS = PAIRS - 1
WPAD = -(-WCOLS // SPLIT_TURNS) * SPLIT_TURNS
WCHUNK = WPAD // SPLIT_TURNS
E1 = [0, 8, None, 12]
E2 = [0, 8, None, 16]
B1ROWS, B2ROWS = 20, 24


class Order:

    def __init__(self, eng, sem):
        self.eng, self.sem, self.base, self.n = eng, sem, 0, 0

    def step(self, ins):
        ins.then_inc(self.sem, 1)
        self.n += 1
        return self.base + self.n

    def then(self, ins):
        self.eng.wait_ge(self.sem, self.step(ins))

    def then_apart(self, ins, m):
        wait_apart(self.eng, m, self.sem, self.step(ins))

    @contextmanager
    def turns(self, count, per):
        start = self.base + self.n
        with self.eng.Fori(0, count) as i:
            self.base, self.n = i * per + start, 0
            yield i
            assert self.n == per, f"{self.n} steps a turn, not {per}"
        self.base, self.n = start + count * per, 0


def barrier(eng, s, n):
    eng.drain().then_inc(s.part_done, 1)
    eng.wait_ge(s.part_done, 4 * n)


def wait_apart(eng, m, sem, value):
    eng.wait_ge(sem, value)
    eng.sem_inc(m.apart, 1)


def bcast(ap, shape):
    return ap.broadcast_to(shape)



def ln_stats(dve, o, m, x, n, done):
    for j in range(n):
        ins = dve.bn_stats(m.stats[:, j, :], x[:, j, :])
    o.then_apart(ins, m)
    for j in range(n):
        ins = dve.bn_aggr(m.mv[:, j, :], m.stats[:, j, :])
    ins.then_inc(done, 1)


def ln_rstd(pool, o, m, n, eps, done):
    o.then(pool.tensor_scalar(m.veps[:, 0:n], m.mv[:, 0:n, 1], eps, 1.0, ALU.add, ALU.mult))
    pool.tensor_tensor(m.rstd[:, 0:n], m.veps[:, 0:n], m.minus_half[:, 0:n], ALU.pow).then_inc(done, 1)


def ln_apply(dve, o, m, x, n, done):
    o.then(dve.tensor_tensor(m.xc[:, 0:n, :], x, bcast(m.mv[:, 0:n, 0:1], [P, n, C]), ALU.subtract))
    dve.tensor_tensor(m.xn[:, 0:n, :], m.xc[:, 0:n, :], bcast(m.rstd[:, 0:n].unsqueeze(2), [P, n, C]),
                      ALU.mult).then_inc(done, 1)



def load_sync(sp, nc, m, s, d):
    sp.dma_start(m.ident[:], d.ident).then_inc(s.ld_ident, 16)
    loads = [
        (m.nat[0:C, 0, 0:C], d.L0_conv_proj_w),
        (m.nat[0:C, 0, C:C + 1], d.L0_conv_proj_b.rearrange("(o a) -> o a", a=1)),
        (m.emb[:, :, :], d.L0_conv_emb.rearrange("(k p) c -> p k c", p=P)),
    ]
    for dst, src in loads:
        sp.dma_start(dst, src, allow_slow_non_contiguous=src.shape[-1] == 1).then_inc(s.ld_first, 16)
    assert len(loads) == FIRST_LOADS


FIRST_LOADS = 3


def load_rest(q, nc, m, s, d):
    n = 0

    def ld(dst, src, sem, slow=False):
        nonlocal n
        q.dma_start(dst, src, allow_slow_non_contiguous=src.shape[-1] == 1 or slow).then_inc(sem, 16)
        n += 1

    for half in range(2):
        rows = slice(half * C, half * C + C)
        for f, (cfg, w) in enumerate(zip(FFN, WHERE)):
            E, H = cfg["E"], cfg["H"]
            ups = {0: [d.L0_ffn_W1], 1: [d.L1_ffn_w1], 2: [d.L2_ffn_w1, d.L2_ffn_w2], 3: [d.L3_ffn_W1]}[f]
            for key, up in zip(("up", "up2"), ups):
                ld(m.wall[rows, w[key]:w[key] + E * H].rearrange("c (e h) -> c e h", e=E),
                   up.rearrange("e c h -> c e h"), s.ld_up)
            gate = {0: d.L0_ffn_gate_w, 1: d.L1_ffn_router_w.rearrange("e c -> c e"),
                    2: d.L2_ffn_gate_w, 3: d.L3_ffn_gate_w}[f]
            ld(m.wall[rows, w["gate"]:w["gate"] + E], gate, s.ld_up, slow=f == 1)
    assert n == UP_LOADS
    n = 0
    for l, gb in ((0, d.L0_ffn_gate_b), (2, d.L2_ffn_gate_b), (3, d.L3_ffn_gate_b)):
        ld(m.gate_b[l][:, :], gb.partition_broadcast(P), s.ld_small)
    ld(m.down[0][:, :, :], d.L0_ffn_W2.rearrange("e h c -> h e c"), s.ld_small)
    ld(m.down[1][:, :, :], d.L1_ffn_w2.rearrange("(g i) h c -> (i h) g c", i=2), s.ld_small)
    ld(m.down[2][:, :, :], d.L2_ffn_w3.rearrange("e h c -> h e c"), s.ld_small)
    ld(m.down[3][:, :, :], d.L3_ffn_W2.rearrange("e h c -> h e c"), s.ld_small)
    ld(m.b1nat[0:8, :], d.L0_ffn_b1, s.ld_small)
    ld(m.b1nat[8:12, :], d.L1_ffn_b1.rearrange("(g i) h -> g (i h)", i=2), s.ld_small)
    ld(m.b1nat[12:20, :], d.L3_ffn_b1, s.ld_small)
    for l, b2 in ((0, d.L0_ffn_b2), (1, d.L1_ffn_b2), (3, d.L3_ffn_b2)):
        ld(m.b2[:, E2[l]:E2[l] + 8, :], b2.partition_broadcast(3), s.ld_small)
    ld(m.partsel[:, 0:2], d.partsel, s.ld_small)
    q.wait_ge(s.padded, 1)
    for slot, off in ((1, 0), (2, C), (3, 2 * C)):
        for (a, b), at, w, bias in (((0, 32), 0, d.L1_conv_qkv_w0, d.L1_conv_qkv_b0),
                                    ((56, 64), 32, d.L1_conv_qkv_w2, d.L1_conv_qkv_b2),
                                    ((32, 56), 40, d.L1_conv_qkv_w1, d.L1_conv_qkv_b1)):
            to = slice(at, at + b - a)
            ld(m.nat[to, slot, 0:C], w[off + a:off + b, :], s.ld_small)
            ld(m.nat[to, slot, C:C + 1], bias[off + a:off + b].rearrange("(o a) -> o a", a=1), s.ld_small)
    ld(m.nat[0:C, 4, 0:32], d.L1_conv_proj_w[:, 0:32], s.ld_small)
    ld(m.nat[0:C, 4, 32:40], d.L1_conv_proj_w[:, 56:64], s.ld_small)
    ld(m.nat[0:C, 4, C:C + 1], d.L1_conv_proj_b.rearrange("(o a) -> o a", a=1), s.ld_small)
    ld(m.nat[0:C, 5, 40:64], d.L1_conv_proj_w[:, 32:56], s.ld_small)
    ld(m.nat[0:C, 6, 0:C], d.L2_conv_W, s.ld_small)
    ld(m.nat[0:C, 6, C:C + 1], d.L2_conv_bias.rearrange("(o a) -> o a", a=1), s.ld_small)
    ld(m.nat[0:C, 7, 0:C], d.L3_conv_conv_w, s.ld_small)
    for half in range(2):
        rows = slice(half * C, half * C + C)
        for k, v in enumerate((d.L3_conv_conv_b, d.L3_conv_bn_gamma, d.L3_conv_bn_beta)):
            ld(m.bn_in[rows, k:k + 1], v.rearrange("(o a) -> o a", a=1), s.ld_small)
    ld(m.mask_in, d.mask_table, s.ld_small)
    ld(m.padn[:, :], d.padn, s.ld_small)
    ld(m.minus_rows[:, :], d.minus_rows, s.ld_small)
    ld(m.padmax[:, :], d.padmax, s.ld_small)
    ld(m.iota[:, :], d.iota, s.ld_small)
    assert n == SMALL_LOADS, n


UP_LOADS = 2 * (5 + 4)
SMALL_LOADS = 3 + 4 + 3 + 3 + 1 + 18 + 4 + 3 + 6 + 5



def c0_pe_first(pe, nc, m, s):
    pe.wait_ge(s.ld_ident, 16)
    pe.wait_ge(s.ld_first, 16 * FIRST_LOADS)
    pe.transpose(m.ps[0:C + 1, 4, 0:C], m.nat[0:C, 0, :], m.ident[0:C, 0:C])
    for k in range(8):
        ins = pe.transpose(m.ps[0:C, k // 4, (k % 4) * P:(k % 4 + 1) * P], m.emb[:, k, :], m.ident[:])
    ins.then_inc(s.codes_t, 1)
    pe.wait_ge(s.codes_sq, 1)
    pe.wait_ge(s.ones_rows, 1)
    for k in range(2):
        ins = pe.matmul(m.ps[0:C + 1, 2 + k, :], m.minus_one[0:C, 0:C + 1], m.codes_sq[:, k * 512:(k + 1) * 512],
                        start=True, stop=True)
    ins.then_inc(s.codes_n, 1)


def c0_act_first(act, nc, m, s):
    act.wait_ge(s.codes_t, 1)
    act.activation(m.proj0[:, :], m.ps[0:C + 1, 4, 0:C], ACT.Copy)
    act.activation(m.codes_sq[:, :], m.ps[0:C, 0:2, :].rearrange("c a k -> c (a k)"), ACT.Square).then_inc(s.codes_sq, 1)
    act.activation(m.codes2[0:C, :], m.ps[0:C, 0:2, :].rearrange("c a k -> c (a k)"), ACT.Copy, scale=2.0)
    act.wait_ge(s.codes_n, 1)
    act.activation(m.codes2[C:C + 1, :], m.ps[C:C + 1, 2:4, :].rearrange("c a k -> c (a k)"), ACT.Copy)\
        .then_inc(s.codes_ready, 1)


def c0_xload(pe, m, s, g):
    pe.wait_ge(s.c0_in, (g + 1) * 16)
    for i in range(2):
        ins = pe.transpose(m.ps[:, 4, i * P:(i + 1) * P], m.xload[:, i * P:(i + 1) * P], m.ident[:])
    ins.then_inc(s.c0_xt, 1)


def c0_normt(pe, m, s, g):
    wait_apart(pe, m, s.c0_xn, g + 1)
    for j in range(PT):
        ins = pe.transpose(m.ps[0:C, 5, j * P:(j + 1) * P], m.xn[:, j, :], m.ident[:])
    ins.then_inc(s.c0_nt, 1)


def c0_project(pe, m, s, g):
    pe.wait_ge(s.c0_xf, g + 1)
    pe.matmul(m.ps[0:C, 4, :], m.proj0[:, :], m.xf[:, :], start=True, stop=True).then_inc(s.c0_zp, 1)


def c0_scores(pe, m, s, g, j):
    if j == 0:
        pe.wait_ge(s.c0_z, g + 1)
    pe.wait_ge(s.c0_read, g * PT + j + 1)
    for k in range(2):
        ins = pe.matmul(m.ps[:, 2 * (j % 2) + k, :], m.z[:, j * P:(j + 1) * P], m.codes2[:, k * 512:(k + 1) * 512],
                        start=True, stop=True)
    ins.then_inc(s.c0_scored, 1)


def c0_pe(pe, nc, m, s):
    c0_pe_first(pe, nc, m, s)
    c0_xload(pe, m, s, 0)
    c0_normt(pe, m, s, 0)
    c0_project(pe, m, s, 0)
    pe.wait_ge(s.codes_ready, 1)

    def turn(g, ahead):
        c0_scores(pe, m, s, g, 0)
        c0_scores(pe, m, s, g, 1)
        if ahead:
            pe.wait_ge(s.c0_z, g + 1)
            c0_xload(pe, m, s, g + 1)
        c0_scores(pe, m, s, g, 2)
        if ahead:
            c0_normt(pe, m, s, g + 1)
        c0_scores(pe, m, s, g, 3)
        if ahead:
            c0_project(pe, m, s, g + 1)

    with pe.Fori(0, PAIRS - 1) as g:
        turn(g, True)
    turn(PAIRS - 1, False)


def c0_act(act, nc, m, s):
    c0_act_first(act, nc, m, s)

    def evacuate(g, first):
        act.wait_ge(s.c0_nt, g + 1)
        if not first:
            act.wait_ge(s.c0_zp, g)
        act.activation(m.xf[0:C, :], m.ps[0:C, 5, :], ACT.Copy).then_inc(s.c0_xf, 1)
        act.wait_ge(s.c0_zp, g + 1)
        if not first:
            act.wait_ge(s.c0_scored, g * PT)
        act.activation(m.z[0:C, :], m.ps[0:C, 4, :], ACT.Copy).then_inc(s.c0_z, 1)

    act.wait_ge(s.ones_rows, 1)
    evacuate(0, True)
    act.wait_ge(s.ld_up, 16 * UP_LOADS)
    with act.Fori(0, PAIRS - 1) as g:
        cols = bass.ds(g * WCHUNK, WCHUNK)
        act.activation(m.w1[:, cols], m.wall[:, cols], ACT.Copy)
        act.activation(m.w3[C:P, cols], m.wall[C:P, cols], ACT.Copy).then_inc(s.split_a, 1)
        evacuate(g + 1, False)
        act.wait_ge(s.split_r, g + 1)
        act.activation(m.w2[:, cols], m.wrest[:, :], ACT.Copy).then_inc(s.split_b, 1)


def c0_dve_arrive(dve, o, m, s, g, first):
    x = m.X[:, bass.ds(g * PT, PT), :]
    dve.wait_ge(s.c0_xt, g + 1)
    o.then_apart(dve.tensor_copy(x.rearrange("p (a i) c -> p i a c", i=2),
                                 m.ps[:, 4, 0:2 * P].rearrange("p (i a c) -> p i a c", i=2, a=2)), m)
    ln_stats(dve, o, m, x, PT, s.c0_mv)


def c0_dve_norm(dve, o, m, s, g, first):
    x = m.X[:, bass.ds(g * PT, PT), :]
    dve.wait_ge(s.c0_rstd, g + 1)
    if not first:
        dve.wait_ge(s.c0_nt, g)
    ln_apply(dve, o, m, x, PT, s.c0_xn)


def c0_dve(dve, nc, m, s):
    o = Order(dve, s.c0_order)
    dve.memset(m.minus_half[:, :], -0.5)
    dve.memset(m.minus_one[:, :], -1.0)
    dve.memset(m.z[C:C + 1, :], 1.0)
    dve.memset(m.wall[:, WCOLS:WPAD + 8], 0.0)
    dve.memset(m.xf[C:C + 1, :], 1.0).then_inc(s.ones_rows, 1)
    dve.memset(m.ones3[:, :], 1.0)
    dve.memset(m.one[:, :], 1.0)
    dve.memset(m.nat[:, 1:6, :], 0.0)
    dve.memset(m.maxp[:, :, :], 0.0)
    dve.memset(m.maxes[:, :, :, :], 0.0)
    dve.memset(m.qs[0:C, LOW:, :], 0.0)
    dve.memset(m.vals[:, :, :, HD:HD + 1], 1.0)
    dve.memset(m.xfp[C:C + 1, :], 1.0)
    dve.memset(m.ot1[C:C + 1, :], 1.0)
    o.then(dve.memset(m.maxparts[:, :, :, :], 0.0))
    dve.memset(m.maxrest[:, :, :], 0.0).then_inc(s.padded, 1)
    dve.sem_inc(s.c0_read, 2)
    c0_dve_arrive(dve, o, m, s, 0, True)
    c0_dve_norm(dve, o, m, s, 0, True)

    def argmax(g, j, first=False):
        wait_apart(dve, m, s.c0_scored, g * PT + j + 1)
        sc = m.ps[:, 2 * (j % 2):2 * (j % 2) + 2, :].rearrange("p a k -> p (a k)")
        n = o.step(dve.max(m.best[:, j, :], sc))
        dve.wait_ge(s.c0_order, n)
        if not first:
            wait_apart(dve, m, s.c0_gathered[j], g * 16)
        dve.max_index(m.code[:, j, :], m.best[:, j, :], sc).then_inc(s.c0_read, 1)

    def turn(g, first=False):
        argmax(g, 0, first)
        c0_dve_arrive(dve, o, m, s, g + 1, False)
        argmax(g, 1, first)
        c0_dve_norm(dve, o, m, s, g + 1, False)
        argmax(g, 2, first)
        argmax(g, 3, first)

    turn(0, True)
    with o.turns(PAIRS - 2, C0_STEPS) as i:
        turn(i + 1)
    for j in range(PT):
        argmax(PAIRS - 1, j)


C0_STEPS = 7


def c0_pool(pool, nc, m, s, d):
    o = Order(pool, s.c0_pool_order)
    pool.wait_ge(s.ones_rows, 1)
    wait_apart(pool, m, s.c0_mv, 1)
    ln_rstd(pool, o, m, PT, 1e-6, s.c0_rstd)

    def gather(g, j):
        wait_apart(pool, m, s.c0_read, 2 + g * PT + j + 1)
        pool.indirect_dma_start(m.zq[j][:, :], None, d.L0_conv_emb,
                                bass.IndirectOffsetOnAxis(ap=m.code[:, j, 0:1], axis=0))\
            .then_inc(s.c0_gathered[j], 16)

    def add(g):
        for j in range(PT):
            wait_apart(pool, m, s.c0_gathered[j], g * 16 + 16)
            x = m.X[:, bass.ds(g * PT + j, 1), :].rearrange("p a c -> p (a c)")
            ins = pool.tensor_tensor(x, x, m.zq[j][:, :], ALU.add)
        o.then(ins)

    with o.turns(PAIRS - 1, 3) as g:
        cols = bass.ds(g * WCHUNK, WCHUNK)
        gather(g, 0)
        wait_apart(pool, m, s.c0_mv, g + 2)
        ln_rstd(pool, o, m, PT, 1e-6, s.c0_rstd)
        gather(g, 1)
        pool.wait_ge(s.split_a, g + 1)
        pool.tensor_tensor(m.wrest[:, :], m.wall[:, cols], m.w1[:, cols], ALU.subtract).then_inc(s.split_r, 1)
        gather(g, 2)
        gather(g, 3)
        pool.wait_ge(s.split_b, g + 1)
        o.then(pool.tensor_tensor(m.w3[0:C, cols], m.wrest[0:C, :], m.w2[0:C, cols], ALU.subtract))
        add(g)
    for j in range(PT):
        gather(PAIRS - 1, j)
    add(PAIRS - 1)



def ffn_counts(l):
    f = FFN[l]
    per = P // f["H"]
    G = f["E"] // per
    return f["E"], G, per, 2 * G


def ffn_pe(pe, nc, m, s, l):
    f, w, q = FFN[l], WHERE[l], s.ffn[l]
    E, G, per, U = ffn_counts(l)
    ahead_at = min(4, G - 1)
    free = 2 if f["gated"] else 4

    def transposes(sb):
        pe.wait_ge(q.parts, sb + 1)
        pe.wait_ge(q.logits_read, sb + 1)
        t6 = m.ps[:, 6, :].bitcast(BF16)
        t7 = m.ps[:, 7, :].bitcast(BF16)
        for t in range(ST):
            pe.transpose(t6[:, t * P:(t + 1) * P], m.parts[:, t, 0:2, :], m.identb[:])
            ins = pe.transpose(t7[:, t * P:(t + 1) * P], m.parts[:, t, 1:3, :], m.identb[:])
        ins.then_inc(q.transposed, 1)

    def three(out, lhs, rhs, stop=True):
        for k, (a, b) in enumerate(zip(lhs, rhs)):
            ins = pe.matmul(out, a, b, start=(k == 0), stop=(k == 2 and stop))
        return ins

    def logits(sb):
        pe.wait_ge(q.xa, sb + 1)
        pe.wait_ge(q.xb, sb + 1)
        gate = slice(w["gate"], w["gate"] + E)
        for t in range(ST):
            a, b = m.xa[:, t * P:(t + 1) * P], m.xb[:, t * P:(t + 1) * P]
            ins = three(m.ps[:, 6, t * E:(t + 1) * E], (a, a, b), (m.w1[:, gate], m.w2[:, gate], m.w3[:, gate]))
        ins.then_inc(q.logits, 1)

    def hidden(sb, u):
        pe.wait_ge(q.act, sb * U + u + 1)
        g, half = u // 2, u % 2
        a, b = (x[:, half * HALF:(half + 1) * HALF] for x in (m.xa, m.xb))
        outs = ((w["up"], u % 4),) if not f["gated"] else ((w["up"], 2 * (u % 2)), (w["up2"], 2 * (u % 2) + 1))
        for at, bank in outs:
            cols = slice(at + g * P, at + (g + 1) * P)
            ins = three(m.ps[:, bank, :], (m.w1[:, cols], m.w2[:, cols], m.w3[:, cols]), (a, a, b))
        ins.then_inc(q.hidden, 1)

    def down(sb, e):
        g, i = e // per, e % per
        pe.wait_ge(q.act, free + sb * U + 2 * g + 2)
        pe.wait_ge(q.weighed, sb * E + e + 1)
        bank = 4 + e % 2
        if f["b2"]:
            pe.matmul(m.ps[:, bank, :], m.ones3[:, :], bcast(m.b2p[:, E2[l] + e, :].unsqueeze(1), [3, ST, C]),
                      start=True, stop=True)
        rows = slice(i * f["H"], (i + 1) * f["H"])
        for t in range(ST):
            ins = pe.matmul(m.ps[:, bank, t * C:(t + 1) * C], m.hid[rows, g % 2, t * P:(t + 1) * P],
                            m.down[l][rows, g, :], start=not f["b2"], stop=True, skip_group_check=f["b2"])
        ins.then_inc(q.down, 1)

    def turn(sb, ahead):
        for u in range(U):
            hidden(sb, u)
            g = u // 2
            if u % 2 and g > 0:
                for i in range(per):
                    down(sb, (g - 1) * per + i)
            if u % 2 and g == ahead_at - 1 and ahead and G > 4:
                transposes(sb + 1)
        if ahead and G <= 4:
            transposes(sb + 1)
        for i in range(per):
            down(sb, (G - 1) * per + i)
        if ahead:
            logits(sb + 1)

    transposes(0)
    logits(0)
    with pe.Fori(0, SUPERS - 1) as sb:
        turn(sb, True)
    turn(SUPERS - 1, False)


def ffn_act(act, nc, m, s, l):
    f, q = FFN[l], s.ffn[l]
    E, G, per, U = ffn_counts(l)
    flat = m.parts

    def part(sb, k, first):
        if k == 0:
            act.wait_ge(q.xn, sb + 1)
            if not first:
                act.wait_ge(q.transposed, sb)
            act.activation(m.parts[:, :, 1, :], m.xn[:, :, :], ACT.Copy).then_inc(q.part1, 1)
        else:
            act.wait_ge(q.rest, sb + 1)
            act.activation(m.parts[:, :, 0, :], m.xc[:, :, :], ACT.Copy).then_inc(q.part2, 1)

    def evacuate(sb, first):
        act.wait_ge(q.transposed, sb + 1)
        if not first:
            act.wait_ge(q.hidden, sb * U)
        act.activation(m.xb[:, :], m.ps[:, 7, :].bitcast(BF16), ACT.Copy).then_inc(q.xb, 1)

    def exps(sb):
        act.wait_ge(q.below_max, sb + 1)
        act.activation(m.ex[:, 0:ST, 0:E + 1], m.below[:, 0:ST, 0:E + 1], ACT.Exp).then_inc(q.exps, 1)

    def unit(sb, u):
        g, half = u // 2, u % 2
        act.wait_ge(q.hidden, sb * U + u + 1)
        if half == 0:
            act.wait_ge(q.down, sb * E + (g + 1) * per)
        out = m.hid[:, g % 2, half * HALF:(half + 1) * HALF]
        if f["gated"]:
            act.wait_ge(q.act, sb * U + u + 1)
            act.activation(m.silu[:, half, :], m.ps[:, 2 * half, :], ACT.Silu).then_inc(q.silu, 1)
        else:
            bias = m.b1t[:, E1[l] + g:E1[l] + g + 1]
            act.activation(out, m.ps[:, u % 4, :], ACT.Gelu, bias=bias).then_inc(q.act, 1)

    def turn(sb, ahead):
        for g in range(G):
            unit(sb, 2 * g)
            unit(sb, 2 * g + 1)
            if g == 0:
                exps(sb)
            if ahead and g == min(2, G - 3):
                part(sb + 1, 0, False)
            if ahead and g == min(3, G - 2):
                part(sb + 1, 1, False)
        if ahead:
            evacuate(sb + 1, False)

    part(0, 0, True)
    part(0, 1, True)
    evacuate(0, True)
    with act.Fori(0, SUPERS - 1) as sb:
        turn(sb, True)
    turn(SUPERS - 1, False)


def ffn_dve(dve, nc, m, s, l):
    f, q = FFN[l], s.ffn[l]
    E, G, per, U = ffn_counts(l)
    o = Order(dve, q.order)
    dve.sem_inc(q.weighed, 2)
    dve.sem_inc(q.logits_read, 1)

    def stats(sb):
        ln_stats(dve, o, m, m.X[:, bass.ds(sb * ST, ST), :], ST, q.mv)

    def norm(sb):
        dve.wait_ge(q.rstd, sb + 1)
        x = m.X[:, bass.ds(sb * ST, ST), :]
        ln_apply(dve, o, m, x, ST, q.xn)
        if f["keep"]:
            dve.wait_ge(q.xn, sb + 1)
            o.then(dve.tensor_tensor(x, x, m.xn[:, :, :], ALU.add))

    def rest(sb):
        dve.wait_ge(q.part1, sb + 1)
        dve.tensor_tensor(m.xc[:, :, :], m.xn[:, :, :], m.parts[:, :, 1, :], ALU.subtract).then_inc(q.rest, 1)

    def third(sb):
        dve.wait_ge(q.part2, sb + 1)
        dve.tensor_tensor(m.parts[:, :, 2, :], m.xc[:, :, :], m.parts[:, :, 0, :], ALU.subtract)\
            .then_inc(q.parts, 1)

    def evacuate(sb, first):
        dve.wait_ge(q.transposed, sb + 1)
        if not first:
            dve.wait_ge(q.hidden, sb * U)
        dve.tensor_copy(m.xa[:, :], m.ps[:, 6, :].bitcast(BF16)).then_inc(q.xa, 1)

    def router(sb):
        dve.wait_ge(q.logits, sb + 1)
        lg = m.lg[:, :, 0:E]
        raw = m.ps[:, 6, 0:ST * E].rearrange("p (t e) -> p t e", e=E)
        if f["gate_b"]:
            ins = dve.tensor_tensor(lg, raw, bcast(m.gate_b[l][:, :].unsqueeze(1), [P, ST, E]), ALU.add)
        else:
            ins = dve.tensor_copy(lg, raw)
        ins.then_inc(q.logits_read, 1)
        wait_apart(dve, m, q.logits_read, sb + 2)
        for t in range(ST):
            ins = dve.max(m.top[:, t, :], m.lg[:, t, 0:E])
        o.then(ins)
        dve.tensor_tensor(m.below[:, :, 0:E], lg, bcast(m.top[:, :, 0:1], [P, ST, E]), ALU.subtract)
        dve.tensor_tensor(m.below[:, :, E], m.top[:, :, 1], m.top[:, :, 0], ALU.subtract).then_inc(q.below_max, 1)
        for t in range(ST):
            ins = dve.max_index(m.topi[:, t, :], m.top[:, t, :], m.lg[:, t, 0:E])
        o.then(ins)
        o.then(dve.tensor_copy(m.topf[:, :, :], m.topi[:, :, 0:2]))
        shape = [P, ST, E]
        for k in range(2):
            ins = dve.tensor_tensor(m.hit[:, k, :, 0:E], bcast(m.iota[:, 0:E].unsqueeze(1), shape),
                                    bcast(m.topf[:, :, k:k + 1], shape), ALU.is_equal)
        o.step(ins)
        dve.wait_ge(q.exps, sb + 1)
        o.then(dve.tensor_reduce(m.sums[:, :], m.ex[:, :, 0:E], AX, ALU.add))
        o.then(dve.reciprocal(m.prob[:, 0, :], m.sums[:, :]))
        o.then(dve.tensor_tensor(m.prob[:, 1, :], m.ex[:, :, E], m.prob[:, 0, :], ALU.mult))
        if f["renorm"]:
            o.then(dve.tensor_tensor(m.sums[:, :], m.prob[:, 0, :], m.prob[:, 1, :], ALU.add))
            if f["floor"] is not None:
                o.then(dve.tensor_scalar(m.sums[:, :], m.sums[:, :], f["floor"], None, ALU.max))
            o.then(dve.reciprocal(m.rsum[:, :], m.sums[:, :]))
            o.then(dve.tensor_tensor(m.prob[:, :, :], m.prob[:, :, :], bcast(m.rsum[:, :].unsqueeze(1), [P, 2, ST]),
                                     ALU.mult))
        for k in range(2):
            ins = dve.tensor_tensor(m.hit[:, k, :, 0:E], m.hit[:, k, :, 0:E],
                                    bcast(m.prob[:, k, :].unsqueeze(2), shape), ALU.mult)
        o.then(ins)
        o.then(dve.tensor_tensor(m.cw[:, :, 0:E], m.hit[:, 0, :, 0:E], m.hit[:, 1, :, 0:E], ALU.add))

    def gate(sb, u):
        g, half = u // 2, u % 2
        dve.wait_ge(q.silu, sb * U + u + 1)
        if half == 0:
            dve.wait_ge(q.down, sb * E + (g + 1) * per)
        dve.tensor_tensor(m.hid[:, g % 2, half * HALF:(half + 1) * HALF], m.silu[:, half, :],
                          m.ps[:, 2 * half + 1, :], ALU.mult).then_inc(q.act, 1)

    def weigh(sb, e):
        dve.wait_ge(q.down, 2 * per + sb * E + e + 1)
        dve.wait_ge(q.added, sb * E + e + 1)
        dve.tensor_tensor(m.prod[:, e % 2, :, :], m.ps[:, 4 + e % 2, :].rearrange("p (t c) -> p t c", c=C),
                          bcast(m.cw[:, :, e:e + 1], [P, ST, C]), ALU.mult).then_inc(q.weighed, 1)

    def turn(sb, ahead):
        if not f["gated"]:
            router(sb)
        pieces = [lambda: stats(sb + 1), lambda: norm(sb + 1), lambda: rest(sb + 1), lambda: third(sb + 1)]
        for g in range(G):
            if f["gated"]:
                gate(sb, 2 * g)
                gate(sb, 2 * g + 1)
                if g == 0:
                    router(sb)
            if g > 0:
                for i in range(per):
                    weigh(sb, (g - 1) * per + i)
            if ahead:
                if G > 4:
                    if g < 4:
                        pieces[g]()
                elif g < 2:
                    pieces[2 * g]()
                    pieces[2 * g + 1]()
        for i in range(per):
            weigh(sb, (G - 1) * per + i)
        if ahead:
            evacuate(sb + 1, False)

    stats(0)
    norm(0)
    rest(0)
    third(0)
    evacuate(0, True)
    with o.turns(SUPERS - 1, FFN_STEPS[l]) as sb:
        turn(sb, True)
    turn(SUPERS - 1, False)


FFN_STEPS = [11, 16, 14, 11]


def ffn_pool(pool, nc, m, s, l):
    f, q = FFN[l], s.ffn[l]
    E, G, per, U = ffn_counts(l)
    o = Order(pool, q.pool_order)
    free = 2 if f["gated"] else 4
    pool.sem_inc(q.added, 2)
    pool.sem_inc(q.act, free)
    pool.sem_inc(q.down, 2 * per)

    def add(sb, e):
        x = m.X[:, bass.ds(sb * ST, ST), :]
        pool.wait_ge(q.weighed, 2 + sb * E + e + 1)
        wait_apart(pool, m, q.added, 2 + sb * E + e)
        pool.tensor_tensor(x, x, m.prod[:, e % 2, :, :], ALU.add).then_inc(q.added, 1)

    def rstd(sb):
        wait_apart(pool, m, q.mv, sb + 1)
        ln_rstd(pool, o, m, ST, 1e-5, q.rstd)

    rstd(0)
    with o.turns(SUPERS - 1, 1) as sb:
        rstd(sb + 1)
        for e in range(E):
            add(sb, e)
    for e in range(E):
        add(SUPERS - 1, e)



BANKS3 = 4 * 160 + 256 + 3 * 128
Q_PARTS = (0, 0, 0, 1, 1, 2)
K_PARTS = (0, 1, 2, 0, 1, 0)
SPLIT_ROWS = 6 * HD
BLOCKS = 5
LOW = 3


def row_parity(ap):
    return ap.rearrange("p (im a py x) -> p im py a x", im=2, py=2, x=SIDE)


def by_parity(ap):
    return ap.rearrange("p (im py a x) -> p im py a x", im=2, py=2, x=SIDE)


HEAD = [(0, 0, 0, 0, "near"), (0, 1, 0, 160, "near"), (0, 2, 0, 320, "near"), (1, 0, 1, 0, "near"),
        (1, 1, 1, 160, "all"), (1, 2, 2, 0, "rows"), (1, 3, 2, 128, "rows"), (1, 4, 2, 256, "rows")]
BANK_COLS = (480, 416, 384)
BANK_AT = (0, 480, 896)


def make_sel(pool, m, s):
    o = Order(pool, s.sel_order)
    o.then(pool.memset(m.sel, 0.0))
    for side, parts in enumerate((Q_PARTS, K_PARTS)):
        for k, part in enumerate(parts):
            for half, first, n in ((0, 0, LOW), (1, LOW, HEADS - LOW)):
                src = m.ident[:, side * C + first * HD:side * C + (first + n) * HD]
                ins = pool.tensor_copy(m.sel[:, side, part, 0:n, half * C + k * HD:half * C + (k + 1) * HD],
                                       src.rearrange("p (n d) -> p n d", d=HD))
    o.step(ins)


def c1_pe(pe, nc, m, s):
    pe.sem_inc(s.c1_o, 1)

    def tokens(p):
        pe.wait_ge(s.c1_xn, p + 1)
        wait_apart(pe, m, s.c1_max, 4 * p + 1)
        for t in range(PT):
            ins = pe.transpose(m.ps[0:C, 0, t * P:(t + 1) * P], m.xn[:, t, :], m.ident[:])
        ins.then_inc(s.c1_nt, 1)

    def queries_keys(p):
        pe.wait_ge(s.c1_xf, p + 1)
        pe.matmul(m.ps[:, 1, :], m.wqk[:, :], m.xf[:, :], start=True, stop=True).then_inc(s.c1_qk, 1)

    def values_of_tokens(p):
        for t in range(PT):
            cols = slice(t * P, (t + 1) * P)
            for x, a, b in ((m.xf, 0, 40), (m.xfp, 40, 64)):
                ins = pe.matmul(m.ps[:, 0, t * C + a:t * C + b], x[:, cols], m.wv[:, a:b], start=True, stop=True)
        ins.then_inc(s.c1_v, 1)

    def spread(p):
        pe.wait_ge(s.c1_part3, p + 1)
        for b in range(BLOCKS):
            for side, (read, done) in enumerate(((s.c1_qs, s.c1_selq), (s.c1_ks, s.c1_selk))):
                pe.wait_ge(read, BLOCKS * p + b + 1)
                out = m.ps[:, 1 + side, :]
                if b < 2:
                    for k in range(3):
                        ins = pe.matmul(out, m.sel[:, side, k, b, :], m.qkp[:, k, :], start=(k == 0), stop=(k == 2))
                    ins.then_inc(done, 1)
                    continue
                if b == 2:
                    for k in range(3):
                        pe.matmul(out[0:C, :], m.sel[:, side, k, b, 0:C], m.qkp[:, k, :],
                                  start=(k == 0), stop=(k == 2))
                for im in range(2):
                    for k in range(3):
                        ins = pe.matmul(out[C:P, im * PLACES:(im + 1) * PLACES], m.sel[:, side, k, b, C:P],
                                        row_parity(m.qkp[:, k, :])[:, im], start=(k == 0), stop=(k == 2))
                ins.then_inc(done, 1)

    def logits(first_bank, stationary, moving, rows, i):
        for b, (n, at) in enumerate(zip(BANK_COLS, (None, MASK_AT["near"], MASK_AT["rows"]))):
            mask = m.mask[:, i * MASK_TILE:(i + 1) * MASK_TILE]
            if b == 1:
                rhs = mask[:, 0:416]
            else:
                kind, w = (("near", 160), None, ("rows", 128))[b]
                rhs = bcast(mask[:, MASK_AT[kind]:MASK_AT[kind] + w].unsqueeze(1), [P, 3, w])
            pe.matmul(m.ps[:, first_bank + b, 0:n], m.identb[:, :], rhs, start=True, stop=True)
        for half, block, b, col, kind in HEAD:
            r = slice(C * half, C * half + rows)
            w = WIDTH[kind]
            lo = dict(near=i * (PLACES - 160), rows=i * P, all=0)[kind]
            ins = pe.matmul(m.ps[:, first_bank + b, col:col + w],
                            stationary(r, block, slice(i * P, (i + 1) * P)), moving(r, block, slice(lo, lo + w)),
                            start=False, stop=True, skip_group_check=True)
        return ins

    def of_image(x, im):
        return lambda r, b, c: x[r, b, im * PLACES + c.start:im * PLACES + c.stop]

    def by_query(p, n):
        if n == 0:
            pe.wait_ge(s.c1_v_read, p + 1)
            pe.wait_ge(s.c1_qs, BLOCKS * p + BLOCKS + 1)
            pe.wait_ge(s.c1_ks, BLOCKS * p + BLOCKS + 1)
        pe.wait_ge(s.c1_max, 4 * p + n + 1)
        logits(0, of_image(m.qs, n // 2), of_image(m.ks, n // 2), SPLIT_ROWS, n % 2).then_inc(s.c1_s, 1)

    def max_rows(p, im):
        pe.wait_ge(s.c1_m, 2 * p + im + 1)
        if im == 0:
            pe.wait_ge(s.c1_ot_read, p + 1)
            pe.wait_ge(s.c1_added, p + 1)
        else:
            pe.wait_ge(s.c1_q2, 2 * p + 1)
        for i in range(2):
            for b in range(BLOCKS):
                ins = pe.transpose(m.ps[:, 6 + i, :].bitcast(BF16)[:, b * P:(b + 1) * P],
                                   m.maxes[:, 2 * im + i, b, :], m.identb[:])
        ins.then_inc(s.c1_mt, 1)

    def by_key(p, n):
        im = n // 2
        pe.wait_ge(s.c1_q2, 2 * p + im + 1)
        pe.wait_ge(s.c1_p, 4 * p + n + 1)
        logits(3, of_image(m.ks, im), lambda r, b, c: m.q2[r, b, c], SPLIT_ROWS + 3, n % 2).then_inc(s.c1_st, 1)

    def weigh(p, im):
        pe.wait_ge(s.c1_p, 4 * p + 2 * im + 3)
        pe.wait_ge(s.c1_on, 2 * p + im + 1)
        if im == 0:
            pe.wait_ge(s.c1_q2, 2 * p + 2)
        for i in range(2):
            for h, (_, _, b, col, kind) in enumerate(HEAD):
                col += BANK_AT[b]
                out = m.ps[:, 7, (i * HEADS + h) * 9:(i * HEADS + h + 1) * 9]
                v = lambda k: m.vals[:, 2 * im + k, h, :]
                pt = lambda k, a, b_: m.pt[:, 2 * im + k, col + a:col + b_]
                if kind == "near":
                    own = pt(i, 0, 128) if i == 0 else pt(i, 32, 160)
                    pe.matmul(out, own, v(i), start=True, stop=True)
                    if i == 0:
                        ins = pe.matmul(out[96:128, :], pt(1, 0, 32), v(1), start=False, stop=True, skip_group_check=True)
                    else:
                        ins = pe.matmul(out[0:32, :], pt(0, 128, 160), v(0), start=False, stop=True, skip_group_check=True)
                elif kind == "rows":
                    ins = pe.matmul(out, pt(i, 0, 128), v(i), start=True, stop=True)
                else:
                    for k in range(2):
                        ins = pe.matmul(out, pt(k, i * P, (i + 1) * P), v(k), start=(k == 0), stop=(k == 1))
        ins.then_inc(s.c1_o, 1)

    def project(p):
        wait_apart(pe, m, s.c1_on, 2 * p + 3)
        for t in range(PT):
            ins = pe.transpose(m.ps[0:C, 6, t * P:(t + 1) * P], m.att[:, t, :], m.ident[:])
        ins.then_inc(s.c1_ot, 1)
        pe.wait_ge(s.c1_ot_read, p + 2)
        for t in range(PT):
            out = m.ps[:, 7, t * C:(t + 1) * C]
            pe.matmul(out, m.ot1[:, t * P:(t + 1) * P], m.wpn[:, :], start=True, stop=False)
            ins = pe.matmul(out, m.ot2[:, t * P:(t + 1) * P], m.wpp[:, :], start=False, stop=True)
        ins.then_inc(s.c1_y, 1)

    def turn(p, ahead):
        by_query(p, 0)
        by_query(p, 1)
        max_rows(p, 0)
        by_query(p, 2)
        by_key(p, 0)
        by_query(p, 3)
        by_key(p, 1)
        max_rows(p, 1)
        if ahead:
            tokens(p + 1)
        weigh(p, 0)
        if ahead:
            queries_keys(p + 1)
        by_key(p, 2)
        if ahead:
            values_of_tokens(p + 1)
        by_key(p, 3)
        if ahead:
            spread(p + 1)
        weigh(p, 1)
        project(p)

    tokens(0)
    queries_keys(0)
    values_of_tokens(0)
    spread(0)
    with pe.Fori(0, PAIRS - 1) as p:
        turn(p, True)
    turn(PAIRS - 1, False)


def c1_act(act, nc, m, s):
    for sem in (s.c1_p, s.c1_ot_read, s.c1_ks):
        act.sem_inc(sem, 1)

    def exps(p, n):
        act.wait_ge(s.c1_st, 4 * p + n + 1)
        if n == 0:
            act.wait_ge(s.c1_o, 2 * p + 1)
        for b, (k, at) in enumerate(zip(BANK_COLS, BANK_AT)):
            ins = act.activation(m.pt[:, n, at:at + k], m.ps[:, 3 + b, 0:k], ACT.Exp)
        ins.then_inc(s.c1_p, 1)

    def emax(p, im):
        act.wait_ge(s.c1_m, 2 * p + im + 1)
        tiles = slice(2 * im, 2 * im + 2)
        act.activation(m.emax[:, tiles, :], m.maxp[:, tiles, :],
                       ACT.Exp, scale=-1.0).then_inc(s.c1_em, 1)

    def tokens(p):
        act.wait_ge(s.c1_nt, p + 1)
        act.activation(m.xf[0:C, :], m.ps[0:C, 0, :], ACT.Copy)
        for py in range(2):
            ins = act.activation(by_parity(m.xfp[0:C, :])[:, :, py], row_parity(m.ps[0:C, 0, :])[:, :, py], ACT.Copy)
        ins.then_inc(s.c1_xf, 1)

    def part1(p):
        act.wait_ge(s.c1_qk, p + 1)
        act.activation(m.qkp[:, 0, :], m.ps[:, 1, :], ACT.Copy).then_inc(s.c1_part1, 1)

    def part2(p):
        act.wait_ge(s.c1_rest, p + 1)
        act.activation(m.qkp[:, 1, :], m.qk_rest, ACT.Copy).then_inc(s.c1_part2, 1)

    def keys(p):
        for b in range(BLOCKS):
            act.wait_ge(s.c1_selk, BLOCKS * p + b + 1)
            r = slice(0 if b < LOW else C, P)
            act.activation(m.ks[r, b, :], m.ps[r, 2, :], ACT.Identity, bias=m.minus_rows[r, :]).then_inc(s.c1_ks, 1)

    def vals(p):
        act.wait_ge(s.c1_v, p + 1)
        act.wait_ge(s.c1_o, 2 * p + 1)
        act.activation(m.vals[:, :, :, 0:HD], m.ps[:, 0, 0:PT * C].rearrange("p (t h d) -> p t h d", t=PT, d=HD),
                       ACT.Copy).then_inc(s.c1_v_read, 1)

    def turn(p, ahead):
        emax(p, 0)
        exps(p, 0)
        exps(p, 1)
        if ahead:
            tokens(p + 1)
        emax(p, 1)
        if ahead:
            part1(p + 1)
        exps(p, 2)
        if ahead:
            part2(p + 1)
        exps(p, 3)
        if ahead:
            keys(p + 1)
            vals(p + 1)
        act.wait_ge(s.c1_ot, p + 1)
        for py in range(2):
            act.activation(row_parity(m.ot2[:, :])[:, :, py], by_parity(m.ps[0:C, 6, :])[:, :, py], ACT.Copy)
        act.activation(m.ot1[0:C, :], m.ps[0:C, 6, :], ACT.Copy).then_inc(s.c1_ot_read, 1)

    tokens(0)
    part1(0)
    part2(0)
    keys(0)
    vals(0)
    with act.Fori(0, PAIRS - 1) as p:
        turn(p, True)
    turn(PAIRS - 1, False)


def c1_dve(dve, nc, m, s):
    o = Order(dve, s.c1_order)
    for sem in (s.c1_max, s.c1_on, s.c1_added, s.c1_qs):
        dve.sem_inc(sem, 1)

    def stats(p):
        ln_stats(dve, o, m, m.X[:, bass.ds(p * PT, PT), :], PT, s.c1_mv)

    def norm(p, first=False):
        dve.wait_ge(s.c1_rstd, p + 1)
        if not first:
            dve.wait_ge(s.c1_nt, p)
        ln_apply(dve, o, m, m.X[:, bass.ds(p * PT, PT), :], PT, s.c1_xn)

    def rest(p):
        dve.wait_ge(s.c1_part1, p + 1)
        dve.tensor_tensor(m.qk_rest, m.ps[:, 1, :], m.qkp[:, 0, :], ALU.subtract).then_inc(s.c1_rest, 1)
        dve.wait_ge(s.c1_part2, p + 1)
        dve.tensor_tensor(m.qkp[:, 2, :], m.qk_rest, m.qkp[:, 1, :], ALU.subtract).then_inc(s.c1_part3, 1)

    def queries(p):
        for b in range(BLOCKS):
            dve.wait_ge(s.c1_selq, BLOCKS * p + b + 1)
            r = slice(0 if b < LOW else C, P)
            dve.tensor_copy(m.qs[r, b, :], m.ps[r, 1, :]).then_inc(s.c1_qs, 1)

    def maxima(p, n):
        dve.wait_ge(s.c1_s, 4 * p + n + 1)
        r = m.maxr[:, n, :]
        dve.tensor_reduce(r[:, 0:3], m.ps[:, 0, 0:480].rearrange("p (h k) -> p h k", h=3), AX, ALU.max)
        dve.tensor_reduce(r[:, 3:4], m.ps[:, 1, 0:160], AX, ALU.max)
        dve.tensor_reduce(r[:, 4:5], m.ps[:, 1, 160:416], AX, ALU.max)
        dve.tensor_reduce(r[:, 5:8], m.ps[:, 2, 0:384].rearrange("p (h k) -> p h k", h=3), AX, ALU.max)\
            .then_inc(s.c1_max, 1)

    def with_padding(p, im):
        t = slice(2 * im, 2 * im + 2)
        dve.wait_ge(s.c1_max, 4 * p + 2 * im + 3)
        pad = m.padmax[:, :].rearrange("p (t h) -> p t h", t=2)
        o.then(dve.tensor_tensor(m.maxp[:, t, :], m.maxr[:, t, :], pad, ALU.max))
        o.then(dve.tensor_copy(m.maxparts[:, :, :, 0], m.maxp[:, t, :]))
        o.then(dve.tensor_tensor(m.maxrest[:, :, :], m.maxp[:, t, :], m.maxparts[:, :, :, 0], ALU.subtract))
        o.then(dve.tensor_copy(m.maxparts[:, :, :, 1], m.maxrest[:, :, :]))
        o.then(dve.tensor_tensor(m.maxparts[:, :, :, 2], m.maxrest[:, :, :], m.maxparts[:, :, :, 1], ALU.subtract))
        for half, first, n in ((0, 0, LOW), (1, LOW, HEADS - LOW)):
            at = half * C + SPLIT_ROWS
            ins = dve.tensor_copy(m.maxes[:, t, 0:n, at:at + 3], m.maxparts[:, :, first:first + n, :])
        ins.then_inc(s.c1_m, 1)

    def q2(p, im):
        dve.wait_ge(s.c1_mt, 2 * p + im + 1)
        if im == 1:
            dve.wait_ge(s.c1_st, 4 * p + 2)
        for i in range(2):
            at = im * PLACES + i * P
            mt = m.ps[:, 6 + i, :].bitcast(BF16)[:, 0:BLOCKS * P].rearrange("p (b q) -> p b q", b=BLOCKS)
            ins = dve.tensor_tensor(m.q2[:, :, i * P:(i + 1) * P], m.qs[:, :, at:at + P], mt, ALU.add)
        ins.then_inc(s.c1_q2, 1)

    def normalise(p, im):
        t = slice(2 * im, 2 * im + 2)
        dve.wait_ge(s.c1_em, 2 * p + im + 1)
        o.then(dve.tensor_tensor(m.den[:, t, :], m.emax[:, t, :], m.padn[:, :].rearrange("p (t h) -> p t h", t=2),
                                 ALU.mult))
        dve.wait_ge(s.c1_o, 2 * p + im + 2)
        out = m.ps[:, 7, 0:2 * HEADS * 9].rearrange("p (t h d) -> p t h d", t=2, d=9)
        o.then(dve.tensor_tensor(m.den[:, t, :], m.den[:, t, :], out[:, :, :, HD], ALU.add))
        o.then(dve.reciprocal(m.rden[:, t, :], m.den[:, t, :]))
        dve.tensor_tensor(m.att[:, t, :].rearrange("p t (h d) -> p t h d", d=HD), out[:, :, :, 0:HD],
                          bcast(m.rden[:, t, :].unsqueeze(3), [P, 2, HEADS, HD]), ALU.mult).then_inc(s.c1_on, 1)

    def turn(p, ahead):
        if ahead:
            stats(p + 1)
        maxima(p, 0)
        maxima(p, 1)
        with_padding(p, 0)
        if ahead:
            norm(p + 1)
        maxima(p, 2)
        q2(p, 0)
        maxima(p, 3)
        with_padding(p, 1)
        q2(p, 1)
        normalise(p, 0)
        if ahead:
            rest(p + 1)
            queries(p + 1)
        normalise(p, 1)
        dve.wait_ge(s.c1_y, p + 1)
        x = m.X[:, bass.ds(p * PT, PT), :]
        dve.tensor_tensor(x, x, m.ps[:, 7, 0:PT * C].rearrange("p (t c) -> p t c", c=C), ALU.add)\
            .then_inc(s.c1_added, 1)

    stats(0)
    norm(0, True)
    rest(0)
    queries(0)
    with o.turns(PAIRS - 1, 18) as p:
        turn(p, True)
    turn(PAIRS - 1, False)


def clear(pool, q):
    for sem in q:
        pool.sem_clear(sem)


def c1_pool(pool, nc, m, s):
    clear(pool, s.ffn[0])
    o = Order(pool, s.c1_pool_order)
    with o.turns(PAIRS, 1) as p:
        wait_apart(pool, m, s.c1_mv, p + 1)
        ln_rstd(pool, o, m, PT, 1e-6, s.c1_rstd)




def c2_pe(pe, nc, m, s):
    for sem in (s.c2_lin, s.c2_y,):
        pe.sem_inc(sem, 1)
    with pe.Fori(0, PAIRS) as p:
        pe.wait_ge(s.c2_xn, p + 1)
        wait_apart(pe, m, s.c2_xf, 2 * p + 1)
        for t in range(PT):
            ins = pe.transpose(m.ps[0:C, 0, t * P:(t + 1) * P], m.xn[:, t, :], m.ident[:])
        ins.then_inc(s.c2_nt, 1)
        pe.wait_ge(s.c2_xf, 2 * p + 3)
        pe.wait_ge(s.c2_inv, 2 * p + 1)
        pe.matmul(m.ps[:, 2, :], m.one[0:C, :], m.xsq[:, :], start=True, stop=True).then_inc(s.c2_nq, 1)
        pe.wait_ge(s.c2_relu, 2 * p + 1)
        for im in range(2):
            for i in range(2):
                at = im * PLACES
                ins = pe.matmul(m.ps[:, 3 + im, i * PLACES:(i + 1) * PLACES],
                                m.xf[0:C, at + i * P:at + (i + 1) * P], m.xf[0:C, at:at + PLACES],
                                start=True, stop=True)
            ins.then_inc(s.c2_dots, 1)
        pe.wait_ge(s.c2_tx, p + 1)
        for t in range(PT):
            ins = pe.matmul(m.ps[:, 1, t * C:(t + 1) * C], m.xf[:, t * P:(t + 1) * P], m.w_l2[:, :],
                            start=True, stop=True)
        ins.then_inc(s.c2_lin, 1)
        pe.wait_ge(s.c2_tx, p + 2)
        pe.wait_ge(s.c2_added, p + 1)
        for im in range(2):
            pe.wait_ge(s.c2_sim, 2 * p + im + 2)
            for i in range(2):
                for k in range(2):
                    ins = pe.matmul(m.ps[:, 5, (2 * im + i) * C:(2 * im + i + 1) * C],
                                    m.sim[:, im, k, i * P:(i + 1) * P], m.tx[:, 2 * im + k, :],
                                    start=(k == 0), stop=(k == 1))
        ins.then_inc(s.c2_y, 1)


def c2_act(act, nc, m, s):
    for sem in (s.c2_relu, s.c2_tx, s.c2_xf,):
        act.sem_inc(sem, 1)
    with act.Fori(0, PAIRS) as p:
        act.wait_ge(s.c2_nt, p + 1)
        act.wait_ge(s.c2_lin, p + 1)
        act.activation(m.xsq[:, :], m.ps[0:C, 0, :], ACT.Square).then_inc(s.c2_xf, 1)
        act.activation(m.xf[0:C, :], m.ps[0:C, 0, :], ACT.Copy).then_inc(s.c2_xf, 1)
        for im in range(2):
            act.wait_ge(s.c2_dots, 2 * p + im + 1)
            act.wait_ge(s.c2_sim, 2 * p + 1)
            act.activation(m.relu[:, im, :], m.ps[:, 3 + im, :], ACT.Relu).then_inc(s.c2_relu, 1)
        act.wait_ge(s.c2_lin, p + 2)
        act.wait_ge(s.c2_y, p + 1)
        act.activation(m.tx[:, :, :], m.ps[:, 1, 0:PT * C].rearrange("p (t c) -> p t c", c=C), ACT.Copy)\
            .then_inc(s.c2_tx, 1)
        for im in range(2):
            act.wait_ge(s.c2_relu, 2 * p + im + 2)
            act.activation(m.relu2[:, im, :], m.relu[:, im, :], ACT.Square).then_inc(s.c2_sq, 1)


def c2_dve(dve, nc, m, s):
    for sem in (s.c2_inv, s.c2_added, s.c2_sim,):
        dve.sem_inc(sem, 1)
    o = Order(dve, s.c2_order)

    def norms(n):
        o.then(dve.tensor_tensor(m.xc[:, 0:n, :], m.xn[:, 0:n, :], m.xn[:, 0:n, :], ALU.mult))
        o.then(dve.tensor_reduce(m.n2[:, 0:n], m.xc[:, 0:n, :], AX, ALU.add))

    def stats(p):
        ln_stats(dve, o, m, m.X[:, bass.ds(p * PT, PT), :], PT, s.c2_mv)

    def norm(p):
        dve.wait_ge(s.c2_rstd, p + 1)
        dve.wait_ge(s.c2_nt, p)
        ln_apply(dve, o, m, m.X[:, bass.ds(p * PT, PT), :], PT, s.c2_xn)
        dve.wait_ge(s.c2_xn, p + 1)
        norms(PT)

    def turn(p, ahead):
        dve.wait_ge(s.c2_nq, p + 1)
        for im in range(2):
            for i in range(2):
                ins = dve.tensor_scalar(m.d2[:, im, i * PLACES:(i + 1) * PLACES],
                                        m.ps[:, 2, im * PLACES:(im + 1) * PLACES],
                                        m.n2[:, 2 * im + i:2 * im + i + 1], 1e-16, ALU.mult, ALU.max)
            ins.then_inc(s.c2_inv, 1)
            dve.wait_ge(s.c2_inv, 2 * p + im + 2)
            o.then(dve.reciprocal(m.inv[:, im, :], m.d2[:, im, :]))
        if ahead:
            stats(p + 1)
        for im in range(2):
            dve.wait_ge(s.c2_sq, 2 * p + im + 1)
            dve.wait_ge(s.c2_y, p + 1)
            dve.tensor_tensor(m.sim[:, im, :, :].rearrange("p k q -> p (k q)"), m.relu2[:, im, :], m.inv[:, im, :],
                              ALU.mult).then_inc(s.c2_sim, 1)
        if ahead:
            norm(p + 1)
        dve.wait_ge(s.c2_y, p + 2)
        x = m.X[:, bass.ds(p * PT, PT), :]
        dve.tensor_tensor(x, x, m.ps[:, 5, 0:PT * C].rearrange("p (t c) -> p t c", c=C), ALU.add)\
            .then_inc(s.c2_added, 1)

    stats(0)
    norm(0)
    with o.turns(PAIRS - 1, 6) as p:
        turn(p, True)
    turn(PAIRS - 1, False)


def c2_pool(pool, nc, m, s):
    clear(pool, s.ffn[1])
    o = Order(pool, s.c2_pool_order)
    with o.turns(PAIRS, 1) as p:
        wait_apart(pool, m, s.c2_mv, p + 1)
        ln_rstd(pool, o, m, PT, 1e-6, s.c2_rstd)



def c3_tokens_pe(pe, m, s, p):
    pe.wait_ge(s.c3_xn2, p + 1)
    pe.wait_ge(s.c3_xm, p + 1)
    for t in range(PT):
        ins = pe.transpose(m.ps[:, 0, t * P:(t + 1) * P], m.xn2[:, t, :, :].rearrange("p a c -> p (a c)"),
                           m.ident[:])
    ins.then_inc(s.c3_nt, 1)


def c3_t_pe(pe, m, s, p):
    pe.wait_ge(s.c3_xm, p + 2)
    for im in range(2):
        ins = pe.matmul(m.ps[:, 1, im * PLACES:(im + 1) * PLACES].rearrange("p (c b) -> p c b", b=4), m.w_l3[:, :],
                        m.xm[0:C, im, :, :].rearrange("p b c -> p c b"), start=True, stop=True)
    ins.then_inc(s.c3_t, 1)


def c3_pe(pe, nc, m, s):
    for sem in (s.c3_t, s.c3_nt, s.c3_dots, s.c3_y, s.c3_norm,):
        pe.sem_inc(sem, 1)
    with pe.Fori(0, PAIRS) as p:
        c3_tokens_pe(pe, m, s, p)
        pe.wait_ge(s.c3_t_read, p + 1)
        c3_t_pe(pe, m, s, p)
    pe.wait_ge(s.c3_t_read, PAIRS + 1)
    with pe.Fori(0, PAIRS) as r:
        p = r + PAIRS
        c3_tokens_pe(pe, m, s, p)
        pe.wait_ge(s.c3_tr, r + 1)
        c3_t_pe(pe, m, s, p)
        pe.wait_ge(s.c3_sumsq, r + 1)
        pe.wait_ge(s.c3_inv, r + 1)
        pe.matmul(m.ps[:, 2, 0:2], m.one[:, :], m.n2[:, 0:2], start=True, stop=True).then_inc(s.c3_norm, 1)
        pe.wait_ge(s.c3_relu, 2 * r + 1)
        for im in range(2):
            for par in range(2):
                rows = slice(par * C, (par + 1) * C)
                for k in range(2):
                    ins = pe.matmul(m.ps[:, 3 + 3 * im + par, k * P:(k + 1) * P],
                                    m.xm[rows, im, 2 * k:2 * k + 2, :].rearrange("p b c -> p (b c)"),
                                    m.xn2[rows, 2 * im:2 * im + 2, 0, :], start=True, stop=True)
            ins.then_inc(s.c3_dots, 1)
        pe.wait_ge(s.c3_tr, r + 2)
        pe.wait_ge(s.c3_added, r + 1)
        for im in range(2):
            pe.wait_ge(s.c3_sq, 2 * r + im + 2)
            for par in range(2):
                for k in range(2):
                    ins = pe.matmul(m.ps[par * C:(par + 1) * C, 5, im * P:(im + 1) * P], m.tr[:, im, k, :],
                                    m.sim3[:, par, im, k, :], start=(k == 0), stop=(k == 1))
        ins.then_inc(s.c3_y, 1)


def c3_act(act, nc, m, s):
    for sem in (s.c3_xm, s.c3_tr, s.c3_relu,):
        act.sem_inc(sem, 1)
    def evacuate(p):
        act.wait_ge(s.c3_nt, p + 2)
        act.wait_ge(s.c3_t, p + 1)
        act.activation(m.xm[:, :, :, :], m.ps[:, 0, :].rearrange("p (im c b) -> p im b c", im=2, b=4),
                       ACT.Copy).then_inc(s.c3_xm, 1)

    def twice(p):
        act.wait_ge(s.c3_xn, p + 1)
        act.wait_ge(s.c3_nt, p + 1)
        act.activation(m.xn2[:, :, 1, :], m.xn2[:, :, 0, :], ACT.Copy).then_inc(s.c3_xn2, 1)

    with act.Fori(0, PAIRS) as p:
        twice(p)
        evacuate(p)
    act.wait_ge(s.c3_shift, 1)
    with act.Fori(0, PAIRS) as r:
        twice(r + PAIRS)
        act.wait_ge(s.c3_dots, 2 * r + 1)
        evacuate(r + PAIRS)
        act.wait_ge(s.c3_t, r + PAIRS + 2)
        act.wait_ge(s.c3_y, r + 1)
        for half in range(2):
            rows = slice(half * C, (half + 1) * C)
            t = m.ps[rows, 1, :].rearrange("p (im k b o) -> p im k b o", im=2, k=2, b=2)[:, :, :, half, :]
            ins = act.activation(m.tr[rows, :, :, :], t, ACT.Relu, scale=m.bn_scale[rows, :],
                                 bias=m.bn_shift[rows, :])
        ins.then_inc(s.c3_tr, 1)
        act.wait_ge(s.c3_inv, r + 2)
        for im in range(2):
            act.wait_ge(s.c3_dots, 2 * r + im + 2)
            act.wait_ge(s.c3_sq, 2 * r + 1)
            for par in range(2):
                ins = act.activation(m.relu[:, im, par * 2 * P:(par + 1) * 2 * P],
                                     m.ps[:, 3 + 3 * im + par, 0:2 * P], ACT.Relu, scale=m.inv3[:, im:im + 1])
            ins.then_inc(s.c3_relu, 1)


def c3_dve(dve, nc, m, s):
    for sem in (s.c3_t_read, s.c3_inv, s.c3_added, s.c3_sq,):
        dve.sem_inc(sem, 1)
    o = Order(dve, s.c3_order)

    def tokens(p, q, first):
        x = m.X[:, bass.ds(q * PT, PT), :]
        ln_stats(dve, o, m, x, PT, s.c3_mv)
        dve.wait_ge(s.c3_rstd, p + 1)
        o.then(dve.tensor_tensor(m.xc[:, 0:PT, :], x, bcast(m.mv[:, 0:PT, 0:1], [P, PT, C]), ALU.subtract))
        dve.wait_ge(s.c3_nt, p + 1)
        if not first:
            dve.wait_ge(s.c3_dots, 2 * q + 1)
        dve.tensor_tensor(m.xn2[:, :, 0, :], m.xc[:, 0:PT, :], bcast(m.rstd[:, 0:PT].unsqueeze(2), [P, PT, C]),
                          ALU.mult).then_inc(s.c3_xn, 1)

    with o.turns(PAIRS, 2) as p:
        tokens(p, p, True)
        wait_apart(dve, m, s.c3_t, p + 2)
        dve.bn_stats(m.bstats[:, bass.ds(p, 1), :].rearrange("p a b -> p (a b)"), m.ps[:, 1, :])\
            .then_inc(s.c3_t_read, 1)
    dve.wait_ge(s.c3_t_read, PAIRS + 1)
    dve.bn_aggr(m.bmv[:, :], m.bstats[:, :, :].rearrange("p a b -> p (a b)")).then_inc(s.c3_bmv, 1)
    dve.wait_ge(s.c3_bmv, 1)
    o.then(dve.tensor_tensor(m.bn_mean[:, :], m.bmv[:, 0:1], m.bn_in[:, 0:1], ALU.add))
    o.then(dve.tensor_tensor(m.bn_shift[:, :], m.bn_in[:, 0:1], m.bn_mean[:, :], ALU.subtract))
    dve.wait_ge(s.c3_brstd, 1)
    o.then(dve.tensor_tensor(m.bn_scale[:, :], m.brstd[:, :], m.bn_in[:, 1:2], ALU.mult))
    o.then(dve.tensor_tensor(m.bn_shift[:, :], m.bn_shift[:, :], m.bn_scale[:, :], ALU.mult))
    dve.tensor_tensor(m.bn_shift[:, :], m.bn_shift[:, :], m.bn_in[:, 2:3], ALU.add).then_inc(s.c3_shift, 1)
    with o.turns(PAIRS, 3) as r:
        tokens(r + PAIRS, r, False)
        dve.wait_ge(s.c3_xn, r + PAIRS + 1)
        o.then(dve.tensor_tensor(m.xc[:, 0:PT, :], m.xn2[:, :, 0, :], m.xn2[:, :, 0, :], ALU.mult))
        dve.wait_ge(s.c3_norm, r + 1)
        dve.tensor_reduce(m.n2[:, 0:2], m.xc[:, 0:PT, :].rearrange("p (im t) c -> p im (t c)", im=2), AX, ALU.add)\
            .then_inc(s.c3_sumsq, 1)
        dve.wait_ge(s.c3_norm, r + 2)
        dve.wait_ge(s.c3_relu, 2 * r + 1)
        dve.reciprocal(m.inv3[:, :], m.ps[:, 2, 0:2]).then_inc(s.c3_inv, 1)
        for im in range(2):
            dve.wait_ge(s.c3_relu, 2 * r + im + 2)
            dve.wait_ge(s.c3_y, r + 1)
            src = m.relu[:, im, :].rearrange("p (a k n) -> p a (k n)", a=2, k=2)
            dve.tensor_tensor(m.sim3[:, :, im, :, :].rearrange("p a k n -> p a (k n)"), src, src, ALU.mult)\
                .then_inc(s.c3_sq, 1)
        dve.wait_ge(s.c3_y, r + 2)
        x = m.X[:, bass.ds(r * PT, PT), :]
        dve.tensor_tensor(x, x, m.ps[:, 5, 0:PT * C].rearrange("p (t c) -> p t c", c=C), ALU.add)\
            .then_inc(s.c3_added, 1)


def c3_pool(pool, nc, m, s):
    o = Order(pool, s.c3_pool_order)
    with o.turns(PAIRS, 1) as p:
        wait_apart(pool, m, s.c3_mv, p + 1)
        ln_rstd(pool, o, m, PT, 1e-6, s.c3_rstd)
    pool.wait_ge(s.c3_bmv, 1)
    o.then(pool.tensor_scalar(m.bveps[:, :], m.bmv[:, 1:2], 1e-5, 1.0, ALU.add, ALU.mult))
    pool.tensor_tensor(m.brstd[:, :], m.bveps[:, :], m.minus_half[:, 0:1], ALU.pow).then_inc(s.c3_brstd, 1)
    with o.turns(PAIRS, 1) as p:
        wait_apart(pool, m, s.c3_mv, p + PAIRS + 1)
        ln_rstd(pool, o, m, PT, 1e-6, s.c3_rstd)



def prepare_pe(pe, nc, m, s):
    pe.wait_ge(s.ld_small, 16 * SMALL_LOADS)
    pe.wait_ge(s.ld_ident, 16)
    for k, (slot, n) in enumerate(((3, 65), (4, 65), (5, 64), (6, 65), (7, 64), (1, 65), (2, 65))):
        pe.transpose(m.ps[0:n, 0, k * C:(k + 1) * C], m.nat[0:C, slot, 0:n], m.ident[0:C, 0:C])
    pe.transpose(m.ps[:, 1, 0:B1ROWS], m.b1nat[:, :], m.ident[0:B1ROWS, 0:B1ROWS]).then_inc(s.weights_t, 1)


def prepare_act(act, nc, m, s):
    act.wait_ge(s.weights_t, 1)
    act.wait_ge(s.padded, 1)
    act.activation(m.wqk[:, 0:C], m.ps[0:C + 1, 0, 5 * C:6 * C], ACT.Copy, scale=SCALE)
    act.activation(m.wqk[:, C:2 * C], m.ps[0:C + 1, 0, 6 * C:7 * C], ACT.Copy)
    act.activation(m.wv[:, :], m.ps[0:C + 1, 0, 0:C], ACT.Copy)
    act.activation(m.wpn[:, :], m.ps[0:C + 1, 0, C:2 * C], ACT.Copy)
    act.activation(m.wpp[:, :], m.ps[0:C, 0, 2 * C:3 * C], ACT.Copy)
    act.activation(m.w_l2[:, :], m.ps[0:C + 1, 0, 3 * C:4 * C], ACT.Copy)
    for k in range(2):
        act.activation(m.w_l3[:, k * C:(k + 1) * C], m.ps[0:C, 0, 4 * C:5 * C], ACT.Copy)
    act.activation(m.b1t[:, :], m.ps[:, 1, 0:B1ROWS], ACT.Copy)
    act.activation(m.mask[:, :], m.mask_in, ACT.Copy, scale=NEG)
    act.activation(m.identb[:, :], m.ident[:, :], ACT.Copy).then_inc(s.prepared, 1)


def prepare_dve(dve, nc, m, s):
    o = Order(dve, s.prep_order)
    dve.wait_ge(s.ld_small, 16 * SMALL_LOADS)
    neg = m.partsel[:, 2:4]
    o.then(dve.tensor_scalar(neg, m.partsel[:, 0:2], -1.0, None, ALU.mult))
    for k in range(2):
        o.then(dve.tensor_copy(m.b2p[:, :, :], m.b2[:, :, :]))
        o.then(dve.scalar_tensor_tensor(m.b2[:, :, :], m.b2p[:, :, :], neg[:, k:k + 1], m.b2[:, :, :],
                                        ALU.mult, ALU.add))
    o.then(dve.tensor_copy(m.b2p[:, :, :], m.b2[:, :, :]))



def out_dve(dve, nc, m, s):
    with dve.Fori(0, PAIRS) as g:
        dve.wait_ge(s.out_t, g + 1)
        x = m.X[:, bass.ds(g * PT, PT), :]
        dve.tensor_copy(m.stage[:, :, :, :], x.rearrange("p (a i) c -> p i a c", i=2)).then_inc(s.out_x, 1)


def out_pe(pe, nc, m, s):
    pe.sem_inc(s.out_t, 1)
    pe.sem_inc(s.out_y, 1)
    with pe.Fori(0, PAIRS) as g:
        pe.wait_ge(s.out_x, g + 1)
        pe.wait_ge(s.out_y, g + 1)
        for i in range(2):
            ins = pe.transpose(m.ps[:, 0, i * P:(i + 1) * P], m.stage[:, i, :, :], m.ident[:])
        ins.then_inc(s.out_t, 1)


def out_act(act, nc, m, s):
    with act.Fori(0, PAIRS) as g:
        act.wait_ge(s.out_t, g + 2)
        act.activation(m.y[:, bass.ds(g, 1), :].rearrange("p a n -> p (a n)"), m.ps[:, 0, 0:PLACES], ACT.Copy).then_inc(s.out_y, 1)


def out_sync(sp, nc, m, s, out):
    y = out.rearrange("(g a) c h w -> g (a c) (h w)", a=2)
    with sp.Fori(0, PAIRS) as g:
        sp.wait_ge(s.out_y, g + 2)
        sp.dma_start(y[bass.ds(g, 1), :, :].rearrange("g p w -> p (g w)"),
                     m.y[:, bass.ds(g, 1), :].rearrange("p a n -> p (a n)")).then_inc(s.out_sent, 16)
    sp.wait_ge(s.out_sent, 16 * PAIRS)


FFN_SEMS = ["mv", "rstd", "xn", "part1", "rest", "part2", "parts", "transposed", "xa", "xb", "logits",
            "logits_read", "hidden", "act", "silu", "down", "weighed", "added", "below_max", "exps",
            "order", "pool_order"]
SEMS = ["ld_ident", "ld_first", "ld_up", "ld_small", "codes_t", "codes_sq", "codes_n", "codes_ready",
        "c0_in",
        "c2_mv", "c2_rstd", "c2_xn", "c2_nt", "c2_xf", "c2_nq", "c2_inv", "c2_relu", "c2_dots", "c2_tx", "c2_lin", "c2_added", "c2_sim", "c2_y", "c2_sq", "c2_order", "c2_pool_order",
        "c3_mv", "c3_rstd", "c3_xn", "c3_xn2", "c3_nt", "c3_xm", "c3_t", "c3_t_read", "c3_bmv", "c3_brstd", "c3_shift", "c3_sumsq", "c3_norm", "c3_inv", "c3_dots", "c3_relu", "c3_tr", "c3_sq", "c3_y", "c3_added", "c3_order", "c3_pool_order",
        "c1_mv", "c1_rstd", "c1_xn", "c1_nt", "c1_xf", "c1_qk", "c1_part1", "c1_part2", "c1_part3", "c1_rest", "c1_selq", "c1_selk", "c1_qs", "c1_ks", "sel_order", "c1_v", "c1_v_read", "c1_s", "c1_max", "c1_m", "c1_mt", "c1_q2", "c1_st", "c1_p", "c1_o", "c1_em", "c1_on", "c1_ot", "c1_ot_read", "c1_y", "c1_added", "c1_order", "c1_pool_order", "c0_xt", "c0_mv", "c0_rstd", "c0_xn", "c0_nt", "c0_xf", "c0_zp", "c0_z", "c0_read",
        "c0_scored", "ones_rows", "split_a", "split_r", "split_b", "c0_order", "c0_pool_order",
        "weights_t", "padded", "prepared", "prep_order", "out_t", "out_x", "out_y", "out_sent", "part_done", "apart"]


FfnSems = namedtuple("FfnSems", FFN_SEMS)
Sems = namedtuple("Sems", SEMS + ["c0_gathered", "ffn"])


class Memory:
    pass


def program(nc, d, out):
    with ExitStack() as ctx:
        m = Memory()

        def sb(name, shape, dt=F32):
            return ctx.enter_context(nc.sbuf_tensor(name, shape, dt))

        new = lambda name: ctx.enter_context(nc.semaphore(name))
        s = Sems(*[new(n) for n in SEMS],
                 c0_gathered=[new(f"c0_gathered{j}") for j in range(PT)],
                 ffn=[FfnSems(*[new(f"ffn{l}_{n}") for n in FFN_SEMS]) for l in range(2)] * 2)
        m.apart = s.apart
        m.ps = ctx.enter_context(nc.psum_tensor("ps", [P, 8, 512], F32))
        m.X = sb("X", [P, TILES, C])
        m.ident = sb("ident", [P, P])
        m.identb = sb("identb", [P, P], BF16)
        m.nat = sb("nat", [C, 8, C + 1])
        m.emb = sb("emb", [P, CODES // P, C])
        m.codes2 = sb("codes2", [C + 1, CODES])
        m.proj0 = sb("proj0", [C + 1, C])
        m.minus_one = sb("minus_one", [P, C + 1])
        m.minus_half = sb("minus_half", [P, ST])
        m.xload = sb("xload", [P, PLACES])
        m.stats = sb("stats", [P, ST, 6])
        m.mv = sb("mv", [P, ST, 2])
        m.veps = sb("veps", [P, ST])
        m.rstd = sb("rstd", [P, ST])
        m.xc = sb("xc", [P, ST, C])
        m.xn = sb("xn", [P, ST, C])
        m.xf = sb("xf", [C + 1, 512])
        m.z = sb("z", [C + 1, 512])
        m.best = sb("best", [P, PT, 8])
        m.code = sb("code", [P, PT, 8], U32)
        m.zq = [sb(f"zq{j}", [P, C]) for j in range(PT)]
        m.wall = sb("wall", [P, WPAD + 8])
        m.w1 = sb("w1", [P, WPAD], BF16)
        m.w2 = sb("w2", [P, WPAD], BF16)
        m.w3 = sb("w3", [P, WPAD], BF16)
        m.gate_b = {l: sb(f"gate_b{l}", [P, FFN[l]["E"]]) for l in (0, 2, 3)}
        m.down = [sb(f"down{l}", [P, ffn_counts(l)[1], C]) for l in range(4)]
        m.b1nat = sb("b1nat", [B1ROWS, P])
        m.b1t = sb("b1t", [P, B1ROWS])
        m.b2 = sb("b2", [3, B2ROWS, C])
        m.b2p = sb("b2p", [3, B2ROWS, C], BF16)
        m.partsel = sb("partsel", [3, 4])
        m.ones3 = sb("ones3", [3, P], BF16)
        m.bn_in = sb("bn_in", [P, 3])
        m.mask = sb("mask", [P, MASK_COLS], BF16)
        m.padn = sb("padn", [P, 2 * HEADS])
        m.padmax = sb("padmax", [P, 2 * HEADS])
        m.iota = sb("iota", [P, 16])
        m.wqk = sb("wqk", [C + 1, 2 * C])
        m.wv = sb("wv", [C + 1, C])
        m.wpn = sb("wpn", [C + 1, C])
        m.wpp = sb("wpp", [C, C])
        m.w_l2 = sb("w_l2", [C + 1, C])
        m.w_l3 = sb("w_l3", [C, P])
        m.parts = sb("parts", [P, ST, 3, C], BF16)
        m.xa = sb("xa", [P, SPAN], BF16)
        m.xb = sb("xb", [P, SPAN], BF16)
        m.hid = m.wall[:, 0:2 * SPAN].rearrange("p (a n) -> p a n", a=2)
        m.silu = m.wall[:, 2 * SPAN:3 * SPAN].rearrange("p (a n) -> p a n", a=2)
        m.prod = m.wall[:, 3 * SPAN:4 * SPAN].rearrange("p (a t c) -> p a t c", a=2, t=ST)
        m.sel = m.wall[:, 4 * SPAN:4 * SPAN + 2 * 3 * BLOCKS * P // 2].bitcast(BF16).rearrange(
            "p (a k b r) -> p a k b r", a=2, k=3, b=BLOCKS)
        m.qkp = m.parts[:, :, :, :].rearrange("p t k c -> p (t k c)").rearrange("p (k n) -> p k n", k=3)
        m.qk_rest = m.xa[:, :].bitcast(F32)
        m.y = m.wall[:, 0:PAIRS * PLACES].rearrange("p (g n) -> p g n", g=PAIRS)
        m.xfp = sb("xfp", [C + 1, 512])
        m.qs = sb("qs", [P, BLOCKS, 512], BF16)
        m.ks = sb("ks", [P, BLOCKS, 512], BF16)
        m.q2 = sb("q2", [P, BLOCKS, PLACES], BF16)
        m.vals = sb("vals", [P, PT, HEADS, HD + 1])
        m.maxr = sb("maxr", [P, PT, HEADS])
        m.maxp = sb("maxp", [P, PT, HEADS])
        m.maxes = sb("maxes", [P, PT, BLOCKS, P], BF16)
        m.maxparts = sb("maxparts", [P, 2, HEADS, 3], BF16)
        m.maxrest = sb("maxrest", [P, 2, HEADS])
        m.minus_rows = sb("minus_rows", [P, 1])
        m.pt = sb("pt", [P, PT, BANKS3])
        m.emax = sb("emax", [P, PT, HEADS])
        m.den = sb("den", [P, PT, HEADS])
        m.rden = sb("rden", [P, PT, HEADS])
        m.att = sb("att", [P, PT, C])
        m.ot1 = sb("ot1", [C + 1, 512])
        m.ot2 = sb("ot2", [C, 512])
        m.one = sb("one", [P, P])
        m.xsq = sb("xsq", [C, 512])
        m.n2 = sb("n2", [P, PT])
        m.codes_sq = m.pt[0:C, 0, 0:CODES]
        m.wrest = m.pt[:, 1, 0:WCHUNK]
        m.mask_in = m.pt[:, 2, 0:MASK_COLS]
        room = m.pt[:, :, :].rearrange("p t k -> p (t k)")
        m.d2, m.inv, m.relu, m.relu2, m.sim = (
            room[:, k * 1024:(k + 1) * 1024].rearrange("p (im q) -> p im q", im=2) for k in range(5))
        m.sim3 = m.d2.rearrange("p im q -> p (im q)").rearrange("p (a im k n) -> p a im k n", a=2, im=2, k=2)
        m.sim = m.sim.rearrange("p im (k q) -> p im k q", k=2)
        m.tx = sb("tx", [P, PT, C])
        m.xn2 = sb("xn2", [P, PT, 2, C])
        m.xm = sb("xm", [P, 2, 4, C])
        m.tr = sb("tr", [P, 2, 2, C])
        m.inv3 = sb("inv3", [P, 2])
        m.bstats = sb("bstats", [P, PAIRS, 6])
        m.bmv = sb("bmv", [P, 2])
        m.bn_mean, m.bn_scale, m.bn_shift, m.brstd, m.bveps = (
            sb(name, [P, 1]) for name in ("bn_mean", "bn_scale", "bn_shift", "brstd", "bveps"))
        m.lg = sb("lg", [P, ST, 16])
        m.below = sb("below", [P, ST, 17])
        m.ex = sb("ex", [P, ST, 17])
        m.top = sb("top", [P, ST, 8])
        m.topi = sb("topi", [P, ST, 8], U32)
        m.topf = sb("topf", [P, ST, 2])
        m.hit = sb("hit", [P, 2, ST, 16])
        m.sums = sb("sums", [P, ST])
        m.rsum = sb("rsum", [P, ST])
        m.prob = sb("prob", [P, 2, ST])
        m.cw = sb("cw", [P, ST, 16])
        m.stage = sb("stage", [P, 2, 2, C])
        block = ctx.enter_context(nc.Block())

        @block.sync
        def _(sp):
            load_sync(sp, nc, m, s, d)
            xs = d.x.rearrange("(g a) c h w -> g (a c) (h w)", a=2)
            sp.dma_start(m.xload[:, :], xs[0]).then_inc(s.c0_in, 16)
            with sp.Fori(1, PAIRS) as g:
                sp.wait_ge(s.c0_xt, g)
                sp.dma_start(m.xload[:, :], xs[bass.ds(g, 1), :, :].rearrange("g p w -> p (g w)"))\
                    .then_inc(s.c0_in, 16)
            out_sync(sp, nc, m, s, out)

        @block.tensor
        def _(pe):
            c0_pe(pe, nc, m, s)
            barrier(pe, s, 1)
            prepare_pe(pe, nc, m, s)
            barrier(pe, s, 2)
            ffn_pe(pe, nc, m, s, 0)
            barrier(pe, s, 3)
            c1_pe(pe, nc, m, s)
            barrier(pe, s, 4)
            ffn_pe(pe, nc, m, s, 1)
            barrier(pe, s, 5)
            c2_pe(pe, nc, m, s)
            barrier(pe, s, 6)
            ffn_pe(pe, nc, m, s, 2)
            barrier(pe, s, 7)
            c3_pe(pe, nc, m, s)
            barrier(pe, s, 8)
            ffn_pe(pe, nc, m, s, 3)
            barrier(pe, s, 9)
            out_pe(pe, nc, m, s)

        @block.scalar
        def _(act):
            load_rest(act, nc, m, s, d)
            c0_act(act, nc, m, s)
            barrier(act, s, 1)
            prepare_act(act, nc, m, s)
            barrier(act, s, 2)
            ffn_act(act, nc, m, s, 0)
            barrier(act, s, 3)
            c1_act(act, nc, m, s)
            barrier(act, s, 4)
            ffn_act(act, nc, m, s, 1)
            barrier(act, s, 5)
            c2_act(act, nc, m, s)
            barrier(act, s, 6)
            ffn_act(act, nc, m, s, 2)
            barrier(act, s, 7)
            c3_act(act, nc, m, s)
            barrier(act, s, 8)
            ffn_act(act, nc, m, s, 3)
            barrier(act, s, 9)
            out_act(act, nc, m, s)

        @block.vector
        def _(dve):
            c0_dve(dve, nc, m, s)
            barrier(dve, s, 1)
            prepare_dve(dve, nc, m, s)
            barrier(dve, s, 2)
            ffn_dve(dve, nc, m, s, 0)
            barrier(dve, s, 3)
            c1_dve(dve, nc, m, s)
            barrier(dve, s, 4)
            ffn_dve(dve, nc, m, s, 1)
            barrier(dve, s, 5)
            c2_dve(dve, nc, m, s)
            barrier(dve, s, 6)
            ffn_dve(dve, nc, m, s, 2)
            barrier(dve, s, 7)
            c3_dve(dve, nc, m, s)
            barrier(dve, s, 8)
            ffn_dve(dve, nc, m, s, 3)
            barrier(dve, s, 9)
            out_dve(dve, nc, m, s)

        @block.gpsimd
        def _(pool):
            c0_pool(pool, nc, m, s, d)
            barrier(pool, s, 1)
            make_sel(pool, m, s)
            barrier(pool, s, 2)
            ffn_pool(pool, nc, m, s, 0)
            barrier(pool, s, 3)
            c1_pool(pool, nc, m, s)
            barrier(pool, s, 4)
            ffn_pool(pool, nc, m, s, 1)
            barrier(pool, s, 5)
            c2_pool(pool, nc, m, s)
            barrier(pool, s, 6)
            ffn_pool(pool, nc, m, s, 2)
            barrier(pool, s, 7)
            c3_pool(pool, nc, m, s)
            barrier(pool, s, 8)
            ffn_pool(pool, nc, m, s, 3)
            barrier(pool, s, 9)


def attention_tables():
    mask = np.zeros((P, MASK_COLS), np.float32)
    padn = np.zeros((P, 2, HEADS), np.float32)
    for t in range(2):
        for r in range(P):
            for (ks, dil, heads), (kind, lo) in zip(RANGES, (("near", 0), ("rows", 1), ("all", 2))):
                y, x = place(kind, t, r)
                reach = ks // 2
                inside = 0
                for c in range(WIDTH[kind]):
                    ky, kx = key_place(kind, t, c)
                    dy, dx = ky - y, kx - x
                    sees = dy % dil == 0 and dx % dil == 0 and abs(dy) <= reach * dil and abs(dx) <= reach * dil
                    inside += sees
                    mask[r, t * MASK_TILE + MASK_AT[kind] + c] = not sees
                for h in heads:
                    padn[r, t, (0, 1, 2, 3, 7, 4, 5, 6).index(h)] = ks * ks - inside
    padmax = np.where(padn > 0, 0.0, -3e38).astype(np.float32)
    return mask, padn.reshape(P, -1), padmax.reshape(P, -1)


WIDTH = dict(near=160, rows=128, all=256)
MASK_AT = dict(near=0, all=160, rows=416)
MASK_TILE = 160 + 128 + 256
MASK_COLS = 2 * MASK_TILE


def place(kind, t, r):
    if kind == "rows":
        return 2 * (r // SIDE) + t, r % SIDE
    return (t * P + r) // SIDE, r % SIDE


def key_place(kind, t, c):
    if kind == "rows":
        return place(kind, t, c)
    if kind == "near":
        c += t * (PLACES - WIDTH["near"])
    return c // SIDE, c % SIDE


def constants():
    mask, padn, padmax = attention_tables()
    partsel = np.array([[0, 0, 0, 0], [1, 0, 0, 0], [1, 1, 0, 0]], np.float32)[:, :2].copy()
    minus_rows = np.zeros((P, 1), np.float32)
    for half in range(2):
        at = half * C + SPLIT_ROWS
        minus_rows[at:at + 3] = -1.0
    return dict(minus_rows=minus_rows, ident=np.eye(P, dtype=np.float32), mask_table=mask, padn=padn, padmax=padmax, partsel=partsel,
                iota=np.tile(np.arange(16, dtype=np.float32), (P, 1)))


INPUTS = [
    "x", "L0_conv_proj_w", "L0_conv_proj_b", "L0_conv_emb",
    "L0_ffn_gate_w", "L0_ffn_gate_b", "L0_ffn_W1", "L0_ffn_b1", "L0_ffn_W2", "L0_ffn_b2",
    "L1_conv_qkv_w0", "L1_conv_qkv_b0", "L1_conv_qkv_w1", "L1_conv_qkv_b1", "L1_conv_qkv_w2", "L1_conv_qkv_b2",
    "L1_conv_proj_w", "L1_conv_proj_b",
    "L1_ffn_router_w", "L1_ffn_w1", "L1_ffn_b1", "L1_ffn_w2", "L1_ffn_b2",
    "L2_conv_W", "L2_conv_bias", "L2_ffn_gate_w", "L2_ffn_gate_b", "L2_ffn_w1", "L2_ffn_w2", "L2_ffn_w3",
    "L3_conv_conv_w", "L3_conv_conv_b", "L3_conv_bn_gamma", "L3_conv_bn_beta",
    "L3_ffn_gate_w", "L3_ffn_gate_b", "L3_ffn_W1", "L3_ffn_b1", "L3_ffn_W2", "L3_ffn_b2"]


def kernel(**inputs):
    import concourse.bacc as bacc
    from concourse.bass_utils import run_bass_kernel_spmd

    nc = bacc.Bacc("TRN2", target_bir_lowering=False, num_devices=1)
    arrays, args = {}, {}
    for name, a in list({n: inputs[n] for n in INPUTS}.items()) + list(constants().items()):
        a = np.ascontiguousarray(a)
        arrays[f"in_{name}_dram"] = a
        args[name] = nc.dram_tensor(f"in_{name}_dram", a.shape, mybir.dt.from_np(a.dtype), kind="ExternalInput").ap()
    out = nc.dram_tensor("out_dram", (IMAGES, C, SIDE, SIDE), F32, kind="ExternalOutput").ap()
    program(nc, namedtuple("Inputs", list(args))(**args), out)
    r = run_bass_kernel_spmd(nc, [arrays], core_ids=[0])
    return r.results[0]["out_dram"]
```

```python
from collections import namedtuple
from contextlib import ExitStack, contextmanager

import numpy as np

import concourse.bass as bass
from concourse import mybir

F32 = mybir.dt.float32
BF16 = mybir.dt.bfloat16
U32 = mybir.dt.uint32
ALU = mybir.AluOpType
ACT = mybir.ActivationFunctionType
AX = mybir.AxisListType.X

P = 128
C = 64
IMAGES = 16
SIDE = 16
PLACES = SIDE * SIDE
TILES = IMAGES * PLACES // P
CODES = 1024
PAIRS = IMAGES // 2
PT = TILES // PAIRS
SUPERS = 4
ST = TILES // SUPERS
SPAN = ST * P
HALF = SPAN // 2

HEADS, HD = 8, 8
SCALE = HD ** -0.5
NEG = -1e30

RANGES = [(5, 1, (0, 1, 2, 3)), (7, 2, (4, 5, 6)), (9, 3, (7,))]

FFN = [
    dict(E=8, H=128, gated=False, renorm=False, floor=None, gate_b=True, b1=True, b2=True, keep=False),
    dict(E=8, H=64, gated=False, renorm=True, floor=1e-12, gate_b=False, b1=True, b2=True, keep=True),
    dict(E=16, H=128, gated=True, renorm=True, floor=None, gate_b=True, b1=False, b2=False, keep=False),
    dict(E=8, H=128, gated=False, renorm=False, floor=None, gate_b=True, b1=True, b2=True, keep=False),
]


def weight_columns():
    at, where = 0, []
    for f in FFN:
        w = dict(up=at)
        at += f["E"] * f["H"]
        if f["gated"]:
            w["up2"] = at
            at += f["E"] * f["H"]
        w["gate"] = at
        at += f["E"]
        where.append(w)
    return where, at


WHERE, WCOLS = weight_columns()
SPLIT_TURNS = PAIRS - 1
WPAD = -(-WCOLS // SPLIT_TURNS) * SPLIT_TURNS
WCHUNK = WPAD // SPLIT_TURNS
E1 = [0, 8, None, 12]
E2 = [0, 8, None, 16]
B1ROWS, B2ROWS = 20, 24


class Order:

    def __init__(self, eng, sem):
        self.eng, self.sem, self.base, self.n = eng, sem, 0, 0

    def step(self, ins):
        ins.then_inc(self.sem, 1)
        self.n += 1
        return self.base + self.n

    def then(self, ins):
        self.eng.wait_ge(self.sem, self.step(ins))

    def then_apart(self, ins, m):
        wait_apart(self.eng, m, self.sem, self.step(ins))

    @contextmanager
    def turns(self, count, per):
        start = self.base + self.n
        with self.eng.Fori(0, count) as i:
            self.base, self.n = i * per + start, 0
            yield i
            assert self.n == per, f"{self.n} steps a turn, not {per}"
        self.base, self.n = start + count * per, 0


def barrier(eng, s, n):
    eng.drain().then_inc(s.part_done, 1)
    eng.wait_ge(s.part_done, 4 * n)


def wait_apart(eng, m, sem, value):
    eng.wait_ge(sem, value)
    eng.sem_inc(m.apart, 1)


def bcast(ap, shape):
    return ap.broadcast_to(shape)



def ln_stats(dve, o, m, x, n, done):
    for j in range(n):
        ins = dve.bn_stats(m.stats[:, j, :], x[:, j, :])
    o.then_apart(ins, m)
    for j in range(n):
        ins = dve.bn_aggr(m.mv[:, j, :], m.stats[:, j, :])
    ins.then_inc(done, 1)


def ln_rstd(pool, o, m, n, eps, done):
    o.then(pool.tensor_scalar(m.veps[:, 0:n], m.mv[:, 0:n, 1], eps, 1.0, ALU.add, ALU.mult))
    pool.tensor_tensor(m.rstd[:, 0:n], m.veps[:, 0:n], m.minus_half[:, 0:n], ALU.pow).then_inc(done, 1)


def ln_apply(dve, o, m, x, n, done):
    o.then(dve.tensor_tensor(m.xc[:, 0:n, :], x, bcast(m.mv[:, 0:n, 0:1], [P, n, C]), ALU.subtract))
    dve.tensor_tensor(m.xn[:, 0:n, :], m.xc[:, 0:n, :], bcast(m.rstd[:, 0:n].unsqueeze(2), [P, n, C]),
                      ALU.mult).then_inc(done, 1)



def load_first(sp, nc, m, s, d):
    sp.dma_start(m.ident[:], d.ident).then_inc(s.ld_ident, 16)
    sp.dma_start(m.xload[:, :], pair_of_images(d.x, 0)).then_inc(s.c0_in, 16)
    loads = [
        (m.emb[:, :, 0, :], d.L0_conv_emb.rearrange("(k p) c -> p k c", p=P)),
        (m.emb[:, :, 1, :], d.L0_conv_emb.rearrange("(k p) c -> p k c", p=P)),
        (m.nat[0:C, 0, 0:C], d.L0_conv_proj_w),
        (m.nat[0:C, 0, C:C + 1], d.L0_conv_proj_b.rearrange("(o a) -> o a", a=1)),
        (m.partsel[:, 0:2], d.partsel),
    ]
    for dst, src in loads:
        sp.dma_start(dst, src, allow_slow_non_contiguous=src.shape[-1] == 1).then_inc(s.ld_first, 16)
    assert len(loads) == FIRST_LOADS


def pair_of_images(x, g):
    return x.rearrange("(g a) c h w -> g (a c) (h w)", a=2)[bass.ds(g, 1), :, :].rearrange("g p w -> p (g w)")


FIRST_LOADS = 5


def load_rest(q, nc, m, s, d, next_pair):
    n = 0

    def ld(dst, src, sem, slow=False):
        nonlocal n
        q.dma_start(dst, src, allow_slow_non_contiguous=src.shape[-1] == 1 or slow).then_inc(sem, 16)
        n += 1

    for half in range(2):
        rows = slice(half * C, half * C + C)
        for f, (cfg, w) in enumerate(zip(FFN, WHERE)):
            E, H = cfg["E"], cfg["H"]
            ups = {0: [d.L0_ffn_W1], 1: [d.L1_ffn_w1], 2: [d.L2_ffn_w1, d.L2_ffn_w2], 3: [d.L3_ffn_W1]}[f]
            for key, up in zip(("up", "up2"), ups):
                ld(m.wall[rows, w[key]:w[key] + E * H].rearrange("c (e h) -> c e h", e=E),
                   up.rearrange("e c h -> c e h"), s.ld_up)
            gate = {0: d.L0_ffn_gate_w, 1: d.L1_ffn_router_w.rearrange("e c -> c e"),
                    2: d.L2_ffn_gate_w, 3: d.L3_ffn_gate_w}[f]
            ld(m.wall[rows, w["gate"]:w["gate"] + E], gate, s.ld_up, slow=f == 1)
    assert n == UP_LOADS
    n = 0
    next_pair()
    for l, gb in ((0, d.L0_ffn_gate_b), (2, d.L2_ffn_gate_b), (3, d.L3_ffn_gate_b)):
        ld(m.gate_b[l][:, :], gb.partition_broadcast(P), s.ld_small)
    ld(m.down[0][:, :, :], d.L0_ffn_W2.rearrange("e h c -> h e c"), s.ld_small)
    ld(m.down[1][:, :, :], d.L1_ffn_w2.rearrange("(g i) h c -> (i h) g c", i=2), s.ld_small)
    ld(m.down[2][:, :, :], d.L2_ffn_w3.rearrange("e h c -> h e c"), s.ld_small)
    ld(m.down[3][:, :, :], d.L3_ffn_W2.rearrange("e h c -> h e c"), s.ld_small)
    ld(m.b1nat[0:8, :], d.L0_ffn_b1, s.ld_small)
    ld(m.b1nat[8:12, :], d.L1_ffn_b1.rearrange("(g i) h -> g (i h)", i=2), s.ld_small)
    ld(m.b1nat[12:20, :], d.L3_ffn_b1, s.ld_small)
    for l, b2 in ((0, d.L0_ffn_b2), (1, d.L1_ffn_b2), (3, d.L3_ffn_b2)):
        ld(m.b2[:, E2[l]:E2[l] + 8, :], b2.partition_broadcast(3), s.ld_small)
    q.wait_ge(s.padded, 1)
    for slot, off in ((1, 0), (2, C), (3, 2 * C)):
        for (a, b), at, w, bias in (((0, 32), 0, d.L1_conv_qkv_w0, d.L1_conv_qkv_b0),
                                    ((56, 64), 32, d.L1_conv_qkv_w2, d.L1_conv_qkv_b2),
                                    ((32, 56), 40, d.L1_conv_qkv_w1, d.L1_conv_qkv_b1)):
            to = slice(at, at + b - a)
            ld(m.nat[to, slot, 0:C], w[off + a:off + b, :], s.ld_small)
            ld(m.nat[to, slot, C:C + 1], bias[off + a:off + b].rearrange("(o a) -> o a", a=1), s.ld_small)
    ld(m.nat[0:C, 4, 0:32], d.L1_conv_proj_w[:, 0:32], s.ld_small)
    ld(m.nat[0:C, 4, 32:40], d.L1_conv_proj_w[:, 56:64], s.ld_small)
    ld(m.nat[0:C, 4, C:C + 1], d.L1_conv_proj_b.rearrange("(o a) -> o a", a=1), s.ld_small)
    ld(m.nat[0:C, 5, 40:64], d.L1_conv_proj_w[:, 32:56], s.ld_small)
    ld(m.nat[0:C, 6, 0:C], d.L2_conv_W, s.ld_small)
    ld(m.nat[0:C, 6, C:C + 1], d.L2_conv_bias.rearrange("(o a) -> o a", a=1), s.ld_small)
    ld(m.nat[0:C, 7, 0:C], d.L3_conv_conv_w, s.ld_small)
    for half in range(2):
        rows = slice(half * C, half * C + C)
        for k, v in enumerate((d.L3_conv_conv_b, d.L3_conv_bn_gamma, d.L3_conv_bn_beta)):
            ld(m.bn_in[rows, k:k + 1], v.rearrange("(o a) -> o a", a=1), s.ld_small)
    ld(m.mask_in, d.mask_table, s.ld_small)
    ld(m.padn[:, :], d.padn, s.ld_small)
    ld(m.minus_rows[:, :], d.minus_rows, s.ld_small)
    ld(m.padmax[:, :], d.padmax, s.ld_small)
    ld(m.iota[:, :], d.iota, s.ld_small)
    assert n == SMALL_LOADS, n


UP_LOADS = 2 * (5 + 4)
SMALL_LOADS = 3 + 4 + 3 + 3 + 18 + 4 + 3 + 6 + 5



def c0_pe_first(pe, nc, m, s):
    pe.wait_ge(s.ld_first, 16 * FIRST_LOADS)
    pe.transpose(m.ps[0:C + 1, 6, 0:C], m.nat[0:C, 0, :], m.ident[0:C, 0:C])
    for k in range(CODES // P):
        ins = pe.transpose(m.ps[:, k // 4, (k % 4) * P:(k % 4 + 1) * P],
                           m.emb[:, k, :, :].rearrange("p a c -> p (a c)"), m.ident[:])
    ins.then_inc(s.codes_t, 1)
    pe.wait_ge(s.codes_sq, 1)
    pe.wait_ge(s.ones_rows, 1)
    for k in range(2):
        ins = pe.matmul(m.ps[0:3, 2 + k, :], m.minus_one[0:C, 0:3], m.codes_sq[:, k * 512:(k + 1) * 512],
                        start=True, stop=True)
    ins.then_inc(s.codes_n, 1)


def c0_act_first(act, nc, m, s):
    codes = m.ps[:, 0:2, :].rearrange("c a k -> c (a k)")
    act.wait_ge(s.codes_t, 1)
    act.activation(m.codes_sq[:, :], codes[0:C, :], ACT.Square).then_inc(s.codes_sq, 1)
    act.activation(m.codes_a, codes, ACT.Copy, scale=2.0).then_inc(s.codes_1, 1)
    for half in range(2):
        act.activation(m.proj0[:, half * C:half * C + C], m.ps[0:C + 1, 6, 0:C], ACT.Copy)
    act.wait_ge(s.codes_rest, 1)
    act.activation(m.codes_c[C:P, :], m.codes_a[C:P, :], ACT.Copy)
    act.activation(m.codes_b, m.rest_of_codes[:, :], ACT.Copy).then_inc(s.codes_2, 1)


def c0_dve_first(dve, nc, m, s, o):
    codes = m.ps[:, 0:2, :].rearrange("c a k -> c (a k)")
    neg = m.partsel[:, 2:4]
    dve.wait_ge(s.codes_1, 1)
    dve.scalar_tensor_tensor(m.rest_of_codes[:, :], codes, 2.0, m.codes_a, ALU.mult, ALU.subtract)\
        .then_inc(s.codes_rest, 1)
    dve.wait_ge(s.ld_first, 16 * FIRST_LOADS)
    dve.wait_ge(s.codes_n, 1)
    dve.tensor_copy(m.norms, m.ps[0:3, 2:4, :].rearrange("c a k -> c (a k)"))
    o.then(dve.tensor_scalar(neg, m.partsel[:, 0:2], -1.0, None, ALU.mult))
    for k in range(2):
        o.then(dve.tensor_copy(m.norm_parts[:, :], m.norms))
        o.then(dve.scalar_tensor_tensor(m.norms, m.norm_parts[:, :], neg[:, k:k + 1], m.norms, ALU.mult, ALU.add))
    dve.tensor_copy(m.norm_parts[:, :], m.norms)
    dve.wait_ge(s.codes_2, 1)
    dve.tensor_tensor(m.codes_c[0:C, :], m.rest_of_codes[0:C, :], m.codes_b[0:C, :], ALU.subtract)\
        .then_inc(s.codes_ready, 1)


def c0_xload(pe, m, s, g):
    pe.wait_ge(s.c0_in, (g + 1) * 16)
    for i in range(2):
        ins = pe.transpose(m.ps[:, 4, i * P:(i + 1) * P], m.xload[:, i * P:(i + 1) * P], m.ident[:])
    ins.then_inc(s.c0_xt, 1)


def c0_normt(pe, m, s, g):
    wait_apart(pe, m, s.c0_xn, g + 1)
    for j in range(PT):
        ins = pe.transpose(m.ps[0:C, 5, j * P:(j + 1) * P], m.xn[:, j, :], m.ident[:])
    ins.then_inc(s.c0_nt, 1)


def c0_project(pe, m, s, g):
    pe.wait_ge(s.c0_xf, g + 1)
    pe.matmul(m.ps[:, 4, :], m.proj0[:, :], m.xf[:, :], start=True, stop=True).then_inc(s.c0_zp, 1)


def c0_scores(pe, m, s, g, j, b):
    if j == 0:
        pe.wait_ge(s.c0_z, g + 1)
    pe.wait_ge(s.c0_read, g * PT + j + 1)
    at = slice(b * 512 + j * P, b * 512 + (j + 1) * P)
    za, zb = m.xa[:, at], m.xb[:, at]
    passes = ((m.ones3[:, :], m.norm_parts), (za, m.codes_a), (za, m.codes_b), (zb, m.codes_c))
    for n, (z, codes) in enumerate(passes):
        for k in range(2):
            ins = pe.matmul(m.ps[:, 2 * (j % 2) + k, :], z, codes[:, k * 512:(k + 1) * 512],
                            start=(n == 0), stop=(n == len(passes) - 1))
    ins.then_inc(s.c0_scored, 1)


def c0_pe(pe, nc, m, s):
    pe.wait_ge(s.ld_ident, 16)
    c0_xload(pe, m, s, 0)
    c0_pe_first(pe, nc, m, s)
    c0_normt(pe, m, s, 0)
    c0_project(pe, m, s, 0)
    pe.wait_ge(s.codes_ready, 1)

    def turn(g, b, ahead=True):
        if ahead:
            pe.wait_ge(s.c0_rest, g + 1)
            c0_xload(pe, m, s, g + 1)
        c0_scores(pe, m, s, g, 0, b)
        c0_scores(pe, m, s, g, 1, b)
        if ahead:
            c0_normt(pe, m, s, g + 1)
        c0_scores(pe, m, s, g, 2, b)
        if ahead:
            c0_project(pe, m, s, g + 1)
        c0_scores(pe, m, s, g, 3, b)

    turn(0, 0)
    with pe.Fori(0, PAIRS // 2 - 1) as i:
        turn(2 * i + 1, 1)
        turn(2 * i + 2, 0)
    turn(PAIRS - 1, 1, False)


def c0_act(act, nc, m, s):
    def features(g, first=False):
        act.wait_ge(s.c0_nt, g + 1)
        if not first:
            act.wait_ge(s.c0_zp, g)
        act.activation(m.xf[0:C, :], m.ps[0:C, 5, :], ACT.Copy).then_inc(s.c0_xf, 1)

    def split(g, b):
        cols = slice(b * 512, b * 512 + 512)
        act.wait_ge(s.c0_zp, g + 1)
        act.activation(m.xa[:, cols], m.ps[:, 4, :], ACT.Copy).then_inc(s.c0_z1, 1)
        act.wait_ge(s.c0_rest, g + 1)
        act.activation(m.xb[0:C, cols], m.xa[0:C, cols], ACT.Copy).then_inc(s.c0_z1, 1)
        act.activation(m.xb[C:P, cols], m.z_rest[C:P, :], ACT.Copy)
        act.wait_ge(s.c0_z1, 2 * g + 2)
        act.activation(m.xa[0:C, cols], m.z_rest[0:C, :], ACT.Copy).then_inc(s.c0_z2, 1)

    def turn(g, b, first=False):
        cols = bass.ds(g * WCHUNK, WCHUNK)
        act.activation(m.w1[:, cols], m.wall[:, cols], ACT.Copy)
        act.activation(m.w3[C:P, cols], m.wall[C:P, cols], ACT.Copy).then_inc(s.split_a, 1)
        features(g + 1)
        act.wait_ge(s.split_r, g + 1)
        act.activation(m.w2[:, cols], m.wrest[:, :], ACT.Copy).then_inc(s.split_b, 1)
        if not first:
            act.wait_ge(s.c0_scored, g * PT)
        split(g + 1, 1 - b)

    act.wait_ge(s.ones_rows, 1)
    c0_act_first(act, nc, m, s)
    features(0, True)
    split(0, 0)
    act.wait_ge(s.ld_up, 16 * UP_LOADS)
    turn(0, 0, True)
    with act.Fori(0, PAIRS // 2 - 1) as i:
        turn(2 * i + 1, 1)
        turn(2 * i + 2, 0)


def c0_dve_arrive(dve, o, m, s, g, first):
    x = m.X[:, bass.ds(g * PT, PT), :]
    dve.wait_ge(s.c0_xt, g + 1)
    o.then_apart(dve.tensor_copy(x.rearrange("p (a i) c -> p i a c", i=2),
                                 m.ps[:, 4, 0:2 * P].rearrange("p (i a c) -> p i a c", i=2, a=2)), m)
    ln_stats(dve, o, m, x, PT, s.c0_mv)


def c0_dve_norm(dve, o, m, s, g, first):
    x = m.X[:, bass.ds(g * PT, PT), :]
    dve.wait_ge(s.c0_rstd, g + 1)
    if not first:
        dve.wait_ge(s.c0_nt, g)
    ln_apply(dve, o, m, x, PT, s.c0_xn)


def c0_dve(dve, nc, m, s):
    o = m.dve_order
    dve.memset(m.minus_half[:, :], -0.5)
    dve.memset(m.minus_one[:, :], -1.0)
    dve.memset(m.wall[:, WCOLS:WPAD + 8], 0.0)
    dve.memset(m.ones3[:, :], 1.0)
    dve.memset(m.xf[C:C + 1, :], 1.0).then_inc(s.ones_rows, 1)
    dve.memset(m.one[:, :], 1.0)
    dve.memset(m.nat[:, 1:6, :], 0.0)
    dve.memset(m.maxp[:, :, :], 0.0)
    dve.memset(m.maxes[:, :, :, :], 0.0)
    dve.memset(m.qs[0:C, LOW:, :], 0.0)
    dve.memset(m.vals[:, :, :, HD:HD + 1], 1.0)
    dve.memset(m.xfp[C:C + 1, :], 1.0)
    dve.memset(m.ot1[C:C + 1, :], 1.0)
    o.then(dve.memset(m.maxparts[:, :, :, :], 0.0))
    dve.memset(m.maxrest[:, :, :], 0.0).then_inc(s.padded, 1)
    dve.sem_inc(s.c0_read, 2)
    c0_dve_arrive(dve, o, m, s, 0, True)
    c0_dve_norm(dve, o, m, s, 0, True)
    c0_dve_first(dve, nc, m, s, o)

    def rest(g, b):
        dve.wait_ge(s.c0_z1, 2 * g + 1)
        dve.tensor_tensor(m.z_rest, m.ps[:, 4, :], m.xa[:, b * 512:b * 512 + 512], ALU.subtract).then_inc(s.c0_rest, 1)

    def third(g, b):
        dve.wait_ge(s.c0_z2, g + 1)
        z3 = m.xb[C:P, b * 512:b * 512 + 512]
        dve.tensor_tensor(z3, m.z_rest[C:P, :], z3, ALU.subtract).then_inc(s.c0_z, 1)

    rest(0, 0)
    third(0, 0)

    def argmax(g, j, first=False):
        wait_apart(dve, m, s.c0_scored, g * PT + j + 1)
        sc = m.ps[:, 2 * (j % 2):2 * (j % 2) + 2, :].rearrange("p a k -> p (a k)")
        n = o.step(dve.max(m.best[:, j, :], sc))
        dve.wait_ge(s.dve_order, n)
        if not first:
            wait_apart(dve, m, s.c0_gathered[j], g * 16)
        dve.max_index(m.code[:, j, :], m.best[:, j, :], sc).then_inc(s.c0_read, 1)

    def turn(g, b, first=False):
        c0_dve_arrive(dve, o, m, s, g + 1, False)
        argmax(g, 0, first)
        c0_dve_norm(dve, o, m, s, g + 1, False)
        argmax(g, 1, first)
        rest(g + 1, 1 - b)
        argmax(g, 2, first)
        third(g + 1, 1 - b)
        argmax(g, 3, first)

    turn(0, 0, True)
    with o.turns(PAIRS // 2 - 1, 2 * C0_STEPS) as i:
        turn(2 * i + 1, 1)
        turn(2 * i + 2, 0)
    for j in range(PT):
        argmax(PAIRS - 1, j)


C0_STEPS = 7


def c0_pool(pool, nc, m, s, d):
    o = m.pool_order
    pool.wait_ge(s.ones_rows, 1)
    wait_apart(pool, m, s.c0_mv, 1)
    ln_rstd(pool, o, m, PT, 1e-6, s.c0_rstd)

    def gather(g, j):
        wait_apart(pool, m, s.c0_read, 2 + g * PT + j + 1)
        pool.indirect_dma_start(m.zq[j][:, :], None, d.L0_conv_emb,
                                bass.IndirectOffsetOnAxis(ap=m.code[:, j, 0:1], axis=0))\
            .then_inc(s.c0_gathered[j], 16)

    def add(g):
        for j in range(PT):
            wait_apart(pool, m, s.c0_gathered[j], g * 16 + 16)
            x = m.X[:, bass.ds(g * PT + j, 1), :].rearrange("p a c -> p (a c)")
            ins = pool.tensor_tensor(x, x, m.zq[j][:, :], ALU.add)
        o.then(ins)

    def turn(g, first=False):
        cols = bass.ds(g * WCHUNK, WCHUNK)
        wait_apart(pool, m, s.c0_mv, g + 2)
        ln_rstd(pool, o, m, PT, 1e-6, s.c0_rstd)
        if not first:
            add(g - 1)
        gather(g, 0)
        pool.wait_ge(s.split_a, g + 1)
        pool.tensor_tensor(m.wrest[:, :], m.wall[:, cols], m.w1[:, cols], ALU.subtract).then_inc(s.split_r, 1)
        gather(g, 1)
        gather(g, 2)
        pool.wait_ge(s.split_b, g + 1)
        o.then(pool.tensor_tensor(m.w3[0:C, cols], m.wrest[0:C, :], m.w2[0:C, cols], ALU.subtract))
        gather(g, 3)

    turn(0, True)
    with o.turns(PAIRS - 2, 3) as g:
        turn(g + 1)
    add(PAIRS - 2)
    for j in range(PT):
        gather(PAIRS - 1, j)
    add(PAIRS - 1)



def ffn_counts(l):
    f = FFN[l]
    per = P // f["H"]
    G = f["E"] // per
    return f["E"], G, per, 2 * G


def ffn_pe(pe, nc, m, s, l):
    f, w, q = FFN[l], WHERE[l], s.ffn[l]
    E, G, per, U = ffn_counts(l)
    ahead_at = min(4, G - 1)
    free = 2 if f["gated"] else 4

    def transposes(sb):
        pe.wait_ge(q.parts, sb + 1)
        pe.wait_ge(q.logits_read, sb + 1)
        t6 = m.ps[:, 6, :].bitcast(BF16)
        t7 = m.ps[:, 7, :].bitcast(BF16)
        for t in range(ST):
            pe.transpose(t6[:, t * P:(t + 1) * P], m.parts[:, t, 0:2, :], m.identb[:])
            ins = pe.transpose(t7[:, t * P:(t + 1) * P], m.parts[:, t, 1:3, :], m.identb[:])
        ins.then_inc(q.transposed, 1)

    def three(out, lhs, rhs, stop=True):
        for k, (a, b) in enumerate(zip(lhs, rhs)):
            ins = pe.matmul(out, a, b, start=(k == 0), stop=(k == 2 and stop))
        return ins

    def logits(sb):
        pe.wait_ge(q.xa, sb + 1)
        pe.wait_ge(q.xb, sb + 1)
        gate = slice(w["gate"], w["gate"] + E)
        for t in range(ST):
            a, b = m.xa[:, t * P:(t + 1) * P], m.xb[:, t * P:(t + 1) * P]
            ins = three(m.ps[:, 6, t * E:(t + 1) * E], (a, a, b), (m.w1[:, gate], m.w2[:, gate], m.w3[:, gate]))
        ins.then_inc(q.logits, 1)

    def hidden(sb, u):
        pe.wait_ge(q.act, sb * U + u + 1)
        g, half = u // 2, u % 2
        a, b = (x[:, half * HALF:(half + 1) * HALF] for x in (m.xa, m.xb))
        outs = ((w["up"], u % 4),) if not f["gated"] else ((w["up"], 2 * (u % 2)), (w["up2"], 2 * (u % 2) + 1))
        for at, bank in outs:
            cols = slice(at + g * P, at + (g + 1) * P)
            ins = three(m.ps[:, bank, :], (m.w1[:, cols], m.w2[:, cols], m.w3[:, cols]), (a, a, b))
        ins.then_inc(q.hidden, 1)

    def down(sb, e):
        g, i = e // per, e % per
        pe.wait_ge(q.act, free + sb * U + 2 * g + 2)
        pe.wait_ge(q.weighed, sb * E + e + 1)
        bank = 4 + e % 2
        if f["b2"]:
            pe.matmul(m.ps[:, bank, :], m.ones3[:, :], bcast(m.b2p[:, E2[l] + e, :].unsqueeze(1), [3, ST, C]),
                      start=True, stop=True)
        rows = slice(i * f["H"], (i + 1) * f["H"])
        for t in range(ST):
            ins = pe.matmul(m.ps[:, bank, t * C:(t + 1) * C], m.hid[rows, g % 2, t * P:(t + 1) * P],
                            m.down[l][rows, g, :], start=not f["b2"], stop=True, skip_group_check=f["b2"])
        ins.then_inc(q.down, 1)

    def turn(sb, ahead):
        for u in range(U):
            hidden(sb, u)
            g = u // 2
            if u % 2 and g > 0:
                for i in range(per):
                    down(sb, (g - 1) * per + i)
            if u % 2 and g == ahead_at - 1 and ahead and G > 4:
                transposes(sb + 1)
        if ahead and G <= 4:
            transposes(sb + 1)
        for i in range(per):
            down(sb, (G - 1) * per + i)
        if ahead:
            logits(sb + 1)

    transposes(0)
    logits(0)
    with pe.Fori(0, SUPERS - 1) as sb:
        turn(sb, True)
    turn(SUPERS - 1, False)


def ffn_act(act, nc, m, s, l):
    f, q = FFN[l], s.ffn[l]
    E, G, per, U = ffn_counts(l)
    flat = m.parts

    def part(sb, k, first):
        if k == 0:
            act.wait_ge(q.xn, sb + 1)
            if not first:
                act.wait_ge(q.transposed, sb)
            act.activation(m.parts[:, :, 1, :], m.xn[:, :, :], ACT.Copy).then_inc(q.part1, 1)
        else:
            act.wait_ge(q.rest, sb + 1)
            act.activation(m.parts[:, :, 0, :], m.xc[:, :, :], ACT.Copy).then_inc(q.part2, 1)

    def evacuate(sb, first):
        act.wait_ge(q.transposed, sb + 1)
        if not first:
            act.wait_ge(q.hidden, sb * U)
        act.activation(m.xb[:, :], m.ps[:, 7, :].bitcast(BF16), ACT.Copy).then_inc(q.xb, 1)

    def exps(sb):
        act.wait_ge(q.below_max, sb + 1)
        act.activation(m.ex[:, 0:ST, 0:E + 1], m.below[:, 0:ST, 0:E + 1], ACT.Exp).then_inc(q.exps, 1)

    def unit(sb, u):
        g, half = u // 2, u % 2
        act.wait_ge(q.hidden, sb * U + u + 1)
        if half == 0:
            act.wait_ge(q.down, sb * E + (g + 1) * per)
        out = m.hid[:, g % 2, half * HALF:(half + 1) * HALF]
        if f["gated"]:
            act.wait_ge(q.act, sb * U + u + 1)
            act.activation(m.silu[:, half, :], m.ps[:, 2 * half, :], ACT.Silu).then_inc(q.silu, 1)
        else:
            bias = m.b1t[:, E1[l] + g:E1[l] + g + 1]
            act.activation(out, m.ps[:, u % 4, :], ACT.Gelu, bias=bias).then_inc(q.act, 1)

    def turn(sb, ahead):
        for g in range(G):
            unit(sb, 2 * g)
            unit(sb, 2 * g + 1)
            if g == 0:
                exps(sb)
            if ahead and g == min(2, G - 3):
                part(sb + 1, 0, False)
            if ahead and g == min(3, G - 2):
                part(sb + 1, 1, False)
        if ahead:
            evacuate(sb + 1, False)

    part(0, 0, True)
    part(0, 1, True)
    evacuate(0, True)
    with act.Fori(0, SUPERS - 1) as sb:
        turn(sb, True)
    turn(SUPERS - 1, False)


def ffn_dve(dve, nc, m, s, l):
    f, q = FFN[l], s.ffn[l]
    E, G, per, U = ffn_counts(l)
    o = Order(dve, q.order)
    dve.sem_inc(q.weighed, 2)
    dve.sem_inc(q.logits_read, 1)

    def stats(sb):
        ln_stats(dve, o, m, m.X[:, bass.ds(sb * ST, ST), :], ST, q.mv)

    def norm(sb):
        dve.wait_ge(q.rstd, sb + 1)
        x = m.X[:, bass.ds(sb * ST, ST), :]
        ln_apply(dve, o, m, x, ST, q.xn)
        if f["keep"]:
            dve.wait_ge(q.xn, sb + 1)
            o.then(dve.tensor_tensor(x, x, m.xn[:, :, :], ALU.add))

    def rest(sb):
        dve.wait_ge(q.part1, sb + 1)
        dve.tensor_tensor(m.xc[:, :, :], m.xn[:, :, :], m.parts[:, :, 1, :], ALU.subtract).then_inc(q.rest, 1)

    def third(sb):
        dve.wait_ge(q.part2, sb + 1)
        dve.tensor_tensor(m.parts[:, :, 2, :], m.xc[:, :, :], m.parts[:, :, 0, :], ALU.subtract)\
            .then_inc(q.parts, 1)

    def evacuate(sb, first):
        dve.wait_ge(q.transposed, sb + 1)
        if not first:
            dve.wait_ge(q.hidden, sb * U)
        dve.tensor_copy(m.xa[:, :], m.ps[:, 6, :].bitcast(BF16)).then_inc(q.xa, 1)

    def router(sb):
        dve.wait_ge(q.logits, sb + 1)
        lg = m.lg[:, :, 0:E]
        raw = m.ps[:, 6, 0:ST * E].rearrange("p (t e) -> p t e", e=E)
        if f["gate_b"]:
            ins = dve.tensor_tensor(lg, raw, bcast(m.gate_b[l][:, :].unsqueeze(1), [P, ST, E]), ALU.add)
        else:
            ins = dve.tensor_copy(lg, raw)
        ins.then_inc(q.logits_read, 1)
        wait_apart(dve, m, q.logits_read, sb + 2)
        for t in range(ST):
            ins = dve.max(m.top[:, t, :], m.lg[:, t, 0:E])
        o.then(ins)
        dve.tensor_tensor(m.below[:, :, 0:E], lg, bcast(m.top[:, :, 0:1], [P, ST, E]), ALU.subtract)
        dve.tensor_tensor(m.below[:, :, E], m.top[:, :, 1], m.top[:, :, 0], ALU.subtract).then_inc(q.below_max, 1)
        for t in range(ST):
            ins = dve.max_index(m.topi[:, t, :], m.top[:, t, :], m.lg[:, t, 0:E])
        o.then(ins)
        o.then(dve.tensor_copy(m.topf[:, :, :], m.topi[:, :, 0:2]))
        shape = [P, ST, E]
        for k in range(2):
            ins = dve.tensor_tensor(m.hit[:, k, :, 0:E], bcast(m.iota[:, 0:E].unsqueeze(1), shape),
                                    bcast(m.topf[:, :, k:k + 1], shape), ALU.is_equal)
        o.step(ins)
        dve.wait_ge(q.exps, sb + 1)
        o.then(dve.tensor_reduce(m.sums[:, :], m.ex[:, :, 0:E], AX, ALU.add))
        o.then(dve.reciprocal(m.prob[:, 0, :], m.sums[:, :]))
        o.then(dve.tensor_tensor(m.prob[:, 1, :], m.ex[:, :, E], m.prob[:, 0, :], ALU.mult))
        if f["renorm"]:
            o.then(dve.tensor_tensor(m.sums[:, :], m.prob[:, 0, :], m.prob[:, 1, :], ALU.add))
            if f["floor"] is not None:
                o.then(dve.tensor_scalar(m.sums[:, :], m.sums[:, :], f["floor"], None, ALU.max))
            o.then(dve.reciprocal(m.rsum[:, :], m.sums[:, :]))
            o.then(dve.tensor_tensor(m.prob[:, :, :], m.prob[:, :, :], bcast(m.rsum[:, :].unsqueeze(1), [P, 2, ST]),
                                     ALU.mult))
        for k in range(2):
            ins = dve.tensor_tensor(m.hit[:, k, :, 0:E], m.hit[:, k, :, 0:E],
                                    bcast(m.prob[:, k, :].unsqueeze(2), shape), ALU.mult)
        o.then(ins)
        o.then(dve.tensor_tensor(m.cw[:, :, 0:E], m.hit[:, 0, :, 0:E], m.hit[:, 1, :, 0:E], ALU.add))

    def gate(sb, u):
        g, half = u // 2, u % 2
        dve.wait_ge(q.silu, sb * U + u + 1)
        if half == 0:
            dve.wait_ge(q.down, sb * E + (g + 1) * per)
        dve.tensor_tensor(m.hid[:, g % 2, half * HALF:(half + 1) * HALF], m.silu[:, half, :],
                          m.ps[:, 2 * half + 1, :], ALU.mult).then_inc(q.act, 1)

    def weigh(sb, e):
        dve.wait_ge(q.down, 2 * per + sb * E + e + 1)
        dve.wait_ge(q.added, sb * E + e + 1)
        dve.tensor_tensor(m.prod[:, e % 2, :, :], m.ps[:, 4 + e % 2, :].rearrange("p (t c) -> p t c", c=C),
                          bcast(m.cw[:, :, e:e + 1], [P, ST, C]), ALU.mult).then_inc(q.weighed, 1)

    def turn(sb, ahead):
        if not f["gated"]:
            router(sb)
        pieces = [lambda: stats(sb + 1), lambda: norm(sb + 1), lambda: rest(sb + 1), lambda: third(sb + 1)]
        for g in range(G):
            if f["gated"]:
                gate(sb, 2 * g)
                gate(sb, 2 * g + 1)
                if g == 0:
                    router(sb)
            if g > 0:
                for i in range(per):
                    weigh(sb, (g - 1) * per + i)
            if ahead:
                if G > 4:
                    if g < 4:
                        pieces[g]()
                elif g < 2:
                    pieces[2 * g]()
                    pieces[2 * g + 1]()
        for i in range(per):
            weigh(sb, (G - 1) * per + i)
        if ahead:
            evacuate(sb + 1, False)

    stats(0)
    norm(0)
    rest(0)
    third(0)
    evacuate(0, True)
    with o.turns(SUPERS - 1, FFN_STEPS[l]) as sb:
        turn(sb, True)
    turn(SUPERS - 1, False)


FFN_STEPS = [11, 16, 14, 11]


def ffn_pool(pool, nc, m, s, l):
    f, q = FFN[l], s.ffn[l]
    E, G, per, U = ffn_counts(l)
    o = Order(pool, q.pool_order)
    free = 2 if f["gated"] else 4
    pool.sem_inc(q.added, 2)
    pool.sem_inc(q.act, free)
    pool.sem_inc(q.down, 2 * per)

    def add(sb, e):
        x = m.X[:, bass.ds(sb * ST, ST), :]
        pool.wait_ge(q.weighed, 2 + sb * E + e + 1)
        wait_apart(pool, m, q.added, 2 + sb * E + e)
        pool.tensor_tensor(x, x, m.prod[:, e % 2, :, :], ALU.add).then_inc(q.added, 1)

    def rstd(sb):
        wait_apart(pool, m, q.mv, sb + 1)
        ln_rstd(pool, o, m, ST, 1e-5, q.rstd)

    rstd(0)
    with o.turns(SUPERS - 1, 1) as sb:
        rstd(sb + 1)
        for e in range(E):
            add(sb, e)
    for e in range(E):
        add(SUPERS - 1, e)



BANKS3 = 4 * 160 + 256 + 3 * 128
Q_PARTS = (0, 0, 0, 1, 1, 2)
K_PARTS = (0, 1, 2, 0, 1, 0)
SPLIT_ROWS = 6 * HD
BLOCKS = 5
LOW = 3


def row_parity(ap):
    return ap.rearrange("p (im a py x) -> p im py a x", im=2, py=2, x=SIDE)


def by_parity(ap):
    return ap.rearrange("p (im py a x) -> p im py a x", im=2, py=2, x=SIDE)


HEAD = [(0, 0, 0, 0, "near"), (0, 1, 0, 160, "near"), (0, 2, 0, 320, "near"), (1, 0, 1, 0, "near"),
        (1, 1, 1, 160, "all"), (1, 2, 2, 0, "rows"), (1, 3, 2, 128, "rows"), (1, 4, 2, 256, "rows")]
BANK_COLS = (480, 416, 384)
BANK_AT = (0, 480, 896)


def make_sel(pool, m, s):
    o = m.pool_order
    o.then(pool.memset(m.sel, 0.0))
    for side, parts in enumerate((Q_PARTS, K_PARTS)):
        for k, part in enumerate(parts):
            for half, first, n in ((0, 0, LOW), (1, LOW, HEADS - LOW)):
                src = m.ident[:, side * C + first * HD:side * C + (first + n) * HD]
                ins = pool.tensor_copy(m.sel[:, side, part, 0:n, half * C + k * HD:half * C + (k + 1) * HD],
                                       src.rearrange("p (n d) -> p n d", d=HD))
    o.step(ins)


def c1_pe(pe, nc, m, s):
    pe.sem_inc(s.c1_o, 2)

    def tokens(p):
        pe.wait_ge(s.c1_xn, p + 1)
        wait_apart(pe, m, s.c1_max, 4 * p + 1)
        for t in range(PT):
            ins = pe.transpose(m.ps[0:C, 0, t * P:(t + 1) * P], m.xn[:, t, :], m.ident[:])
        ins.then_inc(s.c1_nt, 1)

    def queries_keys(p):
        pe.wait_ge(s.c1_xf, p + 1)
        pe.matmul(m.ps[:, 1, :], m.wqk[:, :], m.xf[:, :], start=True, stop=True).then_inc(s.c1_qk, 1)

    def values_of_tokens(p):
        for t in range(PT):
            cols = slice(t * P, (t + 1) * P)
            for x, a, b in ((m.xf, 0, 40), (m.xfp, 40, 64)):
                ins = pe.matmul(m.ps[:, 0, t * C + a:t * C + b], x[:, cols], m.wv[:, a:b], start=True, stop=True)
        ins.then_inc(s.c1_v, 1)

    def spread(p):
        pe.wait_ge(s.c1_part3, p + 1)
        for b in range(BLOCKS):
            for side, (read, done) in enumerate(((s.c1_qs, s.c1_selq), (s.c1_ks, s.c1_selk))):
                pe.wait_ge(read, BLOCKS * p + b + 1)
                out = m.ps[:, 1 + side, :]
                if b < 2:
                    for k in range(3):
                        ins = pe.matmul(out, m.sel[:, side, k, b, :], m.qkp[:, k, :], start=(k == 0), stop=(k == 2))
                    ins.then_inc(done, 1)
                    continue
                if b == 2:
                    for k in range(3):
                        pe.matmul(out[0:C, :], m.sel[:, side, k, b, 0:C], m.qkp[:, k, :],
                                  start=(k == 0), stop=(k == 2))
                for im in range(2):
                    for k in range(3):
                        ins = pe.matmul(out[C:P, im * PLACES:(im + 1) * PLACES], m.sel[:, side, k, b, C:P],
                                        row_parity(m.qkp[:, k, :])[:, im], start=(k == 0), stop=(k == 2))
                ins.then_inc(done, 1)

    def logits(first_bank, stationary, moving, rows, i):
        for b, (n, at) in enumerate(zip(BANK_COLS, (None, MASK_AT["near"], MASK_AT["rows"]))):
            mask = m.mask[:, i * MASK_TILE:(i + 1) * MASK_TILE]
            if b == 1:
                rhs = mask[:, 0:416]
            else:
                kind, w = (("near", 160), None, ("rows", 128))[b]
                rhs = bcast(mask[:, MASK_AT[kind]:MASK_AT[kind] + w].unsqueeze(1), [P, 3, w])
            pe.matmul(m.ps[:, first_bank + b, 0:n], m.identb[:, :], rhs, start=True, stop=True)
        for half, block, b, col, kind in HEAD:
            r = slice(C * half, C * half + rows)
            w = WIDTH[kind]
            lo = dict(near=i * (PLACES - 160), rows=i * P, all=0)[kind]
            ins = pe.matmul(m.ps[:, first_bank + b, col:col + w],
                            stationary(r, block, slice(i * P, (i + 1) * P)), moving(r, block, slice(lo, lo + w)),
                            start=False, stop=True, skip_group_check=True)
        return ins

    def of_image(x, im):
        return lambda r, b, c: x[r, b, im * PLACES + c.start:im * PLACES + c.stop]

    def by_query(p, n):
        if n == 0:
            pe.wait_ge(s.c1_v_read, p + 1)
            pe.wait_ge(s.c1_qs, BLOCKS * p + BLOCKS + 1)
            pe.wait_ge(s.c1_ks, BLOCKS * p + BLOCKS + 1)
        pe.wait_ge(s.c1_max, 4 * p + n + 1)
        logits(0, of_image(m.qs, n // 2), of_image(m.ks, n // 2), SPLIT_ROWS, n % 2).then_inc(s.c1_s, 1)

    def max_rows(p, im):
        pe.wait_ge(s.c1_m, 2 * p + im + 1)
        if im == 0:
            pe.wait_ge(s.c1_ot_read, p + 1)
            pe.wait_ge(s.c1_added, p + 1)
        else:
            pe.wait_ge(s.c1_q2, 2 * p + 1)
        for i in range(2):
            for b in range(BLOCKS):
                ins = pe.transpose(m.ps[:, 6 + i, :].bitcast(BF16)[:, b * P:(b + 1) * P],
                                   m.maxes[:, 2 * im + i, b, :], m.identb[:])
        ins.then_inc(s.c1_mt, 1)

    def by_key(p, n):
        im = n // 2
        pe.wait_ge(s.c1_q2, 2 * p + im + 1)
        pe.wait_ge(s.c1_p, 4 * p + n + 1)
        logits(3, of_image(m.ks, im), lambda r, b, c: m.q2[r, b, c], SPLIT_ROWS + 3, n % 2).then_inc(s.c1_st, 1)

    def weigh(p, im):
        pe.wait_ge(s.c1_p, 4 * p + 2 * im + 3)
        pe.wait_ge(s.c1_on, 2 * p + im + 1)
        if im == 0:
            pe.wait_ge(s.c1_vals, p + 2)
            pe.wait_ge(s.c1_q2, 2 * p + 2)
        for i in range(2):
            for h, (_, _, b, col, kind) in enumerate(HEAD):
                col += BANK_AT[b]
                out = m.ps[:, 7, (i * HEADS + h) * 9:(i * HEADS + h + 1) * 9]
                v = lambda k: m.vals[:, 2 * im + k, h, :]
                pt = lambda k, a, b_: m.pt[:, 2 * im + k, col + a:col + b_]
                if kind == "near":
                    own = pt(i, 0, 128) if i == 0 else pt(i, 32, 160)
                    pe.matmul(out, own, v(i), start=True, stop=True)
                    if i == 0:
                        ins = pe.matmul(out[96:128, :], pt(1, 0, 32), v(1), start=False, stop=True, skip_group_check=True)
                    else:
                        ins = pe.matmul(out[0:32, :], pt(0, 128, 160), v(0), start=False, stop=True, skip_group_check=True)
                elif kind == "rows":
                    ins = pe.matmul(out, pt(i, 0, 128), v(i), start=True, stop=True)
                else:
                    for k in range(2):
                        ins = pe.matmul(out, pt(k, i * P, (i + 1) * P), v(k), start=(k == 0), stop=(k == 1))
        ins.then_inc(s.c1_o, 1)

    def outputs_t(p):
        wait_apart(pe, m, s.c1_on, 2 * p + 3)
        for t in range(PT):
            ins = pe.transpose(m.ps[0:C, 6, t * P:(t + 1) * P], m.att[:, t, :], m.ident[:])
        ins.then_inc(s.c1_ot, 1)

    def project(p):
        pe.wait_ge(s.c1_ot_read, p + 2)
        for t in range(PT):
            out = m.ps[:, 7, t * C:(t + 1) * C]
            pe.matmul(out, m.ot1[:, t * P:(t + 1) * P], m.wpn[:, :], start=True, stop=False)
            ins = pe.matmul(out, m.ot2[:, t * P:(t + 1) * P], m.wpp[:, :], start=False, stop=True)
        ins.then_inc(s.c1_y, 1)

    def turn(p, behind, ahead):
        by_query(p, 0)
        if behind:
            weigh(p - 1, 1)
        by_query(p, 1)
        if behind:
            outputs_t(p - 1)
        by_query(p, 2)
        if behind:
            project(p - 1)
        max_rows(p, 0)
        by_key(p, 0)
        by_query(p, 3)
        if ahead:
            tokens(p + 1)
        by_key(p, 1)
        max_rows(p, 1)
        if ahead:
            queries_keys(p + 1)
        weigh(p, 0)
        by_key(p, 2)
        if ahead:
            values_of_tokens(p + 1)
        by_key(p, 3)
        if ahead:
            spread(p + 1)

    tokens(0)
    queries_keys(0)
    values_of_tokens(0)
    spread(0)
    turn(0, False, True)
    with pe.Fori(1, PAIRS - 1) as p:
        turn(p, True, True)
    turn(PAIRS - 1, True, False)
    weigh(PAIRS - 1, 1)
    outputs_t(PAIRS - 1)
    project(PAIRS - 1)


def c1_act(act, nc, m, s):
    for sem in (s.c1_p, s.c1_ot_read, s.c1_ks):
        act.sem_inc(sem, 1)

    def exps(p, n):
        act.wait_ge(s.c1_st, 4 * p + n + 1)
        if n % 2 == 0:
            act.wait_ge(s.c1_o, 2 * p + 1 + n // 2)
        for b, (k, at) in enumerate(zip(BANK_COLS, BANK_AT)):
            ins = act.activation(m.pt[:, n, at:at + k], m.ps[:, 3 + b, 0:k], ACT.Exp)
        ins.then_inc(s.c1_p, 1)

    def emax(p, im):
        act.wait_ge(s.c1_m, 2 * p + im + 1)
        tiles = slice(2 * im, 2 * im + 2)
        act.activation(m.emax[:, tiles, :], m.maxp[:, tiles, :],
                       ACT.Exp, scale=-1.0).then_inc(s.c1_em, 1)

    def tokens(p):
        act.wait_ge(s.c1_nt, p + 1)
        act.activation(m.xf[0:C, :], m.ps[0:C, 0, :], ACT.Copy)
        for py in range(2):
            ins = act.activation(by_parity(m.xfp[0:C, :])[:, :, py], row_parity(m.ps[0:C, 0, :])[:, :, py], ACT.Copy)
        ins.then_inc(s.c1_xf, 1)

    def part1(p):
        act.wait_ge(s.c1_qk, p + 1)
        act.activation(m.qkp[:, 0, :], m.ps[:, 1, :], ACT.Copy).then_inc(s.c1_part1, 1)

    def part2(p):
        act.wait_ge(s.c1_rest, p + 1)
        act.activation(m.qkp[:, 1, :], m.qk_rest, ACT.Copy).then_inc(s.c1_part2, 1)

    def keys(p):
        for b in range(BLOCKS):
            act.wait_ge(s.c1_selk, BLOCKS * p + b + 1)
            r = slice(0 if b < LOW else C, P)
            act.activation(m.ks[r, b, :], m.ps[r, 2, :], ACT.Identity, bias=m.minus_rows[r, :]).then_inc(s.c1_ks, 1)

    def vals(p):
        act.wait_ge(s.c1_v, p + 1)
        act.wait_ge(s.c1_vals, p + 1)
        act.activation(m.vals_next[:, :, :], m.ps[:, 0, 0:PT * C].rearrange("p (t c) -> p t c", t=PT),
                       ACT.Copy).then_inc(s.c1_v_read, 1)

    def outputs(p):
        act.wait_ge(s.c1_ot, p + 1)
        for py in range(2):
            act.activation(row_parity(m.ot2[:, :])[:, :, py], by_parity(m.ps[0:C, 6, :])[:, :, py], ACT.Copy)
        act.activation(m.ot1[0:C, :], m.ps[0:C, 6, :], ACT.Copy).then_inc(s.c1_ot_read, 1)

    def turn(p, behind, ahead):
        if behind:
            outputs(p - 1)
        emax(p, 0)
        exps(p, 0)
        if ahead:
            tokens(p + 1)
        exps(p, 1)
        emax(p, 1)
        if ahead:
            part1(p + 1)
            part2(p + 1)
        exps(p, 2)
        if ahead:
            vals(p + 1)
        exps(p, 3)
        if ahead:
            keys(p + 1)

    tokens(0)
    part1(0)
    part2(0)
    vals(0)
    keys(0)
    turn(0, False, True)
    with act.Fori(1, PAIRS - 1) as p:
        turn(p, True, True)
    turn(PAIRS - 1, True, False)
    outputs(PAIRS - 1)


def c1_dve(dve, nc, m, s):
    o = m.dve_order
    for sem in (s.c1_max, s.c1_on, s.c1_added, s.c1_qs):
        dve.sem_inc(sem, 1)

    def stats(p):
        ln_stats(dve, o, m, m.X[:, bass.ds(p * PT, PT), :], PT, s.c1_mv)

    def norm(p, first=False):
        dve.wait_ge(s.c1_rstd, p + 1)
        if not first:
            dve.wait_ge(s.c1_nt, p)
        ln_apply(dve, o, m, m.X[:, bass.ds(p * PT, PT), :], PT, s.c1_xn)

    def rest(p):
        dve.wait_ge(s.c1_part1, p + 1)
        dve.tensor_tensor(m.qk_rest, m.ps[:, 1, :], m.qkp[:, 0, :], ALU.subtract).then_inc(s.c1_rest, 1)
        dve.wait_ge(s.c1_part2, p + 1)
        dve.tensor_tensor(m.qkp[:, 2, :], m.qk_rest, m.qkp[:, 1, :], ALU.subtract).then_inc(s.c1_part3, 1)

    def queries(p):
        for b in range(BLOCKS):
            dve.wait_ge(s.c1_selq, BLOCKS * p + b + 1)
            r = slice(0 if b < LOW else C, P)
            dve.tensor_copy(m.qs[r, b, :], m.ps[r, 1, :]).then_inc(s.c1_qs, 1)

    def maxima(p, n):
        dve.wait_ge(s.c1_s, 4 * p + n + 1)
        r = m.maxr[:, n, :]
        dve.tensor_reduce(r[:, 0:3], m.ps[:, 0, 0:480].rearrange("p (h k) -> p h k", h=3), AX, ALU.max)
        dve.tensor_reduce(r[:, 3:4], m.ps[:, 1, 0:160], AX, ALU.max)
        dve.tensor_reduce(r[:, 4:5], m.ps[:, 1, 160:416], AX, ALU.max)
        dve.tensor_reduce(r[:, 5:8], m.ps[:, 2, 0:384].rearrange("p (h k) -> p h k", h=3), AX, ALU.max)\
            .then_inc(s.c1_max, 1)

    def with_padding(p, im):
        t = slice(2 * im, 2 * im + 2)
        dve.wait_ge(s.c1_max, 4 * p + 2 * im + 3)
        pad = m.padmax[:, :].rearrange("p (t h) -> p t h", t=2)
        o.then(dve.tensor_tensor(m.maxp[:, t, :], m.maxr[:, t, :], pad, ALU.max))
        o.then(dve.tensor_copy(m.maxparts[:, :, :, 0], m.maxp[:, t, :]))
        o.then(dve.tensor_tensor(m.maxrest[:, :, :], m.maxp[:, t, :], m.maxparts[:, :, :, 0], ALU.subtract))
        o.then(dve.tensor_copy(m.maxparts[:, :, :, 1], m.maxrest[:, :, :]))
        o.then(dve.tensor_tensor(m.maxparts[:, :, :, 2], m.maxrest[:, :, :], m.maxparts[:, :, :, 1], ALU.subtract))
        for half, first, n in ((0, 0, LOW), (1, LOW, HEADS - LOW)):
            at = half * C + SPLIT_ROWS
            ins = dve.tensor_copy(m.maxes[:, t, 0:n, at:at + 3], m.maxparts[:, :, first:first + n, :])
        ins.then_inc(s.c1_m, 1)

    def q2(p, im):
        dve.wait_ge(s.c1_mt, 2 * p + im + 1)
        if im == 1:
            dve.wait_ge(s.c1_st, 4 * p + 2)
        for i in range(2):
            at = im * PLACES + i * P
            mt = m.ps[:, 6 + i, :].bitcast(BF16)[:, 0:BLOCKS * P].rearrange("p (b q) -> p b q", b=BLOCKS)
            ins = dve.tensor_tensor(m.q2[:, :, i * P:(i + 1) * P], m.qs[:, :, at:at + P], mt, ALU.add)
        ins.then_inc(s.c1_q2, 1)

    def normalise(p, im):
        t = slice(2 * im, 2 * im + 2)
        dve.wait_ge(s.c1_em, 2 * p + im + 1)
        o.then(dve.tensor_tensor(m.den[:, t, :], m.emax[:, t, :], m.padn[:, :].rearrange("p (t h) -> p t h", t=2),
                                 ALU.mult))
        dve.wait_ge(s.c1_o, 2 * p + im + 3)
        out = m.ps[:, 7, 0:2 * HEADS * 9].rearrange("p (t h d) -> p t h d", t=2, d=9)
        o.then(dve.tensor_tensor(m.den[:, t, :], m.den[:, t, :], out[:, :, :, HD], ALU.add))
        o.then(dve.reciprocal(m.rden[:, t, :], m.den[:, t, :]))
        dve.tensor_tensor(m.att[:, t, :].rearrange("p t (h d) -> p t h d", d=HD), out[:, :, :, 0:HD],
                          bcast(m.rden[:, t, :].unsqueeze(3), [P, 2, HEADS, HD]), ALU.mult).then_inc(s.c1_on, 1)

    def add(p):
        dve.wait_ge(s.c1_y, p + 1)
        x = m.X[:, bass.ds(p * PT, PT), :]
        dve.tensor_tensor(x, x, m.ps[:, 7, 0:PT * C].rearrange("p (t c) -> p t c", c=C), ALU.add)\
            .then_inc(s.c1_added, 1)

    def turn(p, behind, ahead):
        maxima(p, 0)
        if ahead:
            stats(p + 1)
        if behind:
            normalise(p - 1, 1)
        maxima(p, 1)
        with_padding(p, 0)
        if ahead:
            norm(p + 1)
        maxima(p, 2)
        if behind:
            add(p - 1)
        q2(p, 0)
        maxima(p, 3)
        with_padding(p, 1)
        q2(p, 1)
        if ahead:
            rest(p + 1)
        normalise(p, 0)
        if ahead:
            queries(p + 1)

    stats(0)
    norm(0, True)
    rest(0)
    queries(0)
    turn(0, False, True)
    with o.turns(PAIRS - 2, 18) as i:
        turn(i + 1, True, True)
    turn(PAIRS - 1, True, False)
    normalise(PAIRS - 1, 1)
    add(PAIRS - 1)


def clear(pool, q):
    for sem in q:
        pool.sem_clear(sem)


def c1_pool(pool, nc, m, s):
    clear(pool, s.ffn[0])
    o = m.pool_order
    pool.sem_inc(s.c1_vals, 1)

    def rstd(p):
        wait_apart(pool, m, s.c1_mv, p + 1)
        ln_rstd(pool, o, m, PT, 1e-6, s.c1_rstd)

    def vals(p):
        pool.wait_ge(s.c1_v_read, p + 1)
        wait_apart(pool, m, s.c1_o, 2 * p + 2)
        pool.tensor_copy(m.vals[:, :, :, 0:HD], m.vals_next[:, :, :].rearrange("p t (h d) -> p t h d", d=HD))\
            .then_inc(s.c1_vals, 1)

    rstd(0)
    vals(0)
    with o.turns(PAIRS - 1, 1) as p:
        rstd(p + 1)
        vals(p + 1)



def c2_pe(pe, nc, m, s):
    pe.sem_inc(s.c2_y, 1)

    def tokens(p):
        pe.wait_ge(s.c2_xn, p + 1)
        wait_apart(pe, m, s.c2_xf, p + 1)
        for t in range(PT):
            ins = pe.transpose(m.ps[0:C, 0, t * P:(t + 1) * P], m.xn[:, t, :], m.ident[:])
        ins.then_inc(s.c2_nt, 1)

    def inverse_norms(p):
        pe.wait_ge(s.c2_diag, p + 1)
        pe.wait_ge(s.c2_inv, 2 * p + 1)
        pe.matmul(m.ps[:, 2, :], m.one[:, :], m.diag.rearrange("p t q -> p (t q)"), start=True, stop=True)\
            .then_inc(s.c2_nq, 1)

    def turn(p, ahead):
        pe.wait_ge(s.c2_xf, p + 2)
        pe.wait_ge(s.c2_relu, 2 * p + 1)
        for im in range(2):
            for i in range(2):
                at = im * PLACES
                ins = pe.matmul(m.ps[:, 3 + im, i * PLACES:(i + 1) * PLACES],
                                m.xf[0:C, at + i * P:at + (i + 1) * P], m.xf[0:C, at:at + PLACES],
                                start=True, stop=True)
            ins.then_inc(s.c2_dots, 1)
        pe.wait_ge(s.c2_tx, p + 1)
        for t in range(PT):
            ins = pe.matmul(m.ps[:, 1, t * C:(t + 1) * C], m.xf[:, t * P:(t + 1) * P], m.w_l2[:, :],
                            start=True, stop=True)
        ins.then_inc(s.c2_lin, 1)
        if ahead:
            tokens(p + 1)
            inverse_norms(p + 1)
        pe.wait_ge(s.c2_tx, p + 2)
        pe.wait_ge(s.c2_added, p + 1)
        for im in range(2):
            pe.wait_ge(s.c2_sim, 2 * p + im + 1)
            for i in range(2):
                for k in range(2):
                    ins = pe.matmul(m.ps[:, 5, (2 * im + i) * C:(2 * im + i + 1) * C],
                                    m.sim[:, im, k, i * P:(i + 1) * P], m.tx[:, 2 * im + k, :],
                                    start=(k == 0), stop=(k == 1))
        ins.then_inc(s.c2_y, 1)

    tokens(0)
    inverse_norms(0)
    with pe.Fori(0, PAIRS - 1) as p:
        turn(p, True)
    turn(PAIRS - 1, False)


def c2_act(act, nc, m, s):
    for sem in (s.c2_relu, s.c2_tx, s.c2_xf):
        act.sem_inc(sem, 1)

    def features(p):
        act.wait_ge(s.c2_nt, p + 1)
        act.activation(m.xf[0:C, :], m.ps[0:C, 0, :], ACT.Copy).then_inc(s.c2_xf, 1)

    def turn(p, ahead):
        act.wait_ge(s.c2_y, p + 1)
        for im in range(2):
            act.wait_ge(s.c2_dots, 2 * p + im + 1)
            act.activation(m.relu[:, im, :], m.ps[:, 3 + im, :], ACT.Relu).then_inc(s.c2_relu, 1)
        act.wait_ge(s.c2_lin, p + 1)
        act.activation(m.tx[:, :, :], m.ps[:, 1, 0:PT * C].rearrange("p (t c) -> p t c", c=C), ACT.Copy)\
            .then_inc(s.c2_tx, 1)
        for im in range(2):
            act.wait_ge(s.c2_relu, 2 * p + im + 2)
            act.activation(m.relu2[:, im, :], m.relu[:, im, :], ACT.Square).then_inc(s.c2_sq, 1)
        if ahead:
            features(p + 1)

    features(0)
    with act.Fori(0, PAIRS - 1) as p:
        turn(p, True)
    turn(PAIRS - 1, False)


def c2_dve(dve, nc, m, s):
    for sem in (s.c2_inv, s.c2_added):
        dve.sem_inc(sem, 1)
    o = m.dve_order

    def stats(p):
        ln_stats(dve, o, m, m.X[:, bass.ds(p * PT, PT), :], PT, s.c2_mv)

    def norm(p, first=False):
        dve.wait_ge(s.c2_rstd, p + 1)
        if not first:
            dve.wait_ge(s.c2_nt, p)
        ln_apply(dve, o, m, m.X[:, bass.ds(p * PT, PT), :], PT, s.c2_xn)
        dve.wait_ge(s.c2_xn, p + 1)
        o.then(dve.tensor_tensor(m.xc[:, 0:PT, :], m.xn[:, 0:PT, :], m.xn[:, 0:PT, :], ALU.mult))
        o.then(dve.tensor_reduce(m.n2[:, 0:PT], m.xc[:, 0:PT, :], AX, ALU.add))
        o.then(dve.tensor_scalar(m.n2[:, 0:PT], m.n2[:, 0:PT], 1e-30, None, ALU.max))
        if not first:
            dve.wait_ge(s.c2_inv, 2 * p + 1)
            dve.wait_ge(s.c2_nq, p)
        o.then(dve.reciprocal(m.rn2[:, :], m.n2[:, 0:PT]))
        dve.tensor_tensor(m.diag, bcast(m.ident[:, :].unsqueeze(1), [P, PT, P]),
                          bcast(m.rn2[:, :].unsqueeze(2), [P, PT, P]), ALU.mult).then_inc(s.c2_diag, 1)

    def inverses(p):
        dve.wait_ge(s.c2_nq, p + 1)
        for im in range(2):
            for i in range(2):
                ins = dve.tensor_scalar(m.inv[:, im, i * PLACES:(i + 1) * PLACES],
                                        m.ps[:, 2, im * PLACES:(im + 1) * PLACES],
                                        m.rn2[:, 2 * im + i:2 * im + i + 1], 1e16, ALU.mult, ALU.min)
            ins.then_inc(s.c2_inv, 1)

    def turn(p, ahead):
        if ahead:
            stats(p + 1)
        inverses(p)
        if ahead:
            norm(p + 1)
        for im in range(2):
            dve.wait_ge(s.c2_inv, 2 * p + im + 2)
            dve.wait_ge(s.c2_sq, 2 * p + im + 1)
            dve.tensor_tensor(m.sim[:, im, :, :].rearrange("p k q -> p (k q)"), m.relu2[:, im, :], m.inv[:, im, :],
                              ALU.mult).then_inc(s.c2_sim, 1)
        dve.wait_ge(s.c2_y, p + 2)
        x = m.X[:, bass.ds(p * PT, PT), :]
        dve.tensor_tensor(x, x, m.ps[:, 5, 0:PT * C].rearrange("p (t c) -> p t c", c=C), ALU.add)\
            .then_inc(s.c2_added, 1)

    stats(0)
    norm(0, True)
    with o.turns(PAIRS - 1, 6) as p:
        turn(p, True)
    turn(PAIRS - 1, False)


def c2_pool(pool, nc, m, s):
    clear(pool, s.ffn[1])
    o = m.pool_order
    with o.turns(PAIRS, 1) as p:
        wait_apart(pool, m, s.c2_mv, p + 1)
        ln_rstd(pool, o, m, PT, 1e-6, s.c2_rstd)



def c3_tokens_pe(pe, m, s, p):
    pe.wait_ge(s.c3_xn2, p + 1)
    pe.wait_ge(s.c3_xm, p + 1)
    for t in range(PT):
        ins = pe.transpose(m.ps[:, 0, t * P:(t + 1) * P], m.xn2[:, t, :, :].rearrange("p a c -> p (a c)"),
                           m.ident[:])
    ins.then_inc(s.c3_nt, 1)


def c3_t_pe(pe, m, s, p):
    pe.wait_ge(s.c3_xm, p + 2)
    for im in range(2):
        ins = pe.matmul(m.ps[:, 1, im * PLACES:(im + 1) * PLACES].rearrange("p (c b) -> p c b", b=4), m.w_l3[:, :],
                        m.xm[0:C, im, :, :].rearrange("p b c -> p c b"), start=True, stop=True)
    ins.then_inc(s.c3_t, 1)


def c3_pe(pe, nc, m, s):
    for sem in (s.c3_t, s.c3_nt, s.c3_dots, s.c3_y, s.c3_norm,):
        pe.sem_inc(sem, 1)
    with pe.Fori(0, PAIRS) as p:
        c3_tokens_pe(pe, m, s, p)
        pe.wait_ge(s.c3_t_read, p + 1)
        c3_t_pe(pe, m, s, p)
    pe.wait_ge(s.c3_t_read, PAIRS + 1)
    with pe.Fori(0, PAIRS) as r:
        p = r + PAIRS
        c3_tokens_pe(pe, m, s, p)
        pe.wait_ge(s.c3_tr, r + 1)
        c3_t_pe(pe, m, s, p)
        pe.wait_ge(s.c3_sumsq, r + 1)
        pe.wait_ge(s.c3_inv, r + 1)
        pe.matmul(m.ps[:, 2, 0:2], m.one[:, :], m.n2[:, 0:2], start=True, stop=True).then_inc(s.c3_norm, 1)
        pe.wait_ge(s.c3_relu, 2 * r + 1)
        for im in range(2):
            for par in range(2):
                rows = slice(par * C, (par + 1) * C)
                for k in range(2):
                    ins = pe.matmul(m.ps[:, 3 + 3 * im + par, k * P:(k + 1) * P],
                                    m.xm[rows, im, 2 * k:2 * k + 2, :].rearrange("p b c -> p (b c)"),
                                    m.xn2[rows, 2 * im:2 * im + 2, 0, :], start=True, stop=True)
            ins.then_inc(s.c3_dots, 1)
        pe.wait_ge(s.c3_tr, r + 2)
        pe.wait_ge(s.c3_added, r + 1)
        for im in range(2):
            pe.wait_ge(s.c3_sq, 2 * r + im + 2)
            for par in range(2):
                for k in range(2):
                    ins = pe.matmul(m.ps[par * C:(par + 1) * C, 5, im * P:(im + 1) * P], m.tr[:, im, k, :],
                                    m.sim3[:, par, im, k, :], start=(k == 0), stop=(k == 1))
        ins.then_inc(s.c3_y, 1)


def c3_act(act, nc, m, s):
    for sem in (s.c3_xm, s.c3_tr, s.c3_relu,):
        act.sem_inc(sem, 1)
    def evacuate(p):
        act.wait_ge(s.c3_nt, p + 2)
        act.wait_ge(s.c3_t, p + 1)
        act.activation(m.xm[:, :, :, :], m.ps[:, 0, :].rearrange("p (im c b) -> p im b c", im=2, b=4),
                       ACT.Copy).then_inc(s.c3_xm, 1)

    def twice(p):
        act.wait_ge(s.c3_xn, p + 1)
        act.wait_ge(s.c3_nt, p + 1)
        act.activation(m.xn2[:, :, 1, :], m.xn2[:, :, 0, :], ACT.Copy).then_inc(s.c3_xn2, 1)

    with act.Fori(0, PAIRS) as p:
        twice(p)
        evacuate(p)
    act.wait_ge(s.c3_shift, 1)
    with act.Fori(0, PAIRS) as r:
        twice(r + PAIRS)
        act.wait_ge(s.c3_dots, 2 * r + 1)
        evacuate(r + PAIRS)
        act.wait_ge(s.c3_t, r + PAIRS + 2)
        act.wait_ge(s.c3_y, r + 1)
        for half in range(2):
            rows = slice(half * C, (half + 1) * C)
            t = m.ps[rows, 1, :].rearrange("p (im k b o) -> p im k b o", im=2, k=2, b=2)[:, :, :, half, :]
            ins = act.activation(m.tr[rows, :, :, :], t, ACT.Relu, scale=m.bn_scale[rows, :],
                                 bias=m.bn_shift[rows, :])
        ins.then_inc(s.c3_tr, 1)
        act.wait_ge(s.c3_inv, r + 2)
        for im in range(2):
            act.wait_ge(s.c3_dots, 2 * r + im + 2)
            act.wait_ge(s.c3_sq, 2 * r + 1)
            for par in range(2):
                ins = act.activation(m.relu[:, im, par * 2 * P:(par + 1) * 2 * P],
                                     m.ps[:, 3 + 3 * im + par, 0:2 * P], ACT.Relu, scale=m.inv3[:, im:im + 1])
            ins.then_inc(s.c3_relu, 1)


def c3_dve(dve, nc, m, s):
    for sem in (s.c3_t_read, s.c3_inv, s.c3_added, s.c3_sq,):
        dve.sem_inc(sem, 1)
    o = m.dve_order

    def tokens(p, q, first):
        x = m.X[:, bass.ds(q * PT, PT), :]
        ln_stats(dve, o, m, x, PT, s.c3_mv)
        dve.wait_ge(s.c3_rstd, p + 1)
        o.then(dve.tensor_tensor(m.xc[:, 0:PT, :], x, bcast(m.mv[:, 0:PT, 0:1], [P, PT, C]), ALU.subtract))
        dve.wait_ge(s.c3_nt, p + 1)
        if not first:
            dve.wait_ge(s.c3_dots, 2 * q + 1)
        dve.tensor_tensor(m.xn2[:, :, 0, :], m.xc[:, 0:PT, :], bcast(m.rstd[:, 0:PT].unsqueeze(2), [P, PT, C]),
                          ALU.mult).then_inc(s.c3_xn, 1)

    with o.turns(PAIRS, 2) as p:
        tokens(p, p, True)
        wait_apart(dve, m, s.c3_t, p + 2)
        dve.bn_stats(m.bstats[:, bass.ds(p, 1), :].rearrange("p a b -> p (a b)"), m.ps[:, 1, :])\
            .then_inc(s.c3_t_read, 1)
    dve.wait_ge(s.c3_t_read, PAIRS + 1)
    dve.bn_aggr(m.bmv[:, :], m.bstats[:, :, :].rearrange("p a b -> p (a b)")).then_inc(s.c3_bmv, 1)
    dve.wait_ge(s.c3_bmv, 1)
    o.then(dve.tensor_tensor(m.bn_mean[:, :], m.bmv[:, 0:1], m.bn_in[:, 0:1], ALU.add))
    o.then(dve.tensor_tensor(m.bn_shift[:, :], m.bn_in[:, 0:1], m.bn_mean[:, :], ALU.subtract))
    dve.wait_ge(s.c3_brstd, 1)
    o.then(dve.tensor_tensor(m.bn_scale[:, :], m.brstd[:, :], m.bn_in[:, 1:2], ALU.mult))
    o.then(dve.tensor_tensor(m.bn_shift[:, :], m.bn_shift[:, :], m.bn_scale[:, :], ALU.mult))
    dve.tensor_tensor(m.bn_shift[:, :], m.bn_shift[:, :], m.bn_in[:, 2:3], ALU.add).then_inc(s.c3_shift, 1)
    with o.turns(PAIRS, 3) as r:
        tokens(r + PAIRS, r, False)
        dve.wait_ge(s.c3_xn, r + PAIRS + 1)
        o.then(dve.tensor_tensor(m.xc[:, 0:PT, :], m.xn2[:, :, 0, :], m.xn2[:, :, 0, :], ALU.mult))
        dve.wait_ge(s.c3_norm, r + 1)
        dve.tensor_reduce(m.n2[:, 0:2], m.xc[:, 0:PT, :].rearrange("p (im t) c -> p im (t c)", im=2), AX, ALU.add)\
            .then_inc(s.c3_sumsq, 1)
        dve.wait_ge(s.c3_norm, r + 2)
        dve.wait_ge(s.c3_relu, 2 * r + 1)
        dve.reciprocal(m.inv3[:, :], m.ps[:, 2, 0:2]).then_inc(s.c3_inv, 1)
        for im in range(2):
            dve.wait_ge(s.c3_relu, 2 * r + im + 2)
            dve.wait_ge(s.c3_y, r + 1)
            src = m.relu[:, im, :].rearrange("p (a k n) -> p a (k n)", a=2, k=2)
            dve.tensor_tensor(m.sim3[:, :, im, :, :].rearrange("p a k n -> p a (k n)"), src, src, ALU.mult)\
                .then_inc(s.c3_sq, 1)
        dve.wait_ge(s.c3_y, r + 2)
        x = m.X[:, bass.ds(r * PT, PT), :]
        dve.tensor_tensor(x, x, m.ps[:, 5, 0:PT * C].rearrange("p (t c) -> p t c", c=C), ALU.add)\
            .then_inc(s.c3_added, 1)


def c3_pool(pool, nc, m, s):
    o = m.pool_order
    with o.turns(PAIRS, 1) as p:
        wait_apart(pool, m, s.c3_mv, p + 1)
        ln_rstd(pool, o, m, PT, 1e-6, s.c3_rstd)
    pool.wait_ge(s.c3_bmv, 1)
    o.then(pool.tensor_scalar(m.bveps[:, :], m.bmv[:, 1:2], 1e-5, 1.0, ALU.add, ALU.mult))
    pool.tensor_tensor(m.brstd[:, :], m.bveps[:, :], m.minus_half[:, 0:1], ALU.pow).then_inc(s.c3_brstd, 1)
    with o.turns(PAIRS, 1) as p:
        wait_apart(pool, m, s.c3_mv, p + PAIRS + 1)
        ln_rstd(pool, o, m, PT, 1e-6, s.c3_rstd)



def prepare_pe(pe, nc, m, s):
    pe.wait_ge(s.ld_small, 16 * SMALL_LOADS)
    pe.wait_ge(s.ld_ident, 16)
    for k, (slot, n) in enumerate(((3, 65), (4, 65), (5, 64), (6, 65), (7, 64), (1, 65), (2, 65))):
        pe.transpose(m.ps[0:n, 0, k * C:(k + 1) * C], m.nat[0:C, slot, 0:n], m.ident[0:C, 0:C])
    pe.transpose(m.ps[:, 1, 0:B1ROWS], m.b1nat[:, :], m.ident[0:B1ROWS, 0:B1ROWS]).then_inc(s.weights_t, 1)


def prepare_act(act, nc, m, s):
    act.wait_ge(s.weights_t, 1)
    act.wait_ge(s.padded, 1)
    act.activation(m.wqk[:, 0:C], m.ps[0:C + 1, 0, 5 * C:6 * C], ACT.Copy, scale=SCALE)
    act.activation(m.wqk[:, C:2 * C], m.ps[0:C + 1, 0, 6 * C:7 * C], ACT.Copy)
    act.activation(m.wv[:, :], m.ps[0:C + 1, 0, 0:C], ACT.Copy)
    act.activation(m.wpn[:, :], m.ps[0:C + 1, 0, C:2 * C], ACT.Copy)
    act.activation(m.wpp[:, :], m.ps[0:C, 0, 2 * C:3 * C], ACT.Copy)
    act.activation(m.w_l2[:, :], m.ps[0:C + 1, 0, 3 * C:4 * C], ACT.Copy)
    for k in range(2):
        act.activation(m.w_l3[:, k * C:(k + 1) * C], m.ps[0:C, 0, 4 * C:5 * C], ACT.Copy)
    act.activation(m.b1t[:, :], m.ps[:, 1, 0:B1ROWS], ACT.Copy)
    act.activation(m.mask[:, :], m.mask_in, ACT.Copy, scale=NEG)
    act.activation(m.identb[:, :], m.ident[:, :], ACT.Copy).then_inc(s.prepared, 1)


def prepare_dve(dve, nc, m, s):
    o = m.dve_order
    dve.wait_ge(s.ld_small, 16 * SMALL_LOADS)
    neg = m.partsel[:, 2:4]
    for k in range(2):
        o.then(dve.tensor_copy(m.b2p[:, :, :], m.b2[:, :, :]))
        o.then(dve.scalar_tensor_tensor(m.b2[:, :, :], m.b2p[:, :, :], neg[:, k:k + 1], m.b2[:, :, :],
                                        ALU.mult, ALU.add))
    o.then(dve.tensor_copy(m.b2p[:, :, :], m.b2[:, :, :]))



def out_dve(dve, nc, m, s):
    with dve.Fori(0, PAIRS) as g:
        dve.wait_ge(s.out_t, g + 1)
        x = m.X[:, bass.ds(g * PT, PT), :]
        dve.tensor_copy(m.stage[:, :, :, :], x.rearrange("p (a i) c -> p i a c", i=2)).then_inc(s.out_x, 1)


def out_pe(pe, nc, m, s):
    pe.sem_inc(s.out_t, 1)
    pe.sem_inc(s.out_y, 1)
    with pe.Fori(0, PAIRS) as g:
        pe.wait_ge(s.out_x, g + 1)
        pe.wait_ge(s.out_y, g + 1)
        for i in range(2):
            ins = pe.transpose(m.ps[:, 0, i * P:(i + 1) * P], m.stage[:, i, :, :], m.ident[:])
        ins.then_inc(s.out_t, 1)


def out_act(act, nc, m, s):
    with act.Fori(0, PAIRS) as g:
        act.wait_ge(s.out_t, g + 2)
        act.activation(m.y[:, bass.ds(g, 1), :].rearrange("p a n -> p (a n)"), m.ps[:, 0, 0:PLACES], ACT.Copy).then_inc(s.out_y, 1)


def out_sync(sp, nc, m, s, out):
    y = out.rearrange("(g a) c h w -> g (a c) (h w)", a=2)
    with sp.Fori(0, PAIRS) as g:
        sp.wait_ge(s.out_y, g + 2)
        sp.dma_start(y[bass.ds(g, 1), :, :].rearrange("g p w -> p (g w)"),
                     m.y[:, bass.ds(g, 1), :].rearrange("p a n -> p (a n)")).then_inc(s.out_sent, 16)
    sp.wait_ge(s.out_sent, 16 * PAIRS)


FFN_SEMS = ["mv", "rstd", "xn", "part1", "rest", "part2", "parts", "transposed", "xa", "xb", "logits",
            "logits_read", "hidden", "act", "silu", "down", "weighed", "added", "below_max", "exps",
            "order", "pool_order"]
SEMS = ["ld_ident", "ld_first", "ld_up", "ld_small", "codes_t", "codes_sq", "codes_n", "codes_ready", "codes_1", "codes_2", "codes_rest", "c0_z1", "c0_z2", "c0_rest",
        "c0_in",
        "c2_mv", "c2_rstd", "c2_xn", "c2_nt", "c2_xf", "c2_nq", "c2_inv", "c2_relu", "c2_dots", "c2_diag", "c2_tx", "c2_lin", "c2_added", "c2_sim", "c2_y", "c2_sq", 
        "c3_mv", "c3_rstd", "c3_xn", "c3_xn2", "c3_nt", "c3_xm", "c3_t", "c3_t_read", "c3_bmv", "c3_brstd", "c3_shift", "c3_sumsq", "c3_norm", "c3_inv", "c3_dots", "c3_relu", "c3_tr", "c3_sq", "c3_y", "c3_added", 
        "c1_mv", "c1_rstd", "c1_xn", "c1_nt", "c1_xf", "c1_qk", "c1_vals", "c1_part1", "c1_part2", "c1_part3", "c1_rest", "c1_selq", "c1_selk", "c1_qs", "c1_ks", "c1_v", "c1_v_read", "c1_s", "c1_max", "c1_m", "c1_mt", "c1_q2", "c1_st", "c1_p", "c1_o", "c1_em", "c1_on", "c1_ot", "c1_ot_read", "c1_y", "c1_added", "c0_xt", "c0_mv", "c0_rstd", "c0_xn", "c0_nt", "c0_xf", "c0_zp", "c0_z", "c0_read",
        "c0_scored", "ones_rows", "split_a", "split_r", "split_b", 
        "weights_t", "padded", "prepared", "out_t", "out_x", "out_y", "out_sent", "part_done", "apart",
        "dve_order", "pool_order"]


FfnSems = namedtuple("FfnSems", FFN_SEMS)
Sems = namedtuple("Sems", SEMS + ["c0_gathered", "ffn"])


class Memory:
    pass


def program(nc, d, out):
    with ExitStack() as ctx:
        m = Memory()

        def sb(name, shape, dt=F32):
            return ctx.enter_context(nc.sbuf_tensor(name, shape, dt))

        new = lambda name: ctx.enter_context(nc.semaphore(name))
        s = Sems(*[new(n) for n in SEMS],
                 c0_gathered=[new(f"c0_gathered{j}") for j in range(PT)],
                 ffn=[FfnSems(*[new(f"ffn{l}_{n}") for n in FFN_SEMS]) for l in range(2)] * 2)
        m.apart = s.apart
        m.ps = ctx.enter_context(nc.psum_tensor("ps", [P, 8, 512], F32))
        m.X = sb("X", [P, TILES, C])
        m.ident = sb("ident", [P, P])
        m.identb = sb("identb", [P, P], BF16)
        m.nat = sb("nat", [C, 8, C + 1])
        m.emb = sb("emb", [P, CODES // P, 2, C])
        m.rest_of_codes = sb("rest_of_codes", [P, CODES])
        m.norm_parts = sb("norm_parts", [3, CODES], BF16)
        m.proj0 = sb("proj0", [C + 1, 2 * C])
        m.minus_one = sb("minus_one", [P, C + 1])
        m.minus_half = sb("minus_half", [P, ST])
        m.xload = sb("xload", [P, PLACES])
        m.stats = sb("stats", [P, ST, 6])
        m.mv = sb("mv", [P, ST, 2])
        m.veps = sb("veps", [P, ST])
        m.rstd = sb("rstd", [P, ST])
        m.xc = sb("xc", [P, ST, C])
        m.xn = sb("xn", [P, ST, C])
        m.xf = sb("xf", [C + 1, 512])
        m.best = sb("best", [P, PT, 8])
        m.code = sb("code", [P, PT, 8], U32)
        m.zq = [sb(f"zq{j}", [P, C]) for j in range(PT)]
        m.wall = sb("wall", [P, WPAD + 8])
        m.w1 = sb("w1", [P, WPAD], BF16)
        m.w2 = sb("w2", [P, WPAD], BF16)
        m.w3 = sb("w3", [P, WPAD], BF16)
        m.gate_b = {l: sb(f"gate_b{l}", [P, FFN[l]["E"]]) for l in (0, 2, 3)}
        m.down = [sb(f"down{l}", [P, ffn_counts(l)[1], C]) for l in range(4)]
        m.b1nat = sb("b1nat", [B1ROWS, P])
        m.b1t = sb("b1t", [P, B1ROWS])
        m.b2 = sb("b2", [3, B2ROWS, C])
        m.b2p = sb("b2p", [3, B2ROWS, C], BF16)
        m.partsel = sb("partsel", [3, 4])
        m.ones3 = sb("ones3", [3, P], BF16)
        m.bn_in = sb("bn_in", [P, 3])
        m.mask = sb("mask", [P, MASK_COLS], BF16)
        m.padn = sb("padn", [P, 2 * HEADS])
        m.padmax = sb("padmax", [P, 2 * HEADS])
        m.iota = sb("iota", [P, 16])
        m.wqk = sb("wqk", [C + 1, 2 * C])
        m.wv = sb("wv", [C + 1, C])
        m.wpn = sb("wpn", [C + 1, C])
        m.wpp = sb("wpp", [C, C])
        m.w_l2 = sb("w_l2", [C + 1, C])
        m.w_l3 = sb("w_l3", [C, P])
        m.parts = sb("parts", [P, ST, 3, C], BF16)
        m.xa = sb("xa", [P, SPAN], BF16)
        m.xb = sb("xb", [P, SPAN], BF16)
        m.hid = m.wall[:, 0:2 * SPAN].rearrange("p (a n) -> p a n", a=2)
        m.silu = m.wall[:, 2 * SPAN:3 * SPAN].rearrange("p (a n) -> p a n", a=2)
        m.prod = m.wall[:, 3 * SPAN:4 * SPAN].rearrange("p (a t c) -> p a t c", a=2, t=ST)
        m.sel = m.wall[:, 4 * SPAN:4 * SPAN + 2 * 3 * BLOCKS * P // 2].bitcast(BF16).rearrange(
            "p (a k b r) -> p a k b r", a=2, k=3, b=BLOCKS)
        m.qkp = m.parts[:, :, :, :].rearrange("p t k c -> p (t k c)").rearrange("p (k n) -> p k n", k=3)
        m.qk_rest = m.xa[:, :].bitcast(F32)
        m.z_rest = m.parts[:, :, :, :].rearrange("p t k c -> p (t k c)")[:, 0:1024].bitcast(F32)
        m.y = m.wall[:, 0:PAIRS * PLACES].rearrange("p (g n) -> p g n", g=PAIRS)
        m.xfp = sb("xfp", [C + 1, 512])
        m.qs = sb("qs", [P, BLOCKS, 512], BF16)
        m.ks = sb("ks", [P, BLOCKS, 512], BF16)
        m.q2 = sb("q2", [P, BLOCKS, PLACES], BF16)
        m.vals_next = sb("vals_next", [P, PT, C])
        m.vals = sb("vals", [P, PT, HEADS, HD + 1])
        m.maxr = sb("maxr", [P, PT, HEADS])
        m.maxp = sb("maxp", [P, PT, HEADS])
        m.maxes = sb("maxes", [P, PT, BLOCKS, P], BF16)
        m.maxparts = sb("maxparts", [P, 2, HEADS, 3], BF16)
        m.maxrest = sb("maxrest", [P, 2, HEADS])
        m.minus_rows = sb("minus_rows", [P, 1])
        m.pt = sb("pt", [P, PT, BANKS3])
        m.emax = sb("emax", [P, PT, HEADS])
        m.den = sb("den", [P, PT, HEADS])
        m.rden = sb("rden", [P, PT, HEADS])
        m.att = sb("att", [P, PT, C])
        m.ot1 = sb("ot1", [C + 1, 512])
        m.ot2 = sb("ot2", [C, 512])
        m.one = sb("one", [P, P])
        m.n2 = sb("n2", [P, PT])
        m.rn2 = sb("rn2", [P, PT])
        m.codes_a = m.ks[:, 0:2, :].rearrange("p a k -> p (a k)")
        m.codes_b = m.ks[:, 2:4, :].rearrange("p a k -> p (a k)")
        m.codes_c = m.q2[:, 0:4, :].rearrange("p a k -> p (a k)")
        m.codes_sq = m.pt[0:C, 0, 0:CODES]
        m.norms = m.pt[0:3, 3, 0:CODES]
        m.wrest = m.pt[:, 1, 0:WCHUNK]
        m.mask_in = m.pt[:, 2, 0:MASK_COLS]
        room = m.pt[:, :, :].rearrange("p t k -> p (t k)")
        m.diag = room[:, 0:PT * P].rearrange("p (t q) -> p t q", q=P)
        m.d2, m.inv, m.relu, m.relu2, m.sim = (
            room[:, k * 1024:(k + 1) * 1024].rearrange("p (im q) -> p im q", im=2) for k in range(5))
        m.sim3 = m.d2.rearrange("p im q -> p (im q)").rearrange("p (a im k n) -> p a im k n", a=2, im=2, k=2)
        m.sim = m.sim.rearrange("p im (k q) -> p im k q", k=2)
        m.tx = sb("tx", [P, PT, C])
        m.xn2 = sb("xn2", [P, PT, 2, C])
        m.xm = sb("xm", [P, 2, 4, C])
        m.tr = sb("tr", [P, 2, 2, C])
        m.inv3 = sb("inv3", [P, 2])
        m.bstats = sb("bstats", [P, PAIRS, 6])
        m.bmv = sb("bmv", [P, 2])
        m.bn_mean, m.bn_scale, m.bn_shift, m.brstd, m.bveps = (
            sb(name, [P, 1]) for name in ("bn_mean", "bn_scale", "bn_shift", "brstd", "bveps"))
        m.lg = sb("lg", [P, ST, 16])
        m.below = sb("below", [P, ST, 17])
        m.ex = sb("ex", [P, ST, 17])
        m.top = sb("top", [P, ST, 8])
        m.topi = sb("topi", [P, ST, 8], U32)
        m.topf = sb("topf", [P, ST, 2])
        m.hit = sb("hit", [P, 2, ST, 16])
        m.sums = sb("sums", [P, ST])
        m.rsum = sb("rsum", [P, ST])
        m.prob = sb("prob", [P, 2, ST])
        m.cw = sb("cw", [P, ST, 16])
        m.stage = sb("stage", [P, 2, 2, C])
        block = ctx.enter_context(nc.Block())

        @block.sync
        def _(sp):
            load_first(sp, nc, m, s, d)

            def pair(g):
                sp.wait_ge(s.c0_xt, g)
                sp.dma_start(m.xload[:, :], pair_of_images(d.x, g)).then_inc(s.c0_in, 16)

            load_rest(sp, nc, m, s, d, lambda: pair(1))
            with sp.Fori(2, PAIRS) as g:
                pair(g)
            out_sync(sp, nc, m, s, out)

        @block.tensor
        def _(pe):
            c0_pe(pe, nc, m, s)
            barrier(pe, s, 1)
            prepare_pe(pe, nc, m, s)
            barrier(pe, s, 2)
            ffn_pe(pe, nc, m, s, 0)
            barrier(pe, s, 3)
            c1_pe(pe, nc, m, s)
            barrier(pe, s, 4)
            ffn_pe(pe, nc, m, s, 1)
            barrier(pe, s, 5)
            c2_pe(pe, nc, m, s)
            barrier(pe, s, 6)
            ffn_pe(pe, nc, m, s, 2)
            barrier(pe, s, 7)
            c3_pe(pe, nc, m, s)
            barrier(pe, s, 8)
            ffn_pe(pe, nc, m, s, 3)
            barrier(pe, s, 9)
            out_pe(pe, nc, m, s)

        @block.scalar
        def _(act):
            c0_act(act, nc, m, s)
            barrier(act, s, 1)
            prepare_act(act, nc, m, s)
            barrier(act, s, 2)
            ffn_act(act, nc, m, s, 0)
            barrier(act, s, 3)
            c1_act(act, nc, m, s)
            barrier(act, s, 4)
            ffn_act(act, nc, m, s, 1)
            barrier(act, s, 5)
            c2_act(act, nc, m, s)
            barrier(act, s, 6)
            ffn_act(act, nc, m, s, 2)
            barrier(act, s, 7)
            c3_act(act, nc, m, s)
            barrier(act, s, 8)
            ffn_act(act, nc, m, s, 3)
            barrier(act, s, 9)
            out_act(act, nc, m, s)

        @block.vector
        def _(dve):
            m.dve_order = Order(dve, s.dve_order)
            c0_dve(dve, nc, m, s)
            barrier(dve, s, 1)
            prepare_dve(dve, nc, m, s)
            barrier(dve, s, 2)
            ffn_dve(dve, nc, m, s, 0)
            barrier(dve, s, 3)
            c1_dve(dve, nc, m, s)
            barrier(dve, s, 4)
            ffn_dve(dve, nc, m, s, 1)
            barrier(dve, s, 5)
            c2_dve(dve, nc, m, s)
            barrier(dve, s, 6)
            ffn_dve(dve, nc, m, s, 2)
            barrier(dve, s, 7)
            c3_dve(dve, nc, m, s)
            barrier(dve, s, 8)
            ffn_dve(dve, nc, m, s, 3)
            barrier(dve, s, 9)
            out_dve(dve, nc, m, s)

        @block.gpsimd
        def _(pool):
            m.pool_order = Order(pool, s.pool_order)
            c0_pool(pool, nc, m, s, d)
            barrier(pool, s, 1)
            make_sel(pool, m, s)
            barrier(pool, s, 2)
            ffn_pool(pool, nc, m, s, 0)
            barrier(pool, s, 3)
            c1_pool(pool, nc, m, s)
            barrier(pool, s, 4)
            ffn_pool(pool, nc, m, s, 1)
            barrier(pool, s, 5)
            c2_pool(pool, nc, m, s)
            barrier(pool, s, 6)
            ffn_pool(pool, nc, m, s, 2)
            barrier(pool, s, 7)
            c3_pool(pool, nc, m, s)
            barrier(pool, s, 8)
            ffn_pool(pool, nc, m, s, 3)
            barrier(pool, s, 9)


def attention_tables():
    mask = np.zeros((P, MASK_COLS), np.float32)
    padn = np.zeros((P, 2, HEADS), np.float32)
    for t in range(2):
        for r in range(P):
            for (ks, dil, heads), (kind, lo) in zip(RANGES, (("near", 0), ("rows", 1), ("all", 2))):
                y, x = place(kind, t, r)
                reach = ks // 2
                inside = 0
                for c in range(WIDTH[kind]):
                    ky, kx = key_place(kind, t, c)
                    dy, dx = ky - y, kx - x
                    sees = dy % dil == 0 and dx % dil == 0 and abs(dy) <= reach * dil and abs(dx) <= reach * dil
                    inside += sees
                    mask[r, t * MASK_TILE + MASK_AT[kind] + c] = not sees
                for h in heads:
                    padn[r, t, (0, 1, 2, 3, 7, 4, 5, 6).index(h)] = ks * ks - inside
    padmax = np.where(padn > 0, 0.0, -3e38).astype(np.float32)
    return mask, padn.reshape(P, -1), padmax.reshape(P, -1)


WIDTH = dict(near=160, rows=128, all=256)
MASK_AT = dict(near=0, all=160, rows=416)
MASK_TILE = 160 + 128 + 256
MASK_COLS = 2 * MASK_TILE


def place(kind, t, r):
    if kind == "rows":
        return 2 * (r // SIDE) + t, r % SIDE
    return (t * P + r) // SIDE, r % SIDE


def key_place(kind, t, c):
    if kind == "rows":
        return place(kind, t, c)
    if kind == "near":
        c += t * (PLACES - WIDTH["near"])
    return c // SIDE, c % SIDE


def constants():
    mask, padn, padmax = attention_tables()
    partsel = np.array([[0, 0, 0, 0], [1, 0, 0, 0], [1, 1, 0, 0]], np.float32)[:, :2].copy()
    minus_rows = np.zeros((P, 1), np.float32)
    for half in range(2):
        at = half * C + SPLIT_ROWS
        minus_rows[at:at + 3] = -1.0
    return dict(minus_rows=minus_rows, ident=np.eye(P, dtype=np.float32), mask_table=mask, padn=padn, padmax=padmax, partsel=partsel,
                iota=np.tile(np.arange(16, dtype=np.float32), (P, 1)))


INPUTS = [
    "x", "L0_conv_proj_w", "L0_conv_proj_b", "L0_conv_emb",
    "L0_ffn_gate_w", "L0_ffn_gate_b", "L0_ffn_W1", "L0_ffn_b1", "L0_ffn_W2", "L0_ffn_b2",
    "L1_conv_qkv_w0", "L1_conv_qkv_b0", "L1_conv_qkv_w1", "L1_conv_qkv_b1", "L1_conv_qkv_w2", "L1_conv_qkv_b2",
    "L1_conv_proj_w", "L1_conv_proj_b",
    "L1_ffn_router_w", "L1_ffn_w1", "L1_ffn_b1", "L1_ffn_w2", "L1_ffn_b2",
    "L2_conv_W", "L2_conv_bias", "L2_ffn_gate_w", "L2_ffn_gate_b", "L2_ffn_w1", "L2_ffn_w2", "L2_ffn_w3",
    "L3_conv_conv_w", "L3_conv_conv_b", "L3_conv_bn_gamma", "L3_conv_bn_beta",
    "L3_ffn_gate_w", "L3_ffn_gate_b", "L3_ffn_W1", "L3_ffn_b1", "L3_ffn_W2", "L3_ffn_b2"]


def kernel(**inputs):
    import concourse.bacc as bacc
    from concourse.bass_utils import run_bass_kernel_spmd

    nc = bacc.Bacc("TRN2", target_bir_lowering=False, num_devices=1)
    arrays, args = {}, {}
    for name, a in list({n: inputs[n] for n in INPUTS}.items()) + list(constants().items()):
        a = np.ascontiguousarray(a)
        arrays[f"in_{name}_dram"] = a
        args[name] = nc.dram_tensor(f"in_{name}_dram", a.shape, mybir.dt.from_np(a.dtype), kind="ExternalInput").ap()
    out = nc.dram_tensor("out_dram", (IMAGES, C, SIDE, SIDE), F32, kind="ExternalOutput").ap()
    program(nc, namedtuple("Inputs", list(args))(**args), out)
    r = run_bass_kernel_spmd(nc, [arrays], core_ids=[0])
    return r.results[0]["out_dram"]
```

```python
from collections import namedtuple
from contextlib import ExitStack, contextmanager

import numpy as np

import concourse.bass as bass
from concourse import mybir

F32 = mybir.dt.float32
BF16 = mybir.dt.bfloat16
U32 = mybir.dt.uint32
ALU = mybir.AluOpType
ACT = mybir.ActivationFunctionType
AX = mybir.AxisListType.X

P = 128
C = 64
IMAGES = 16
SIDE = 16
PLACES = SIDE * SIDE
TILES = IMAGES * PLACES // P
CODES = 1024
PAIRS = IMAGES // 2
PT = TILES // PAIRS
SUPERS = 4
ST = TILES // SUPERS
SPAN = ST * P
HALF = SPAN // 2

HEADS, HD = 8, 8
SCALE = HD ** -0.5
NEG = -1e30

RANGES = [(5, 1, (0, 1, 2, 3)), (7, 2, (4, 5, 6)), (9, 3, (7,))]

FFN = [
    dict(E=8, H=128, gated=False, renorm=False, floor=None, gate_b=True, b1=True, b2=True, keep=False),
    dict(E=8, H=64, gated=False, renorm=True, floor=1e-12, gate_b=False, b1=True, b2=True, keep=True),
    dict(E=16, H=128, gated=True, renorm=True, floor=None, gate_b=True, b1=False, b2=False, keep=False),
    dict(E=8, H=128, gated=False, renorm=False, floor=None, gate_b=True, b1=True, b2=True, keep=False),
]


def weight_columns():
    at, where = 0, []
    for f in FFN:
        w = dict(up=at)
        at += f["E"] * f["H"]
        if f["gated"]:
            w["up2"] = at
            at += f["E"] * f["H"]
        w["gate"] = at
        at += f["E"]
        where.append(w)
    return where, at


WHERE, WCOLS = weight_columns()
SPLIT_TURNS = PAIRS - 1
WPAD = -(-WCOLS // SPLIT_TURNS) * SPLIT_TURNS
WCHUNK = WPAD // SPLIT_TURNS
E1 = [0, 8, None, 12]
E2 = [0, 8, None, 16]
B1ROWS, B2ROWS = 20, 24


class Order:

    def __init__(self, eng, sem):
        self.eng, self.sem, self.base, self.n = eng, sem, 0, 0

    def step(self, ins):
        ins.then_inc(self.sem, 1)
        self.n += 1
        return self.base + self.n

    def then(self, ins):
        self.eng.wait_ge(self.sem, self.step(ins))

    def then_apart(self, ins, m):
        wait_apart(self.eng, m, self.sem, self.step(ins))

    @contextmanager
    def turns(self, count, per):
        start = self.base + self.n
        with self.eng.Fori(0, count) as i:
            self.base, self.n = i * per + start, 0
            yield i
            assert self.n == per, f"{self.n} steps a turn, not {per}"
        self.base, self.n = start + count * per, 0


def barrier(eng, s, n):
    eng.drain().then_inc(s.part_done, 1)
    eng.wait_ge(s.part_done, 4 * n)


def wait_apart(eng, m, sem, value):
    eng.wait_ge(sem, value)
    eng.sem_inc(m.apart, 1)


def bcast(ap, shape):
    return ap.broadcast_to(shape)



def ln_stats(dve, o, m, x, n, done):
    for j in range(n):
        ins = dve.bn_stats(m.stats[:, j, :], x[:, j, :])
    o.then_apart(ins, m)
    for j in range(n):
        ins = dve.bn_aggr(m.mv[:, j, :], m.stats[:, j, :])
    ins.then_inc(done, 1)


def ln_rstd(pool, o, m, n, eps, done):
    o.then(pool.tensor_scalar(m.veps[:, 0:n], m.mv[:, 0:n, 1], eps, 1.0, ALU.add, ALU.mult))
    pool.tensor_tensor(m.rstd[:, 0:n], m.veps[:, 0:n], m.minus_half[:, 0:n], ALU.pow).then_inc(done, 1)


def ln_apply(dve, o, m, x, n, done):
    o.then(dve.tensor_tensor(m.xc[:, 0:n, :], x, bcast(m.mv[:, 0:n, 0:1], [P, n, C]), ALU.subtract))
    dve.tensor_tensor(m.xn[:, 0:n, :], m.xc[:, 0:n, :], bcast(m.rstd[:, 0:n].unsqueeze(2), [P, n, C]),
                      ALU.mult).then_inc(done, 1)



def load_first(sp, nc, m, s, d):
    sp.dma_start(m.ident[:], d.ident).then_inc(s.ld_ident, 16)
    sp.dma_start(m.xload[:, :], pair_of_images(d.x, 0)).then_inc(s.c0_in, 16)
    loads = [
        (m.emb[:, :, 0, :], d.L0_conv_emb.rearrange("(k p) c -> p k c", p=P)),
        (m.emb[:, :, 1, :], d.L0_conv_emb.rearrange("(k p) c -> p k c", p=P)),
        (m.nat[0:C, 0, 0:C], d.L0_conv_proj_w),
        (m.nat[0:C, 0, C:C + 1], d.L0_conv_proj_b.rearrange("(o a) -> o a", a=1)),
        (m.partsel[:, 0:2], d.partsel),
    ]
    for dst, src in loads:
        sp.dma_start(dst, src, allow_slow_non_contiguous=src.shape[-1] == 1).then_inc(s.ld_first, 16)
    assert len(loads) == FIRST_LOADS


def pair_of_images(x, g):
    return x.rearrange("(g a) c h w -> g (a c) (h w)", a=2)[bass.ds(g, 1), :, :].rearrange("g p w -> p (g w)")


FIRST_LOADS = 5


def load_rest(q, nc, m, s, d, next_pair):
    n = 0

    def ld(dst, src, sem, slow=False):
        nonlocal n
        q.dma_start(dst, src, allow_slow_non_contiguous=src.shape[-1] == 1 or slow).then_inc(sem, 16)
        n += 1

    for half in range(2):
        rows = slice(half * C, half * C + C)
        for f, (cfg, w) in enumerate(zip(FFN, WHERE)):
            E, H = cfg["E"], cfg["H"]
            ups = {0: [d.L0_ffn_W1], 1: [d.L1_ffn_w1], 2: [d.L2_ffn_w1, d.L2_ffn_w2], 3: [d.L3_ffn_W1]}[f]
            for key, up in zip(("up", "up2"), ups):
                ld(m.wall[rows, w[key]:w[key] + E * H].rearrange("c (e h) -> c e h", e=E),
                   up.rearrange("e c h -> c e h"), s.ld_up)
            gate = {0: d.L0_ffn_gate_w, 1: d.L1_ffn_router_w.rearrange("e c -> c e"),
                    2: d.L2_ffn_gate_w, 3: d.L3_ffn_gate_w}[f]
            ld(m.wall[rows, w["gate"]:w["gate"] + E], gate, s.ld_up, slow=f == 1)
    assert n == UP_LOADS
    n = 0
    next_pair()
    for l, gb in ((0, d.L0_ffn_gate_b), (2, d.L2_ffn_gate_b), (3, d.L3_ffn_gate_b)):
        ld(m.gate_b[l][:, :], gb.partition_broadcast(P), s.ld_small)
    ld(m.down[0][:, :, :], d.L0_ffn_W2.rearrange("e h c -> h e c"), s.ld_small)
    for i in range(2):
        ld(m.down[1][i * C:(i + 1) * C, :, i, :], d.L1_ffn_w2.rearrange("(g i) h c -> i h g c", i=2)[i], s.ld_small)
    ld(m.down[2][:, :, :], d.L2_ffn_w3.rearrange("e h c -> h e c"), s.ld_small)
    ld(m.down[3][:, :, :], d.L3_ffn_W2.rearrange("e h c -> h e c"), s.ld_small)
    ld(m.b1nat[0:8, :], d.L0_ffn_b1, s.ld_small)
    ld(m.b1nat[8:12, :], d.L1_ffn_b1.rearrange("(g i) h -> g (i h)", i=2), s.ld_small)
    ld(m.b1nat[12:20, :], d.L3_ffn_b1, s.ld_small)
    for l, b2 in ((0, d.L0_ffn_b2), (1, d.L1_ffn_b2), (3, d.L3_ffn_b2)):
        ld(m.b2[:, E2[l]:E2[l] + 8, :], b2.partition_broadcast(3), s.ld_small)
    q.wait_ge(s.padded, 1)
    for slot, off in ((1, 0), (2, C), (3, 2 * C)):
        for (a, b), at, w, bias in (((0, 32), 0, d.L1_conv_qkv_w0, d.L1_conv_qkv_b0),
                                    ((56, 64), 32, d.L1_conv_qkv_w2, d.L1_conv_qkv_b2),
                                    ((32, 56), 40, d.L1_conv_qkv_w1, d.L1_conv_qkv_b1)):
            to = slice(at, at + b - a)
            ld(m.nat[to, slot, 0:C], w[off + a:off + b, :], s.ld_small)
            ld(m.nat[to, slot, C:C + 1], bias[off + a:off + b].rearrange("(o a) -> o a", a=1), s.ld_small)
    ld(m.nat[0:C, 4, 0:32], d.L1_conv_proj_w[:, 0:32], s.ld_small)
    ld(m.nat[0:C, 4, 32:40], d.L1_conv_proj_w[:, 56:64], s.ld_small)
    ld(m.nat[0:C, 4, C:C + 1], d.L1_conv_proj_b.rearrange("(o a) -> o a", a=1), s.ld_small)
    ld(m.nat[0:C, 5, 40:64], d.L1_conv_proj_w[:, 32:56], s.ld_small)
    ld(m.nat[0:C, 6, 0:C], d.L2_conv_W, s.ld_small)
    ld(m.nat[0:C, 6, C:C + 1], d.L2_conv_bias.rearrange("(o a) -> o a", a=1), s.ld_small)
    ld(m.nat[0:C, 7, 0:C], d.L3_conv_conv_w, s.ld_small)
    for half in range(2):
        rows = slice(half * C, half * C + C)
        for k, v in enumerate((d.L3_conv_conv_b, d.L3_conv_bn_gamma, d.L3_conv_bn_beta)):
            ld(m.bn_in[rows, k:k + 1], v.rearrange("(o a) -> o a", a=1), s.ld_small)
    ld(m.mask_in, d.mask_table, s.ld_small)
    ld(m.padn[:, :], d.padn, s.ld_small)
    ld(m.minus_rows[:, :], d.minus_rows, s.ld_small)
    ld(m.padmax[:, :], d.padmax, s.ld_small)
    ld(m.iota[:, :], d.iota, s.ld_small)
    assert n == SMALL_LOADS, n


UP_LOADS = 2 * (5 + 4)
SMALL_LOADS = 3 + 5 + 3 + 3 + 18 + 4 + 3 + 6 + 5



def c0_pe_first(pe, nc, m, s):
    pe.wait_ge(s.ld_first, 16 * FIRST_LOADS)
    pe.transpose(m.ps[0:C + 1, 6, 0:C], m.nat[0:C, 0, :], m.ident[0:C, 0:C])
    for k in range(CODES // P):
        ins = pe.transpose(m.ps[:, k // 4, (k % 4) * P:(k % 4 + 1) * P],
                           m.emb[:, k, :, :].rearrange("p a c -> p (a c)"), m.ident[:])
    ins.then_inc(s.codes_t, 1)
    pe.wait_ge(s.codes_sq, 1)
    pe.wait_ge(s.ones_rows, 1)
    for k in range(2):
        ins = pe.matmul(m.ps[0:3, 2 + k, :], m.minus_one[0:C, 0:3], m.codes_sq[:, k * 512:(k + 1) * 512],
                        start=True, stop=True)
    ins.then_inc(s.codes_n, 1)


def c0_act_first(act, nc, m, s):
    codes = m.ps[:, 0:2, :].rearrange("c a k -> c (a k)")
    act.wait_ge(s.codes_t, 1)
    act.activation(m.codes_sq[:, :], codes[0:C, :], ACT.Square).then_inc(s.codes_sq, 1)
    act.activation(m.codes_a, codes, ACT.Copy, scale=2.0).then_inc(s.codes_1, 1)
    for half in range(2):
        act.activation(m.proj0[:, half * C:half * C + C], m.ps[0:C + 1, 6, 0:C], ACT.Copy)
    act.wait_ge(s.codes_rest, 1)
    act.activation(m.codes_c[C:P, :], m.codes_a[C:P, :], ACT.Copy)
    act.activation(m.codes_b, m.rest_of_codes[:, :], ACT.Copy).then_inc(s.codes_2, 1)


def c0_dve_first(dve, nc, m, s, o):
    codes = m.ps[:, 0:2, :].rearrange("c a k -> c (a k)")
    neg = m.partsel[:, 2:4]
    dve.wait_ge(s.codes_1, 1)
    dve.scalar_tensor_tensor(m.rest_of_codes[:, :], codes, 2.0, m.codes_a, ALU.mult, ALU.subtract)\
        .then_inc(s.codes_rest, 1)
    dve.wait_ge(s.ld_first, 16 * FIRST_LOADS)
    dve.wait_ge(s.codes_n, 1)
    dve.tensor_copy(m.norms, m.ps[0:3, 2:4, :].rearrange("c a k -> c (a k)"))
    o.then(dve.tensor_scalar(neg, m.partsel[:, 0:2], -1.0, None, ALU.mult))
    for k in range(2):
        o.then(dve.tensor_copy(m.norm_parts[:, :], m.norms))
        o.then(dve.scalar_tensor_tensor(m.norms, m.norm_parts[:, :], neg[:, k:k + 1], m.norms, ALU.mult, ALU.add))
    dve.tensor_copy(m.norm_parts[:, :], m.norms)
    dve.wait_ge(s.codes_2, 1)
    dve.tensor_tensor(m.codes_c[0:C, :], m.rest_of_codes[0:C, :], m.codes_b[0:C, :], ALU.subtract)\
        .then_inc(s.codes_ready, 1)


def c0_xload(pe, m, s, g):
    pe.wait_ge(s.c0_in, (g + 1) * 16)
    for i in range(2):
        ins = pe.transpose(m.ps[:, 4, i * P:(i + 1) * P], m.xload[:, i * P:(i + 1) * P], m.ident[:])
    ins.then_inc(s.c0_xt, 1)


def c0_normt(pe, m, s, g):
    wait_apart(pe, m, s.c0_xn, g + 1)
    for j in range(PT):
        ins = pe.transpose(m.ps[0:C, 5, j * P:(j + 1) * P], m.xn[:, j, :], m.ident[:])
    ins.then_inc(s.c0_nt, 1)


def c0_project(pe, m, s, g):
    pe.wait_ge(s.c0_xf, g + 1)
    pe.matmul(m.ps[:, 4, :], m.proj0[:, :], m.xf[:, :], start=True, stop=True).then_inc(s.c0_zp, 1)


def c0_scores(pe, m, s, g, j, b):
    if j == 0:
        pe.wait_ge(s.c0_z, g + 1)
    pe.wait_ge(s.c0_read, g * PT + j + 1)
    at = slice(b * 512 + j * P, b * 512 + (j + 1) * P)
    za, zb = m.xa[:, at], m.xb[:, at]
    passes = ((m.ones3[:, :], m.norm_parts), (za, m.codes_a), (za, m.codes_b), (zb, m.codes_c))
    for n, (z, codes) in enumerate(passes):
        for k in range(2):
            ins = pe.matmul(m.ps[:, 2 * (j % 2) + k, :], z, codes[:, k * 512:(k + 1) * 512],
                            start=(n == 0), stop=(n == len(passes) - 1))
    ins.then_inc(s.c0_scored, 1)


def c0_pe(pe, nc, m, s):
    pe.wait_ge(s.ld_ident, 16)
    c0_xload(pe, m, s, 0)
    c0_pe_first(pe, nc, m, s)
    c0_normt(pe, m, s, 0)
    c0_project(pe, m, s, 0)
    pe.wait_ge(s.c0_rest, 1)
    c0_xload(pe, m, s, 1)
    pe.wait_ge(s.codes_ready, 1)

    def turn(g, b, ahead=2):
        c0_scores(pe, m, s, g, 0, b)
        if ahead > 0:
            c0_normt(pe, m, s, g + 1)
        c0_scores(pe, m, s, g, 1, b)
        if ahead > 0:
            c0_project(pe, m, s, g + 1)
        c0_scores(pe, m, s, g, 2, b)
        if ahead > 1:
            pe.wait_ge(s.c0_rest, g + 2)
            c0_xload(pe, m, s, g + 2)
        c0_scores(pe, m, s, g, 3, b)

    turn(0, 0)
    with pe.Fori(0, PAIRS // 2 - 2) as i:
        turn(2 * i + 1, 1)
        turn(2 * i + 2, 0)
    turn(PAIRS - 3, 1)
    turn(PAIRS - 2, 0, 1)
    turn(PAIRS - 1, 1, 0)


def c0_act(act, nc, m, s):
    def features(g, first=False):
        act.wait_ge(s.c0_nt, g + 1)
        if not first:
            act.wait_ge(s.c0_zp, g)
        act.activation(m.xf[0:C, :], m.ps[0:C, 5, :], ACT.Copy).then_inc(s.c0_xf, 1)

    def split(g, b, meanwhile=None):
        cols = slice(b * 512, b * 512 + 512)
        act.wait_ge(s.c0_zp, g + 1)
        act.activation(m.xa[:, cols], m.ps[:, 4, :], ACT.Copy).then_inc(s.c0_z1, 1)
        if meanwhile:
            meanwhile()
        act.wait_ge(s.c0_rest, g + 1)
        act.activation(m.xb[0:C, cols], m.xa[0:C, cols], ACT.Copy).then_inc(s.c0_z1, 1)
        act.activation(m.xb[C:P, cols], m.z_rest[C:P, :], ACT.Copy)
        act.wait_ge(s.c0_z1, 2 * g + 2)
        act.activation(m.xa[0:C, cols], m.z_rest[0:C, :], ACT.Copy).then_inc(s.c0_z2, 1)

    def turn(g, b, first=False):
        cols = bass.ds(g * WCHUNK, WCHUNK)
        features(g + 1)
        if not first:
            act.wait_ge(s.c0_scored, g * PT)
        split(g + 1, 1 - b, lambda: act.activation(m.w1[:, cols], m.wall[:, cols], ACT.Copy).then_inc(s.split_a, 1))
        act.activation(m.w3[C:P, cols], m.wall[C:P, cols], ACT.Copy)
        act.wait_ge(s.split_r, g + 1)
        act.activation(m.w2[:, cols], m.wrest[:, :], ACT.Copy).then_inc(s.split_b, 1)

    act.wait_ge(s.ones_rows, 1)
    c0_act_first(act, nc, m, s)
    features(0, True)
    split(0, 0)
    act.wait_ge(s.ld_up, 16 * UP_LOADS)
    turn(0, 0, True)
    with act.Fori(0, PAIRS // 2 - 1) as i:
        turn(2 * i + 1, 1)
        turn(2 * i + 2, 0)


def c0_dve_arrive(dve, o, m, s, g, first):
    x = m.X[:, bass.ds(g * PT, PT), :]
    dve.wait_ge(s.c0_xt, g + 1)
    o.then_apart(dve.tensor_copy(x.rearrange("p (a i) c -> p i a c", i=2),
                                 m.ps[:, 4, 0:2 * P].rearrange("p (i a c) -> p i a c", i=2, a=2)), m)
    ln_stats(dve, o, m, x, PT, s.c0_mv)


def c0_dve_norm(dve, o, m, s, g, first):
    x = m.X[:, bass.ds(g * PT, PT), :]
    dve.wait_ge(s.c0_rstd, g + 1)
    if not first:
        dve.wait_ge(s.c0_nt, g)
    ln_apply(dve, o, m, x, PT, s.c0_xn)


def c0_dve(dve, nc, m, s):
    o = m.dve_order
    dve.memset(m.minus_half[:, :], -0.5)
    dve.memset(m.minus_one[:, :], -1.0)
    dve.memset(m.wall[:, WCOLS:WPAD + 8], 0.0)
    dve.memset(m.ones3[:, :], 1.0)
    dve.memset(m.xf[C:C + 1, :], 1.0).then_inc(s.ones_rows, 1)
    dve.memset(m.one[:, :], 1.0)
    dve.memset(m.nat[:, 1:6, :], 0.0)
    dve.memset(m.maxp[:, :, :], 0.0)
    dve.memset(m.maxes[:, :, :, :], 0.0)
    dve.memset(m.down[1][0:C, :, 1, :], 0.0)
    dve.memset(m.down[1][C:P, :, 0, :], 0.0)
    dve.memset(m.qs[0:C, LOW:, :], 0.0)
    dve.memset(m.vals[:, :, :, HD:HD + 1], 1.0)
    dve.memset(m.xfp[C:C + 1, :], 1.0)
    dve.memset(m.ot1[C:C + 1, :], 1.0)
    o.then(dve.memset(m.maxparts[:, :, :, :], 0.0))
    dve.memset(m.maxrest[:, :, :], 0.0).then_inc(s.padded, 1)
    dve.sem_inc(s.c0_read, 2)
    c0_dve_arrive(dve, o, m, s, 0, True)
    c0_dve_norm(dve, o, m, s, 0, True)
    c0_dve_first(dve, nc, m, s, o)

    def rest(g, b):
        dve.wait_ge(s.c0_z1, 2 * g + 1)
        dve.tensor_tensor(m.z_rest, m.ps[:, 4, :], m.xa[:, b * 512:b * 512 + 512], ALU.subtract).then_inc(s.c0_rest, 1)

    def third(g, b):
        dve.wait_ge(s.c0_z2, g + 1)
        z3 = m.xb[C:P, b * 512:b * 512 + 512]
        dve.tensor_tensor(z3, m.z_rest[C:P, :], z3, ALU.subtract).then_inc(s.c0_z, 1)

    rest(0, 0)
    third(0, 0)
    c0_dve_arrive(dve, o, m, s, 1, False)

    def argmax(g, j, first=False):
        wait_apart(dve, m, s.c0_scored, g * PT + j + 1)
        sc = m.ps[:, 2 * (j % 2):2 * (j % 2) + 2, :].rearrange("p a k -> p (a k)")
        n = o.step(dve.max(m.best[:, j, :], sc))
        dve.wait_ge(s.dve_order, n)
        if not first:
            wait_apart(dve, m, s.c0_gathered[j], g * 16)
        dve.max_index(m.code[:, j, :], m.best[:, j, :], sc).then_inc(s.c0_read, 1)

    def turn(g, b, first=False, last=False):
        c0_dve_norm(dve, o, m, s, g + 1, False)
        argmax(g, 0, first)
        argmax(g, 1, first)
        rest(g + 1, 1 - b)
        argmax(g, 2, first)
        if not last:
            c0_dve_arrive(dve, o, m, s, g + 2, False)
        third(g + 1, 1 - b)
        argmax(g, 3, first)

    turn(0, 0, True)
    with o.turns(PAIRS // 2 - 2, 2 * C0_STEPS) as i:
        turn(2 * i + 1, 1)
        turn(2 * i + 2, 0)
    turn(PAIRS - 3, 1)
    turn(PAIRS - 2, 0, last=True)
    for j in range(PT):
        argmax(PAIRS - 1, j)


C0_STEPS = 7


def c0_pool(pool, nc, m, s, d):
    o = m.pool_order
    pool.wait_ge(s.ones_rows, 1)
    wait_apart(pool, m, s.c0_mv, 1)
    ln_rstd(pool, o, m, PT, 1e-6, s.c0_rstd)

    def gather(g, j):
        wait_apart(pool, m, s.c0_read, 2 + g * PT + j + 1)
        pool.indirect_dma_start(m.zq[j][:, :], None, d.L0_conv_emb,
                                bass.IndirectOffsetOnAxis(ap=m.code[:, j, 0:1], axis=0))\
            .then_inc(s.c0_gathered[j], 16)

    def add(g):
        for j in range(PT):
            wait_apart(pool, m, s.c0_gathered[j], g * 16 + 16)
            x = m.X[:, bass.ds(g * PT + j, 1), :].rearrange("p a c -> p (a c)")
            ins = pool.tensor_tensor(x, x, m.zq[j][:, :], ALU.add)
        o.then(ins)

    def turn(g, first=False, last=False):
        cols = bass.ds(g * WCHUNK, WCHUNK)
        if not first:
            add(g - 1)
        gather(g, 0)
        pool.wait_ge(s.split_a, g + 1)
        pool.tensor_tensor(m.wrest[:, :], m.wall[:, cols], m.w1[:, cols], ALU.subtract).then_inc(s.split_r, 1)
        gather(g, 1)
        gather(g, 2)
        if not last:
            wait_apart(pool, m, s.c0_mv, g + 3)
            ln_rstd(pool, o, m, PT, 1e-6, s.c0_rstd)
        gather(g, 3)
        pool.wait_ge(s.split_b, g + 1)
        o.then(pool.tensor_tensor(m.w3[0:C, cols], m.wrest[0:C, :], m.w2[0:C, cols], ALU.subtract))

    wait_apart(pool, m, s.c0_mv, 2)
    ln_rstd(pool, o, m, PT, 1e-6, s.c0_rstd)
    turn(0, True)
    with o.turns(PAIRS - 3, 3) as g:
        turn(g + 1)
    turn(PAIRS - 2, last=True)
    add(PAIRS - 2)
    for j in range(PT):
        gather(PAIRS - 1, j)
    add(PAIRS - 1)



def ffn_counts(l):
    f = FFN[l]
    per = P // f["H"]
    G = f["E"] // per
    return f["E"], G, per, 2 * G


AHEAD = {4: ((0, 1, 2, 2), (2, 3), 3), 8: ((1, 2, 3, 4), (3, 4), 5), 16: ((3, 4, 6, 8), (5, 7), 10)}


def ffn_pe(pe, nc, m, s, l):
    f, w, q = FFN[l], WHERE[l], s.ffn[l]
    E, G, per, U = ffn_counts(l)
    free = 2 if f["gated"] else 4

    def transposes(sb):
        pe.wait_ge(q.parts, sb + 1)
        pe.wait_ge(q.logits_read, sb + 1)
        t6 = m.ps[:, 6, :].bitcast(BF16)
        t7 = m.ps[:, 7, :].bitcast(BF16)
        for t in range(ST):
            pe.transpose(t6[:, t * P:(t + 1) * P], m.parts[:, t, 0:2, :], m.identb[:])
            ins = pe.transpose(t7[:, t * P:(t + 1) * P], m.parts[:, t, 1:3, :], m.identb[:])
        ins.then_inc(q.transposed, 1)

    def three(out, lhs, rhs, stop=True):
        for k, (a, b) in enumerate(zip(lhs, rhs)):
            ins = pe.matmul(out, a, b, start=(k == 0), stop=(k == 2 and stop))
        return ins

    def logits(sb):
        pe.wait_ge(q.xa, sb + 1)
        pe.wait_ge(q.xb, sb + 1)
        gate = slice(w["gate"], w["gate"] + E)
        for t in range(ST):
            a, b = m.xa[:, t * P:(t + 1) * P], m.xb[:, t * P:(t + 1) * P]
            ins = three(m.ps[:, 6, t * E:(t + 1) * E], (a, a, b), (m.w1[:, gate], m.w2[:, gate], m.w3[:, gate]))
        ins.then_inc(q.logits, 1)

    def hidden(sb, u):
        pe.wait_ge(q.act, sb * U + u + 1)
        g, half = u // 2, u % 2
        a, b = (x[:, half * HALF:(half + 1) * HALF] for x in (m.xa, m.xb))
        outs = ((w["up"], u % 4),) if not f["gated"] else ((w["up"], 2 * (u % 2)), (w["up2"], 2 * (u % 2) + 1))
        for at, bank in outs:
            cols = slice(at + g * P, at + (g + 1) * P)
            ins = three(m.ps[:, bank, :], (m.w1[:, cols], m.w2[:, cols], m.w3[:, cols]), (a, a, b))
        ins.then_inc(q.hidden, 1)

    def down(sb, e):
        g, i = e // per, e % per
        pe.wait_ge(q.weighed, sb * E + e + 1)
        bank = 4 + e % 2
        if per == 2:
            pe.wait_ge(q.act, free + sb * U + 2 * g + 1 + i)
            b2 = m.b2p[:, E2[l] + 2 * g:E2[l] + 2 * g + 2, :].rearrange("k e c -> k (e c)")
            pe.matmul(m.ps[:, bank, :], m.ones3[:, :], bcast(b2.unsqueeze(1), [3, ST // 2, 2 * C]), start=True, stop=True)
            for t in range(ST // 2):
                at = (i * ST // 2 + t) * P
                ins = pe.matmul(m.ps[:, bank, t * 2 * C:(t + 1) * 2 * C], m.hid[:, g % 2, at:at + P],
                                m.down[l][:, g, :, :].rearrange("p e c -> p (e c)"), start=False, stop=True,
                                skip_group_check=True)
            ins.then_inc(q.down, 1)
            return
        pe.wait_ge(q.act, free + sb * U + 2 * g + 2)
        if f["b2"]:
            pe.matmul(m.ps[:, bank, :], m.ones3[:, :], bcast(m.b2p[:, E2[l] + e, :].unsqueeze(1), [3, ST, C]),
                      start=True, stop=True)
        for t in range(ST):
            ins = pe.matmul(m.ps[:, bank, t * C:(t + 1) * C], m.hid[:, g % 2, t * P:(t + 1) * P],
                            m.down[l][:, g, :], start=not f["b2"], stop=True, skip_group_check=f["b2"])
        ins.then_inc(q.down, 1)

    def turn(sb, ahead):
        for u in range(U):
            hidden(sb, u)
            g = u // 2
            if u % 2 and g > 0:
                for i in range(per):
                    down(sb, (g - 1) * per + i)
            if u % 2 and g == AHEAD[G][2] and ahead:
                transposes(sb + 1)
        for i in range(per):
            down(sb, (G - 1) * per + i)
        if ahead:
            logits(sb + 1)

    transposes(0)
    logits(0)
    if f["b2"]:
        pe.wait_ge(s.b2_split, 1 + (0, 1, None, 2)[l])
    with pe.Fori(0, SUPERS - 1) as sb:
        turn(sb, True)
    turn(SUPERS - 1, False)


def ffn_act(act, nc, m, s, l):
    f, q = FFN[l], s.ffn[l]
    E, G, per, U = ffn_counts(l)

    def part(sb, k, first):
        if k == 0:
            act.wait_ge(q.xn, sb + 1)
            if not first:
                act.wait_ge(q.transposed, sb)
            act.activation(m.parts[:, :, 1, :], m.xn[:, :, :], ACT.Copy).then_inc(q.part1, 1)
        else:
            act.wait_ge(q.rest, sb + 1)
            act.activation(m.parts[:, :, 0, :], m.xc[:, :, :], ACT.Copy).then_inc(q.part2, 1)

    def evacuate(sb, first):
        act.wait_ge(q.transposed, sb + 1)
        if not first:
            act.wait_ge(q.hidden, sb * U)
        act.activation(m.xb[:, :], m.ps[:, 7, :].bitcast(BF16), ACT.Copy).then_inc(q.xb, 1)

    def exps(sb):
        act.wait_ge(q.below_max, sb + 1)
        act.activation(m.ex[:, 0:ST, 0:E + 1], m.below[:, 0:ST, 0:E + 1], ACT.Exp).then_inc(q.exps, 1)

    def unit(sb, u):
        g, half = u // 2, u % 2
        act.wait_ge(q.hidden, sb * U + u + 1)
        if half == 0:
            act.wait_ge(q.down, sb * E + (g + 1) * per)
        out = m.hid[:, g % 2, half * HALF:(half + 1) * HALF]
        if f["gated"]:
            act.wait_ge(q.act, sb * U + u + 1)
            act.activation(m.silu[:, half, :], m.ps[:, 2 * half, :], ACT.Silu).then_inc(q.silu, 1)
        else:
            bias = m.b1t[:, E1[l] + g:E1[l] + g + 1]
            act.activation(out, m.ps[:, u % 4, :], ACT.Gelu, bias=bias).then_inc(q.act, 1)

    def turn(sb, ahead):
        for g in range(G):
            unit(sb, 2 * g)
            unit(sb, 2 * g + 1)
            if g == 0:
                exps(sb)
            for k in range(2):
                if ahead and g == AHEAD[G][1][k]:
                    part(sb + 1, k, False)
        if ahead:
            evacuate(sb + 1, False)

    part(0, 0, True)
    part(0, 1, True)
    evacuate(0, True)
    with act.Fori(0, SUPERS - 1) as sb:
        turn(sb, True)
    turn(SUPERS - 1, False)


def ffn_dve(dve, nc, m, s, l):
    f, q = FFN[l], s.ffn[l]
    E, G, per, U = ffn_counts(l)
    o = Order(dve, q.order)
    dve.sem_inc(q.weighed, 2)
    dve.sem_inc(q.logits_read, 1)

    def stats(sb):
        ln_stats(dve, o, m, m.X[:, bass.ds(sb * ST, ST), :], ST, q.mv)

    def norm(sb):
        dve.wait_ge(q.rstd, sb + 1)
        x = m.X[:, bass.ds(sb * ST, ST), :]
        ln_apply(dve, o, m, x, ST, q.xn)
        if f["keep"]:
            dve.wait_ge(q.xn, sb + 1)
            o.then(dve.tensor_tensor(x, x, m.xn[:, :, :], ALU.add))

    def rest(sb):
        dve.wait_ge(q.part1, sb + 1)
        dve.tensor_tensor(m.xc[:, :, :], m.xn[:, :, :], m.parts[:, :, 1, :], ALU.subtract).then_inc(q.rest, 1)

    def third(sb):
        dve.wait_ge(q.part2, sb + 1)
        dve.tensor_tensor(m.parts[:, :, 2, :], m.xc[:, :, :], m.parts[:, :, 0, :], ALU.subtract)\
            .then_inc(q.parts, 1)

    def evacuate(sb, first):
        dve.wait_ge(q.transposed, sb + 1)
        if not first:
            dve.wait_ge(q.hidden, sb * U)
        dve.tensor_copy(m.xa[:, :], m.ps[:, 6, :].bitcast(BF16)).then_inc(q.xa, 1)

    def router(sb):
        dve.wait_ge(q.logits, sb + 1)
        lg = m.lg[:, :, 0:E]
        raw = m.ps[:, 6, 0:ST * E].rearrange("p (t e) -> p t e", e=E)
        if f["gate_b"]:
            ins = dve.tensor_tensor(lg, raw, bcast(m.gate_b[l][:, :].unsqueeze(1), [P, ST, E]), ALU.add)
        else:
            ins = dve.tensor_copy(lg, raw)
        ins.then_inc(q.logits_read, 1)
        wait_apart(dve, m, q.logits_read, sb + 2)
        for t in range(ST):
            ins = dve.max(m.top[:, t, :], m.lg[:, t, 0:E])
        o.then(ins)
        dve.tensor_tensor(m.below[:, :, 0:E], lg, bcast(m.top[:, :, 0:1], [P, ST, E]), ALU.subtract)
        dve.tensor_tensor(m.below[:, :, E], m.top[:, :, 1], m.top[:, :, 0], ALU.subtract).then_inc(q.below_max, 1)
        for t in range(ST):
            ins = dve.max_index(m.topi[:, t, :], m.top[:, t, :], m.lg[:, t, 0:E])
        o.then(ins)
        o.then(dve.tensor_copy(m.topf[:, :, :], m.topi[:, :, 0:2]))

    def combine(sb):
        shape = [P, ST, E]
        for k in range(2):
            ins = dve.tensor_tensor(m.hit[:, k, :, 0:E], bcast(m.iota[:, 0:E].unsqueeze(1), shape),
                                    bcast(m.topf[:, :, k:k + 1], shape), ALU.is_equal)
        o.step(ins)
        dve.wait_ge(q.exps, sb + 1)
        o.then(dve.tensor_reduce(m.sums[:, :], m.ex[:, :, 0:E], AX, ALU.add))
        o.then(dve.reciprocal(m.prob[:, 0, :], m.sums[:, :]))
        o.then(dve.tensor_tensor(m.prob[:, 1, :], m.ex[:, :, E], m.prob[:, 0, :], ALU.mult))
        if f["renorm"]:
            o.then(dve.tensor_tensor(m.sums[:, :], m.prob[:, 0, :], m.prob[:, 1, :], ALU.add))
            if f["floor"] is not None:
                o.then(dve.tensor_scalar(m.sums[:, :], m.sums[:, :], f["floor"], None, ALU.max))
            o.then(dve.reciprocal(m.rsum[:, :], m.sums[:, :]))
            o.then(dve.tensor_tensor(m.prob[:, :, :], m.prob[:, :, :], bcast(m.rsum[:, :].unsqueeze(1), [P, 2, ST]),
                                     ALU.mult))
        for k in range(2):
            ins = dve.tensor_tensor(m.hit[:, k, :, 0:E], m.hit[:, k, :, 0:E],
                                    bcast(m.prob[:, k, :].unsqueeze(2), shape), ALU.mult)
        o.then(ins)
        o.then(dve.tensor_tensor(m.cw[:, :, 0:E], m.hit[:, 0, :, 0:E], m.hit[:, 1, :, 0:E], ALU.add))

    def gate(sb, u):
        g, half = u // 2, u % 2
        dve.wait_ge(q.silu, sb * U + u + 1)
        if half == 0:
            dve.wait_ge(q.down, sb * E + (g + 1) * per)
        dve.tensor_tensor(m.hid[:, g % 2, half * HALF:(half + 1) * HALF], m.silu[:, half, :],
                          m.ps[:, 2 * half + 1, :], ALU.mult).then_inc(q.act, 1)

    def weigh(sb, e):
        dve.wait_ge(q.down, 2 * per + sb * E + e + 1)
        dve.wait_ge(q.added, sb * E + e + 1)
        if per == 2:
            g, i = e // 2, e % 2
            out = m.prod[:, e % 2, :, :].rearrange("p (t j) c -> p t j c", j=2)
            cw = m.cw[:, i * ST // 2:(i + 1) * ST // 2, 2 * g:2 * g + 2]
            o.then(dve.tensor_tensor(out, m.ps[:, 4 + e % 2, :].rearrange("p (t j c) -> p t j c", j=2, c=C),
                                     bcast(cw.unsqueeze(3), [P, ST // 2, 2, C]), ALU.mult))
            dve.tensor_tensor(out[:, :, 0, :], out[:, :, 0, :], out[:, :, 1, :], ALU.add).then_inc(q.weighed, 1)
            return
        dve.tensor_tensor(m.prod[:, e % 2, :, :], m.ps[:, 4 + e % 2, :].rearrange("p (t c) -> p t c", c=C),
                          bcast(m.cw[:, :, e:e + 1], [P, ST, C]), ALU.mult).then_inc(q.weighed, 1)

    def turn(sb, ahead):
        if not f["gated"]:
            router(sb)
            combine(sb)
        steps = (stats, norm, rest, third)
        for g in range(G):
            if f["gated"]:
                gate(sb, 2 * g)
                gate(sb, 2 * g + 1)
                if g == 0:
                    router(sb)
                if g == 1:
                    combine(sb)
            if g > 0:
                for i in range(per):
                    weigh(sb, (g - 1) * per + i)
            for step, at in zip(steps, AHEAD[G][0]):
                if ahead and g == at:
                    step(sb + 1)
        for i in range(per):
            weigh(sb, (G - 1) * per + i)
        if ahead:
            evacuate(sb + 1, False)

    stats(0)
    norm(0)
    rest(0)
    third(0)
    evacuate(0, True)
    if f["b2"]:
        split_b2(dve, m, s, o, l)
    with o.turns(SUPERS - 1, FFN_STEPS[l]) as sb:
        turn(sb, True)
    turn(SUPERS - 1, False)


FFN_STEPS = [11, 24, 14, 11]


def ffn_pool(pool, nc, m, s, l):
    f, q = FFN[l], s.ffn[l]
    E, G, per, U = ffn_counts(l)
    o = Order(pool, q.pool_order)
    free = 2 if f["gated"] else 4
    pool.sem_inc(q.added, 2)
    pool.sem_inc(q.act, free)
    pool.sem_inc(q.down, 2 * per)

    def add(sb, e):
        x = m.X[:, bass.ds(sb * ST, ST), :]
        y = m.prod[:, e % 2, :, :]
        if per == 2:
            x = m.X[:, bass.ds(sb * ST + e % 2 * (ST // 2), ST // 2), :]
            y = y.rearrange("p (t j) c -> p t j c", j=2)[:, :, 0, :]
        pool.wait_ge(q.weighed, 2 + sb * E + e + 1)
        wait_apart(pool, m, q.added, 2 + sb * E + e)
        pool.tensor_tensor(x, x, y, ALU.add).then_inc(q.added, 1)

    def rstd(sb):
        wait_apart(pool, m, q.mv, sb + 1)
        ln_rstd(pool, o, m, ST, 1e-5, q.rstd)

    rstd(0)
    if l == 0:
        make_sel(pool, m, s)
    with o.turns(SUPERS - 1, 1) as sb:
        for e in range(E):
            if e == AHEAD[G][0][0] * per:
                rstd(sb + 1)
            add(sb, e)
    for e in range(E):
        add(SUPERS - 1, e)



BANKS3 = 4 * 160 + 256 + 3 * 128
Q_PARTS = (0, 0, 0, 1, 1, 2)
K_PARTS = (0, 1, 2, 0, 1, 0)
SPLIT_ROWS = 6 * HD
BLOCKS = 5
SHARES = (0, 4, 8, 12, 14, 16)
LOW = 3


def row_parity(ap):
    return ap.rearrange("p (im a py x) -> p im py a x", im=2, py=2, x=SIDE)


def by_parity(ap):
    return ap.rearrange("p (im py a x) -> p im py a x", im=2, py=2, x=SIDE)


HEAD = [(0, 0, 0, 0, "near"), (0, 1, 0, 160, "near"), (0, 2, 0, 320, "near"), (1, 0, 1, 0, "near"),
        (1, 1, 1, 160, "all"), (1, 2, 2, 0, "rows"), (1, 3, 2, 128, "rows"), (1, 4, 2, 256, "rows")]
BANK_COLS = (480, 416, 384)
BANK_AT = (0, 480, 896)


def make_sel(pool, m, s):
    o = m.pool_order
    o.then(pool.memset(m.sel, 0.0))
    for side, parts in enumerate((Q_PARTS, K_PARTS)):
        for k, part in enumerate(parts):
            for half, first, n in ((0, 0, LOW), (1, LOW, HEADS - LOW)):
                src = m.ident[:, side * C + first * HD:side * C + (first + n) * HD]
                ins = pool.tensor_copy(m.sel[:, side, part, 0:n, half * C + k * HD:half * C + (k + 1) * HD],
                                       src.rearrange("p (n d) -> p n d", d=HD))
    o.step(ins)


def c1_pe(pe, nc, m, s):
    pe.sem_inc(s.c1_o, 2)

    def tokens(p):
        pe.wait_ge(s.c1_xn, p + 1)
        wait_apart(pe, m, s.c1_max, 4 * p + 1)
        for t in range(PT):
            ins = pe.transpose(m.ps[0:C, 0, t * P:(t + 1) * P], m.xn[:, t, :], m.ident[:])
        ins.then_inc(s.c1_nt, 1)

    def queries_keys(p):
        pe.wait_ge(s.c1_xf, p + 1)
        pe.matmul(m.ps[:, 1, :], m.wqk[:, :], m.xf[:, :], start=True, stop=True).then_inc(s.c1_qk, 1)

    def values_of_tokens(p):
        for t in range(PT):
            cols = slice(t * P, (t + 1) * P)
            for x, a, b in ((m.xf, 0, 40), (m.xfp, 40, 64)):
                ins = pe.matmul(m.ps[:, 0, t * C + a:t * C + b], x[:, cols], m.wv[:, a:b], start=True, stop=True)
        ins.then_inc(s.c1_v, 1)

    def spread(p, behind=False):
        pe.wait_ge(s.c1_part3, p + 1)
        for b in range(BLOCKS):
            for side, (read, done) in enumerate(((s.c1_qs, s.c1_selq), (s.c1_ks, s.c1_selk))):
                pe.wait_ge(read, BLOCKS * p + b + 1)
                out = m.ps[:, 1 + side, :]
                if b < 2:
                    for k in range(3):
                        ins = pe.matmul(out, m.sel[:, side, k, b, :], m.qkp[:, k, :], start=(k == 0), stop=(k == 2))
                if b == 2:
                    for k in range(3):
                        pe.matmul(out[0:C, :], m.sel[:, side, k, b, 0:C], m.qkp[:, k, :],
                                  start=(k == 0), stop=(k == 2))
                for im in range(2 if b >= 2 else 0):
                    for k in range(3):
                        ins = pe.matmul(out[C:P, im * PLACES:(im + 1) * PLACES], m.sel[:, side, k, b, C:P],
                                        row_parity(m.qkp[:, k, :])[:, im], start=(k == 0), stop=(k == 2))
                ins.then_inc(done, 1)
            if behind:
                weigh(p - 1, 1, SHARES[b], SHARES[b + 1])

    def logits(first_bank, stationary, moving, rows, i, *operands):
        for b, (n, at) in enumerate(zip(BANK_COLS, (None, MASK_AT["near"], MASK_AT["rows"]))):
            mask = m.mask[:, i * MASK_TILE:(i + 1) * MASK_TILE]
            if b == 1:
                rhs = mask[:, 0:416]
            else:
                kind, w = (("near", 160), None, ("rows", 128))[b]
                rhs = bcast(mask[:, MASK_AT[kind]:MASK_AT[kind] + w].unsqueeze(1), [P, 3, w])
            pe.matmul(m.ps[:, first_bank + b, 0:n], m.identb[:, :], rhs, start=True, stop=True)
        for sem, value in operands:
            pe.wait_ge(sem, value)
        for half, block, b, col, kind in HEAD:
            r = slice(C * half, C * half + rows)
            w = WIDTH[kind]
            lo = dict(near=i * (PLACES - 160), rows=i * P, all=0)[kind]
            ins = pe.matmul(m.ps[:, first_bank + b, col:col + w],
                            stationary(r, block, slice(i * P, (i + 1) * P)), moving(r, block, slice(lo, lo + w)),
                            start=False, stop=True, skip_group_check=True)
        return ins

    def of_image(x, im):
        return lambda r, b, c: x[r, b, im * PLACES + c.start:im * PLACES + c.stop]

    def by_query(p, n):
        if n == 0:
            pe.wait_ge(s.c1_v_read, p + 1)
            pe.wait_ge(s.c1_qs, BLOCKS * p + BLOCKS + 1)
            pe.wait_ge(s.c1_ks, BLOCKS * p + BLOCKS + 1)
        pe.wait_ge(s.c1_max, 4 * p + n + 1)
        logits(0, of_image(m.qs, n // 2), of_image(m.ks, n // 2), SPLIT_ROWS, n % 2).then_inc(s.c1_s, 1)

    def max_rows(p, im):
        pe.wait_ge(s.c1_m, 2 * p + im + 1)
        if im == 0:
            pe.wait_ge(s.c1_ot_read, p + 1)
            pe.wait_ge(s.c1_added, p + 1)
        else:
            pe.wait_ge(s.c1_q2, 2 * p + 1)
        for i in range(2):
            for b in range(BLOCKS):
                ins = pe.transpose(m.ps[:, 6 + i, :].bitcast(BF16)[:, b * P:(b + 1) * P],
                                   m.maxes[:, 2 * im + i, b, :], m.identb[:])
        ins.then_inc(s.c1_mt, 1)

    def by_key(p, n):
        im = n // 2
        pe.wait_ge(s.c1_p, 4 * p + n + 1)
        logits(3, of_image(m.ks, im), lambda r, b, c: m.q2[r, b, c], SPLIT_ROWS + 3, n % 2,
               (s.c1_q2, 2 * p + im + 1)).then_inc(s.c1_st, 1)

    def weigh(p, im, first=0, end=2 * HEADS):
        if first == end:
            return
        if first == 0:
            pe.wait_ge(s.c1_p, 4 * p + 2 * im + 3)
            pe.wait_ge(s.c1_on, 2 * p + im + 1)
        if im == 0:
            pe.wait_ge(s.c1_vals, p + 2)
            pe.wait_ge(s.c1_q2, 2 * p + 2)
        for i, h in [divmod(n, HEADS) for n in range(first, end)]:
            _, _, b, col, kind = HEAD[h]
            col += BANK_AT[b]
            out = m.ps[:, 7, (i * HEADS + h) * 9:(i * HEADS + h + 1) * 9]
            v = lambda k: m.vals[:, 2 * im + k, h, :]
            pt = lambda k, a, b_: m.pt[:, 2 * im + k, col + a:col + b_]
            if kind == "near":
                own = pt(i, 0, 128) if i == 0 else pt(i, 32, 160)
                pe.matmul(out, own, v(i), start=True, stop=True)
                if i == 0:
                    ins = pe.matmul(out[96:128, :], pt(1, 0, 32), v(1), start=False, stop=True, skip_group_check=True)
                else:
                    ins = pe.matmul(out[0:32, :], pt(0, 128, 160), v(0), start=False, stop=True, skip_group_check=True)
            elif kind == "rows":
                ins = pe.matmul(out, pt(i, 0, 128), v(i), start=True, stop=True)
            else:
                for k in range(2):
                    ins = pe.matmul(out, pt(k, i * P, (i + 1) * P), v(k), start=(k == 0), stop=(k == 1))
        if end == 2 * HEADS:
            ins.then_inc(s.c1_o, 1)

    def outputs_t(p):
        wait_apart(pe, m, s.c1_on, 2 * p + 3)
        for t in range(PT):
            ins = pe.transpose(m.ps[0:C, 6, t * P:(t + 1) * P], m.att[:, t, :], m.ident[:])
        ins.then_inc(s.c1_ot, 1)

    def project(p):
        pe.wait_ge(s.c1_ot_read, p + 2)
        for t in range(PT):
            out = m.ps[:, 7, t * C:(t + 1) * C]
            pe.matmul(out, m.ot1[:, t * P:(t + 1) * P], m.wpn[:, :], start=True, stop=False)
            ins = pe.matmul(out, m.ot2[:, t * P:(t + 1) * P], m.wpp[:, :], start=False, stop=True)
        ins.then_inc(s.c1_y, 1)

    def turn(p, behind, ahead):
        by_query(p, 0)
        if behind:
            outputs_t(p - 1)
        by_query(p, 1)
        if behind:
            project(p - 1)
        by_query(p, 2)
        max_rows(p, 0)
        by_query(p, 3)
        by_key(p, 0)
        if ahead:
            tokens(p + 1)
        by_key(p, 1)
        max_rows(p, 1)
        if ahead:
            queries_keys(p + 1)
        weigh(p, 0)
        by_key(p, 2)
        if ahead:
            values_of_tokens(p + 1)
        by_key(p, 3)
        if ahead:
            spread(p + 1, True)

    tokens(0)
    queries_keys(0)
    values_of_tokens(0)
    spread(0)
    turn(0, False, True)
    with pe.Fori(1, PAIRS - 1) as p:
        turn(p, True, True)
    turn(PAIRS - 1, True, False)
    weigh(PAIRS - 1, 1)
    outputs_t(PAIRS - 1)
    project(PAIRS - 1)


def c1_act(act, nc, m, s):
    for sem in (s.c1_p, s.c1_ot_read, s.c1_ks):
        act.sem_inc(sem, 1)

    def exps(p, n):
        act.wait_ge(s.c1_st, 4 * p + n + 1)
        if n % 2 == 0:
            act.wait_ge(s.c1_o, 2 * p + 1 + n // 2)
        for b, (k, at) in enumerate(zip(BANK_COLS, BANK_AT)):
            ins = act.activation(m.pt[:, n, at:at + k], m.ps[:, 3 + b, 0:k], ACT.Exp)
        ins.then_inc(s.c1_p, 1)

    def emax(p, im):
        act.wait_ge(s.c1_m, 2 * p + im + 1)
        tiles = slice(2 * im, 2 * im + 2)
        act.activation(m.emax[:, tiles, :], m.maxp[:, tiles, :],
                       ACT.Exp, scale=-1.0).then_inc(s.c1_em, 1)

    def tokens(p):
        act.wait_ge(s.c1_nt, p + 1)
        act.activation(m.xf[0:C, :], m.ps[0:C, 0, :], ACT.Copy)
        for py in range(2):
            ins = act.activation(by_parity(m.xfp[0:C, :])[:, :, py], row_parity(m.ps[0:C, 0, :])[:, :, py], ACT.Copy)
        ins.then_inc(s.c1_xf, 1)

    def part1(p):
        act.wait_ge(s.c1_qk, p + 1)
        act.activation(m.qkp[:, 0, :], m.ps[:, 1, :], ACT.Copy).then_inc(s.c1_part1, 1)

    def part2(p):
        act.wait_ge(s.c1_rest, p + 1)
        act.activation(m.qkp[:, 1, :], m.qk_rest, ACT.Copy).then_inc(s.c1_part2, 1)

    def keys(p):
        for b in range(BLOCKS):
            act.wait_ge(s.c1_selk, BLOCKS * p + b + 1)
            r = slice(0 if b < LOW else C, P)
            act.activation(m.ks[r, b, :], m.ps[r, 2, :], ACT.Identity, bias=m.minus_rows[r, :]).then_inc(s.c1_ks, 1)

    def vals(p):
        act.wait_ge(s.c1_v, p + 1)
        act.wait_ge(s.c1_vals, p + 1)
        act.activation(m.vals_next[:, :, :], m.ps[:, 0, 0:PT * C].rearrange("p (t c) -> p t c", t=PT),
                       ACT.Copy).then_inc(s.c1_v_read, 1)

    def outputs(p):
        act.wait_ge(s.c1_ot, p + 1)
        for py in range(2):
            act.activation(row_parity(m.ot2[:, :])[:, :, py], by_parity(m.ps[0:C, 6, :])[:, :, py], ACT.Copy)
        act.activation(m.ot1[0:C, :], m.ps[0:C, 6, :], ACT.Copy).then_inc(s.c1_ot_read, 1)

    def turn(p, behind, ahead):
        if behind:
            outputs(p - 1)
        emax(p, 0)
        exps(p, 0)
        if ahead:
            tokens(p + 1)
        exps(p, 1)
        emax(p, 1)
        if ahead:
            part1(p + 1)
            part2(p + 1)
        exps(p, 2)
        if ahead:
            vals(p + 1)
        exps(p, 3)
        if ahead:
            keys(p + 1)

    tokens(0)
    part1(0)
    part2(0)
    vals(0)
    keys(0)
    turn(0, False, True)
    with act.Fori(1, PAIRS - 1) as p:
        turn(p, True, True)
    turn(PAIRS - 1, True, False)
    outputs(PAIRS - 1)


def c1_dve(dve, nc, m, s):
    o = m.dve_order
    for sem in (s.c1_max, s.c1_on, s.c1_added, s.c1_qs):
        dve.sem_inc(sem, 1)

    def stats(p):
        ln_stats(dve, o, m, m.X[:, bass.ds(p * PT, PT), :], PT, s.c1_mv)

    def norm(p, first=False):
        dve.wait_ge(s.c1_rstd, p + 1)
        if not first:
            dve.wait_ge(s.c1_nt, p)
        ln_apply(dve, o, m, m.X[:, bass.ds(p * PT, PT), :], PT, s.c1_xn)

    def rest(p):
        dve.wait_ge(s.c1_part1, p + 1)
        dve.tensor_tensor(m.qk_rest, m.ps[:, 1, :], m.qkp[:, 0, :], ALU.subtract).then_inc(s.c1_rest, 1)
        dve.wait_ge(s.c1_part2, p + 1)
        dve.tensor_tensor(m.qkp[:, 2, :], m.qk_rest, m.qkp[:, 1, :], ALU.subtract).then_inc(s.c1_part3, 1)

    def queries(p):
        for b in range(BLOCKS):
            dve.wait_ge(s.c1_selq, BLOCKS * p + b + 1)
            r = slice(0 if b < LOW else C, P)
            dve.tensor_copy(m.qs[r, b, :], m.ps[r, 1, :]).then_inc(s.c1_qs, 1)

    def maxima(p, n):
        dve.wait_ge(s.c1_s, 4 * p + n + 1)
        r = m.maxr[:, n, :]
        dve.tensor_reduce(r[:, 0:3], m.ps[:, 0, 0:480].rearrange("p (h k) -> p h k", h=3), AX, ALU.max)
        dve.tensor_reduce(r[:, 3:4], m.ps[:, 1, 0:160], AX, ALU.max)
        dve.tensor_reduce(r[:, 4:5], m.ps[:, 1, 160:416], AX, ALU.max)
        dve.tensor_reduce(r[:, 5:8], m.ps[:, 2, 0:384].rearrange("p (h k) -> p h k", h=3), AX, ALU.max)\
            .then_inc(s.c1_max, 1)

    def with_padding(p, im):
        t = slice(2 * im, 2 * im + 2)
        dve.wait_ge(s.c1_max, 4 * p + 2 * im + 3)
        pad = m.padmax[:, :].rearrange("p (t h) -> p t h", t=2)
        o.then(dve.tensor_tensor(m.maxp[:, t, :], m.maxr[:, t, :], pad, ALU.max))
        o.then(dve.tensor_copy(m.maxparts[:, :, :, 0], m.maxp[:, t, :]))
        o.then(dve.tensor_tensor(m.maxrest[:, :, :], m.maxp[:, t, :], m.maxparts[:, :, :, 0], ALU.subtract))
        o.then(dve.tensor_copy(m.maxparts[:, :, :, 1], m.maxrest[:, :, :]))
        o.then(dve.tensor_tensor(m.maxparts[:, :, :, 2], m.maxrest[:, :, :], m.maxparts[:, :, :, 1], ALU.subtract))
        for half, first, n in ((0, 0, LOW), (1, LOW, HEADS - LOW)):
            at = half * C + SPLIT_ROWS
            ins = dve.tensor_copy(m.maxes[:, t, 0:n, at:at + 3], m.maxparts[:, :, first:first + n, :])
        ins.then_inc(s.c1_m, 1)

    def q2(p, im):
        dve.wait_ge(s.c1_mt, 2 * p + im + 1)
        if im == 1:
            dve.wait_ge(s.c1_st, 4 * p + 2)
        for i in range(2):
            at = im * PLACES + i * P
            mt = m.ps[:, 6 + i, :].bitcast(BF16)[:, 0:BLOCKS * P].rearrange("p (b q) -> p b q", b=BLOCKS)
            ins = dve.tensor_tensor(m.q2[:, :, i * P:(i + 1) * P], m.qs[:, :, at:at + P], mt, ALU.add)
        ins.then_inc(s.c1_q2, 1)

    def normalise(p, im):
        t = slice(2 * im, 2 * im + 2)
        dve.wait_ge(s.c1_em, 2 * p + im + 1)
        o.then(dve.tensor_tensor(m.den[:, t, :], m.emax[:, t, :], m.padn[:, :].rearrange("p (t h) -> p t h", t=2),
                                 ALU.mult))
        dve.wait_ge(s.c1_o, 2 * p + im + 3)
        out = m.ps[:, 7, 0:2 * HEADS * 9].rearrange("p (t h d) -> p t h d", t=2, d=9)
        o.then(dve.tensor_tensor(m.den[:, t, :], m.den[:, t, :], out[:, :, :, HD], ALU.add))
        o.then(dve.reciprocal(m.rden[:, t, :], m.den[:, t, :]))
        dve.tensor_tensor(m.att[:, t, :].rearrange("p t (h d) -> p t h d", d=HD), out[:, :, :, 0:HD],
                          bcast(m.rden[:, t, :].unsqueeze(3), [P, 2, HEADS, HD]), ALU.mult).then_inc(s.c1_on, 1)

    def add(p):
        dve.wait_ge(s.c1_y, p + 1)
        x = m.X[:, bass.ds(p * PT, PT), :]
        dve.tensor_tensor(x, x, m.ps[:, 7, 0:PT * C].rearrange("p (t c) -> p t c", c=C), ALU.add)\
            .then_inc(s.c1_added, 1)

    def turn(p, behind, ahead):
        if behind:
            normalise(p - 1, 1)
        maxima(p, 0)
        if ahead:
            stats(p + 1)
        maxima(p, 1)
        with_padding(p, 0)
        if behind:
            add(p - 1)
        maxima(p, 2)
        if ahead:
            norm(p + 1)
        q2(p, 0)
        maxima(p, 3)
        with_padding(p, 1)
        q2(p, 1)
        if ahead:
            rest(p + 1)
        normalise(p, 0)
        if ahead:
            queries(p + 1)

    stats(0)
    norm(0, True)
    rest(0)
    queries(0)
    turn(0, False, True)
    with o.turns(PAIRS - 2, 18) as i:
        turn(i + 1, True, True)
    turn(PAIRS - 1, True, False)
    normalise(PAIRS - 1, 1)
    add(PAIRS - 1)


def clear(pool, q):
    for sem in q:
        pool.sem_clear(sem)


def c1_pool(pool, nc, m, s):
    clear(pool, s.ffn[0])
    o = m.pool_order
    pool.sem_inc(s.c1_vals, 1)

    def rstd(p):
        wait_apart(pool, m, s.c1_mv, p + 1)
        ln_rstd(pool, o, m, PT, 1e-6, s.c1_rstd)

    def vals(p):
        pool.wait_ge(s.c1_v_read, p + 1)
        wait_apart(pool, m, s.c1_o, 2 * p + 2)
        pool.tensor_copy(m.vals[:, :, :, 0:HD], m.vals_next[:, :, :].rearrange("p t (h d) -> p t h d", d=HD))\
            .then_inc(s.c1_vals, 1)

    rstd(0)
    vals(0)
    with o.turns(PAIRS - 1, 1) as p:
        rstd(p + 1)
        vals(p + 1)



def c2_pe(pe, nc, m, s):
    pe.sem_inc(s.c2_y, 1)

    def tokens(p):
        pe.wait_ge(s.c2_xn, p + 1)
        wait_apart(pe, m, s.c2_xf, p + 1)
        for t in range(PT):
            ins = pe.transpose(m.ps[0:C, 0, t * P:(t + 1) * P], m.xn[:, t, :], m.ident[:])
        ins.then_inc(s.c2_nt, 1)

    def inverse_norms(p):
        pe.wait_ge(s.c2_diag, p + 1)
        pe.wait_ge(s.c2_inv, 2 * p + 1)
        pe.matmul(m.ps[:, 2, :], m.one[:, :], m.diag.rearrange("p t q -> p (t q)"), start=True, stop=True)\
            .then_inc(s.c2_nq, 1)

    def turn(p, ahead):
        pe.wait_ge(s.c2_xf, p + 2)
        pe.wait_ge(s.c2_relu, 2 * p + 1)
        for im in range(2):
            for i in range(2):
                at = im * PLACES
                ins = pe.matmul(m.ps[:, 3 + im, i * PLACES:(i + 1) * PLACES],
                                m.xf[0:C, at + i * P:at + (i + 1) * P], m.xf[0:C, at:at + PLACES],
                                start=True, stop=True)
            ins.then_inc(s.c2_dots, 1)
        pe.wait_ge(s.c2_tx, p + 1)
        for t in range(PT):
            ins = pe.matmul(m.ps[:, 1, t * C:(t + 1) * C], m.xf[:, t * P:(t + 1) * P], m.w_l2[:, :],
                            start=True, stop=True)
        ins.then_inc(s.c2_lin, 1)
        if ahead:
            tokens(p + 1)
            inverse_norms(p + 1)
        pe.wait_ge(s.c2_tx, p + 2)
        pe.wait_ge(s.c2_added, p + 1)
        for im in range(2):
            pe.wait_ge(s.c2_sim, 2 * p + im + 1)
            for i in range(2):
                for k in range(2):
                    ins = pe.matmul(m.ps[:, 5, (2 * im + i) * C:(2 * im + i + 1) * C],
                                    m.sim[:, im, k, i * P:(i + 1) * P], m.tx[:, 2 * im + k, :],
                                    start=(k == 0), stop=(k == 1))
        ins.then_inc(s.c2_y, 1)

    tokens(0)
    inverse_norms(0)
    with pe.Fori(0, PAIRS - 1) as p:
        turn(p, True)
    turn(PAIRS - 1, False)


def c2_act(act, nc, m, s):
    for sem in (s.c2_relu, s.c2_tx, s.c2_xf):
        act.sem_inc(sem, 1)

    def features(p):
        act.wait_ge(s.c2_nt, p + 1)
        act.activation(m.xf[0:C, :], m.ps[0:C, 0, :], ACT.Copy).then_inc(s.c2_xf, 1)

    def turn(p, ahead):
        act.wait_ge(s.c2_y, p + 1)
        for im in range(2):
            act.wait_ge(s.c2_dots, 2 * p + im + 1)
            act.activation(m.relu[:, im, :], m.ps[:, 3 + im, :], ACT.Relu).then_inc(s.c2_relu, 1)
        act.wait_ge(s.c2_lin, p + 1)
        act.activation(m.tx[:, :, :], m.ps[:, 1, 0:PT * C].rearrange("p (t c) -> p t c", c=C), ACT.Copy)\
            .then_inc(s.c2_tx, 1)
        for im in range(2):
            act.wait_ge(s.c2_relu, 2 * p + im + 2)
            act.activation(m.relu2[:, im, :], m.relu[:, im, :], ACT.Square).then_inc(s.c2_sq, 1)
        if ahead:
            features(p + 1)

    features(0)
    with act.Fori(0, PAIRS - 1) as p:
        turn(p, True)
    turn(PAIRS - 1, False)


def c2_dve(dve, nc, m, s):
    for sem in (s.c2_inv, s.c2_added):
        dve.sem_inc(sem, 1)
    o = m.dve_order

    def stats(p):
        ln_stats(dve, o, m, m.X[:, bass.ds(p * PT, PT), :], PT, s.c2_mv)

    def norm(p, first=False):
        dve.wait_ge(s.c2_rstd, p + 1)
        if not first:
            dve.wait_ge(s.c2_nt, p)
        ln_apply(dve, o, m, m.X[:, bass.ds(p * PT, PT), :], PT, s.c2_xn)
        dve.wait_ge(s.c2_xn, p + 1)
        o.then(dve.tensor_tensor(m.xc[:, 0:PT, :], m.xn[:, 0:PT, :], m.xn[:, 0:PT, :], ALU.mult))
        o.then(dve.tensor_reduce(m.n2[:, 0:PT], m.xc[:, 0:PT, :], AX, ALU.add))
        o.then(dve.tensor_scalar(m.n2[:, 0:PT], m.n2[:, 0:PT], 1e-30, None, ALU.max))
        if not first:
            dve.wait_ge(s.c2_inv, 2 * p + 1)
            dve.wait_ge(s.c2_nq, p)
        o.then(dve.reciprocal(m.rn2[:, :], m.n2[:, 0:PT]))
        dve.tensor_tensor(m.diag, bcast(m.ident[:, :].unsqueeze(1), [P, PT, P]),
                          bcast(m.rn2[:, :].unsqueeze(2), [P, PT, P]), ALU.mult).then_inc(s.c2_diag, 1)

    def inverses(p):
        dve.wait_ge(s.c2_nq, p + 1)
        for im in range(2):
            for i in range(2):
                ins = dve.tensor_scalar(m.inv[:, im, i * PLACES:(i + 1) * PLACES],
                                        m.ps[:, 2, im * PLACES:(im + 1) * PLACES],
                                        m.rn2[:, 2 * im + i:2 * im + i + 1], 1e16, ALU.mult, ALU.min)
            ins.then_inc(s.c2_inv, 1)

    def turn(p, ahead):
        if ahead:
            stats(p + 1)
        inverses(p)
        if ahead:
            norm(p + 1)
        for im in range(2):
            dve.wait_ge(s.c2_inv, 2 * p + im + 2)
            dve.wait_ge(s.c2_sq, 2 * p + im + 1)
            dve.tensor_tensor(m.sim[:, im, :, :].rearrange("p k q -> p (k q)"), m.relu2[:, im, :], m.inv[:, im, :],
                              ALU.mult).then_inc(s.c2_sim, 1)
        dve.wait_ge(s.c2_y, p + 2)
        x = m.X[:, bass.ds(p * PT, PT), :]
        dve.tensor_tensor(x, x, m.ps[:, 5, 0:PT * C].rearrange("p (t c) -> p t c", c=C), ALU.add)\
            .then_inc(s.c2_added, 1)

    stats(0)
    norm(0, True)
    with o.turns(PAIRS - 1, 6) as p:
        turn(p, True)
    turn(PAIRS - 1, False)


def c2_pool(pool, nc, m, s):
    clear(pool, s.ffn[1])
    o = m.pool_order
    with o.turns(PAIRS, 1) as p:
        wait_apart(pool, m, s.c2_mv, p + 1)
        ln_rstd(pool, o, m, PT, 1e-6, s.c2_rstd)



def c3_pe(pe, nc, m, s):
    for sem in (s.c3_t, s.c3_nt, s.c3_dots, s.c3_y):
        pe.sem_inc(sem, 1)

    def tokens(p):
        pe.wait_ge(s.c3_xn2, p + 1)
        pe.wait_ge(s.c3_xm, p + 1)
        for t in range(PT):
            ins = pe.transpose(m.ps[:, 0, t * P:(t + 1) * P], m.xn2[:, t, :, :].rearrange("p a c -> p (a c)"),
                               m.ident[:])
        ins.then_inc(s.c3_nt, 1)

    with pe.Fori(0, PAIRS) as p:
        tokens(p)
        pe.wait_ge(s.c3_xm, p + 2)
        pe.wait_ge(s.c3_t_kept, p + 1)
        for im in range(2):
            ins = pe.matmul(m.ps[:, 1, im * PLACES:(im + 1) * PLACES].rearrange("p (c b) -> p c b", b=4), m.w_l3[:, :],
                            m.xm[0:C, im, :, :].rearrange("p b c -> p c b"), start=True, stop=True)
        ins.then_inc(s.c3_t, 1)
    pe.wait_ge(s.c3_sumsq, 1)
    pe.matmul(m.ps[:, 2, 0:IMAGES], m.one[:, :], m.sumsq[:, :], start=True, stop=True).then_inc(s.c3_norm, 1)

    def outputs(r, im):
        pe.wait_ge(s.c3_sq, 2 * r + im + 2)
        for par in range(2):
            for k in range(2):
                ins = pe.matmul(m.ps[par * C:(par + 1) * C, 5, im * P:(im + 1) * P], m.tr[:, im, k, :],
                                m.sim3[:, par, im, k, :], start=(k == 0), stop=(k == 1))
        return ins

    def turn(r, ahead):
        pe.wait_ge(s.c3_xm, r + PAIRS + 2)
        pe.wait_ge(s.c3_relu, 2 * r + 1)
        for im in range(2):
            for par in range(2):
                rows = slice(par * C, (par + 1) * C)
                for k in range(2):
                    ins = pe.matmul(m.ps[:, 3 + 3 * im + par, k * P:(k + 1) * P],
                                    m.xm[rows, im, 2 * k:2 * k + 2, :].rearrange("p b c -> p (b c)"),
                                    m.xn2[rows, 2 * im:2 * im + 2, 0, :], start=True, stop=True)
            ins.then_inc(s.c3_dots, 1)
        pe.wait_ge(s.c3_tr, r + 1)
        pe.wait_ge(s.c3_added, r + 1)
        outputs(r, 0)
        if ahead:
            tokens(r + PAIRS + 1)
        outputs(r, 1).then_inc(s.c3_y, 1)

    tokens(PAIRS)
    with pe.Fori(0, PAIRS - 1) as r:
        turn(r, True)
    turn(PAIRS - 1, False)


def c3_act(act, nc, m, s):
    for sem in (s.c3_xm, s.c3_relu, s.c3_t_kept):
        act.sem_inc(sem, 1)

    def places(p):
        act.wait_ge(s.c3_nt, p + 2)
        act.activation(m.xm[:, :, :, :], m.ps[:, 0, :].rearrange("p (im c b) -> p im b c", im=2, b=4),
                       ACT.Copy).then_inc(s.c3_xm, 1)

    def twice(p, q, sem, value):
        wait_apart(act, m, sem, value)
        act.activation(m.xn2[:, :, :, :].rearrange("p t a c -> p a t c"),
                       bcast(m.normal[:, bass.ds(q * PT, PT), :].unsqueeze(1), [P, 2, PT, C]), ACT.Copy)\
            .then_inc(s.c3_xn2, 1)

    def first(p, ahead):
        act.wait_ge(s.c3_t, p + 1)
        places(p)
        if ahead:
            twice(p + 1, p + 1, s.c3_xn, p + 2)
        wait_apart(act, m, s.c3_t, p + 2)
        act.activation(m.t[:, bass.ds(p, 1), :].rearrange("p a n -> p (a n)"), m.ps[:, 1, :], ACT.Copy)\
            .then_inc(s.c3_t_kept, 1)

    twice(0, 0, s.c3_xn, 1)
    with act.Fori(0, PAIRS - 1) as p:
        first(p, True)
    first(PAIRS - 1, False)

    def second(r, ahead):
        wait_apart(act, m, s.c3_y, r + 1)
        for half in range(2):
            rows = slice(half * C, (half + 1) * C)
            t = m.t[rows, bass.ds(r, 1), :].rearrange("p a (im k b o) -> p (a im) k b o", im=2, k=2, b=2)[:, :, :, half, :]
            ins = act.activation(m.tr[rows, :, :, :], t, ACT.Relu, scale=m.bn_scale[rows, :],
                                 bias=m.bn_shift[rows, :])
        ins.then_inc(s.c3_tr, 1)
        act.wait_ge(s.c3_inv, r + 1)
        for im in range(2):
            act.wait_ge(s.c3_dots, 2 * r + im + 2)
            act.wait_ge(s.c3_sq, 2 * r + 1)
            for par in range(2):
                ins = act.activation(m.relu[:, im, par * 2 * P:(par + 1) * 2 * P],
                                     m.ps[:, 3 + 3 * im + par, 0:2 * P], ACT.Relu, scale=m.inv3[:, im:im + 1])
            ins.then_inc(s.c3_relu, 1)
        if ahead:
            twice(r + PAIRS + 1, r + 1, s.c3_dots, 2 * r + 3)
            places(r + PAIRS + 1)

    act.wait_ge(s.c3_nt, PAIRS + 1)
    twice(PAIRS, 0, s.c3_shift, 1)
    places(PAIRS)
    with act.Fori(0, PAIRS - 1) as r:
        second(r, True)
    second(PAIRS - 1, False)


def c3_dve(dve, nc, m, s):
    for sem in (s.c3_added, s.c3_sq):
        dve.sem_inc(sem, 1)
    o = m.dve_order

    def stats(p):
        ln_stats(dve, o, m, m.X[:, bass.ds(p * PT, PT), :], PT, s.c3_mv)

    def moments(p):
        wait_apart(dve, m, s.c3_t_kept, p + 2)
        dve.bn_stats(m.bstats[:, bass.ds(p, 1), :].rearrange("p a b -> p (a b)"),
                     m.t[:, bass.ds(p, 1), :].rearrange("p a n -> p (a n)"))\
            .then_inc(s.c3_t_read, 1)

    def first(p, behind, ahead):
        x, xn = m.X[:, bass.ds(p * PT, PT), :], m.normal[:, bass.ds(p * PT, PT), :]
        dve.wait_ge(s.c3_rstd, p + 1)
        o.then(dve.tensor_tensor(m.xc[:, 0:PT, :], x, bcast(m.mv[:, 0:PT, 0:1], [P, PT, C]), ALU.subtract))
        dve.tensor_tensor(xn, m.xc[:, 0:PT, :], bcast(m.rstd[:, 0:PT].unsqueeze(2), [P, PT, C]), ALU.mult)\
            .then_inc(s.c3_xn, 1)
        if ahead:
            stats(p + 1)
        dve.wait_ge(s.c3_xn, p + 1)
        o.then_apart(dve.tensor_tensor(m.xc[:, 0:PT, :], xn, xn, ALU.mult), m)
        ins = dve.tensor_reduce(m.sumsq[:, bass.ds(2 * p, 2)], m.xc[:, 0:PT, :].rearrange("p (im t) c -> p im (t c)", im=2),
                                AX, ALU.add)
        o.then(ins)
        if behind:
            moments(p - 1)

    stats(0)
    first(0, False, True)
    with o.turns(PAIRS - 2, 4) as i:
        first(i + 1, True, True)
    first(PAIRS - 1, True, False)
    dve.drain().then_inc(s.c3_sumsq, 1)
    moments(PAIRS - 1)
    dve.wait_ge(s.c3_t_read, PAIRS)
    dve.bn_aggr(m.bmv[:, :], m.bstats[:, :, :].rearrange("p a b -> p (a b)")).then_inc(s.c3_bmv, 1)
    dve.wait_ge(s.c3_norm, 1)
    o.then(dve.reciprocal(m.inv_all[:, :], m.ps[:, 2, 0:IMAGES]))
    dve.wait_ge(s.c3_bmv, 1)
    o.then(dve.tensor_tensor(m.bn_mean[:, :], m.bmv[:, 0:1], m.bn_in[:, 0:1], ALU.add))
    o.then(dve.tensor_tensor(m.bn_shift[:, :], m.bn_in[:, 0:1], m.bn_mean[:, :], ALU.subtract))
    dve.wait_ge(s.c3_brstd, 1)
    o.then(dve.tensor_tensor(m.bn_scale[:, :], m.brstd[:, :], m.bn_in[:, 1:2], ALU.mult))
    o.then(dve.tensor_tensor(m.bn_shift[:, :], m.bn_shift[:, :], m.bn_scale[:, :], ALU.mult))
    dve.tensor_tensor(m.bn_shift[:, :], m.bn_shift[:, :], m.bn_in[:, 2:3], ALU.add).then_inc(s.c3_shift, 1)

    def inverse_norms(r):
        dve.tensor_copy(m.inv3[:, :], m.inv_all[:, bass.ds(2 * r, 2)]).then_inc(s.c3_inv, 1)

    def second(r, ahead):
        for im in range(2):
            dve.wait_ge(s.c3_relu, 2 * r + im + 2)
            dve.wait_ge(s.c3_y, r + 1)
            src = m.relu[:, im, :].rearrange("p (a k n) -> p a (k n)", a=2, k=2)
            dve.tensor_tensor(m.sim3[:, :, im, :, :].rearrange("p a k n -> p a (k n)"), src, src, ALU.mult)\
                .then_inc(s.c3_sq, 1)
        if ahead:
            inverse_norms(r + 1)
        dve.wait_ge(s.c3_y, r + 2)
        x = m.X[:, bass.ds(r * PT, PT), :]
        dve.tensor_tensor(x, x, m.ps[:, 5, 0:PT * C].rearrange("p (t c) -> p t c", c=C), ALU.add)\
            .then_inc(s.c3_added, 1)

    inverse_norms(0)
    with dve.Fori(0, PAIRS - 1) as r:
        second(r, True)
    second(PAIRS - 1, False)


def c3_pool(pool, nc, m, s):
    o = m.pool_order
    with o.turns(PAIRS, 1) as p:
        wait_apart(pool, m, s.c3_mv, p + 1)
        ln_rstd(pool, o, m, PT, 1e-6, s.c3_rstd)
    pool.wait_ge(s.c3_bmv, 1)
    o.then(pool.tensor_scalar(m.bveps[:, :], m.bmv[:, 1:2], 1e-5, 1.0, ALU.add, ALU.mult))
    pool.tensor_tensor(m.brstd[:, :], m.bveps[:, :], m.minus_half[:, 0:1], ALU.pow).then_inc(s.c3_brstd, 1)



def prepare_pe(pe, nc, m, s):
    pe.wait_ge(s.ld_small, 16 * SMALL_LOADS)
    pe.wait_ge(s.ld_ident, 16)
    for k, (slot, n) in enumerate(((3, 65), (4, 65), (5, 64), (6, 65), (7, 64), (1, 65), (2, 65))):
        pe.transpose(m.ps[0:n, 6, k * C:(k + 1) * C], m.nat[0:C, slot, 0:n], m.ident[0:C, 0:C])
    pe.transpose(m.ps[:, 7, 0:B1ROWS], m.b1nat[:, :], m.ident[0:B1ROWS, 0:B1ROWS]).then_inc(s.weights_t, 1)


def prepare_act(act, nc, m, s):
    act.wait_ge(s.weights_t, 1)
    act.wait_ge(s.padded, 1)
    act.activation(m.wqk[:, 0:C], m.ps[0:C + 1, 6, 5 * C:6 * C], ACT.Copy, scale=SCALE)
    act.activation(m.wqk[:, C:2 * C], m.ps[0:C + 1, 6, 6 * C:7 * C], ACT.Copy)
    act.activation(m.wv[:, :], m.ps[0:C + 1, 6, 0:C], ACT.Copy)
    act.activation(m.wpn[:, :], m.ps[0:C + 1, 6, C:2 * C], ACT.Copy)
    act.activation(m.wpp[:, :], m.ps[0:C, 6, 2 * C:3 * C], ACT.Copy)
    act.activation(m.w_l2[:, :], m.ps[0:C + 1, 6, 3 * C:4 * C], ACT.Copy)
    for k in range(2):
        act.activation(m.w_l3[:, k * C:(k + 1) * C], m.ps[0:C, 6, 4 * C:5 * C], ACT.Copy)
    act.activation(m.b1t[:, :], m.ps[:, 7, 0:B1ROWS], ACT.Copy)
    act.activation(m.mask[:, :], m.mask_in, ACT.Copy, scale=NEG)
    act.activation(m.identb[:, :], m.ident[:, :], ACT.Copy).then_inc(s.prepared, 1)


def split_b2(dve, m, s, o, l):
    rows = slice(E2[l], E2[l] + FFN[l]["E"])
    b2, parts, neg = m.b2[:, rows, :], m.b2p[:, rows, :], m.partsel[:, 2:4]
    dve.wait_ge(s.ld_small, 16 * SMALL_LOADS)
    for k in range(2):
        o.then(dve.tensor_copy(parts, b2))
        o.then(dve.scalar_tensor_tensor(b2, parts, neg[:, k:k + 1], b2, ALU.mult, ALU.add))
    dve.tensor_copy(parts, b2).then_inc(s.b2_split, 1)



def out_dve(dve, nc, m, s):
    with dve.Fori(0, PAIRS) as g:
        dve.wait_ge(s.out_t, g + 1)
        x = m.X[:, bass.ds(g * PT, PT), :]
        dve.tensor_copy(m.stage[:, :, :, :], x.rearrange("p (a i) c -> p i a c", i=2)).then_inc(s.out_x, 1)


def out_pe(pe, nc, m, s):
    pe.sem_inc(s.out_t, 1)
    pe.sem_inc(s.out_y, 1)
    with pe.Fori(0, PAIRS) as g:
        pe.wait_ge(s.out_x, g + 1)
        pe.wait_ge(s.out_y, g + 1)
        for i in range(2):
            ins = pe.transpose(m.ps[:, 0, i * P:(i + 1) * P], m.stage[:, i, :, :], m.ident[:])
        ins.then_inc(s.out_t, 1)


def out_act(act, nc, m, s):
    with act.Fori(0, PAIRS) as g:
        act.wait_ge(s.out_t, g + 2)
        act.activation(m.y[:, bass.ds(g, 1), :].rearrange("p a n -> p (a n)"), m.ps[:, 0, 0:PLACES], ACT.Copy).then_inc(s.out_y, 1)


def out_sync(sp, nc, m, s, out):
    y = out.rearrange("(g a) c h w -> g (a c) (h w)", a=2)
    with sp.Fori(0, PAIRS) as g:
        sp.wait_ge(s.out_y, g + 2)
        sp.dma_start(y[bass.ds(g, 1), :, :].rearrange("g p w -> p (g w)"),
                     m.y[:, bass.ds(g, 1), :].rearrange("p a n -> p (a n)")).then_inc(s.out_sent, 16)
    sp.wait_ge(s.out_sent, 16 * PAIRS)


FFN_SEMS = ["mv", "rstd", "xn", "part1", "rest", "part2", "parts", "transposed", "xa", "xb", "logits",
            "logits_read", "hidden", "act", "silu", "down", "weighed", "added", "below_max", "exps",
            "order", "pool_order"]
SEMS = ["ld_ident", "ld_first", "ld_up", "ld_small", "codes_t", "codes_sq", "codes_n", "codes_ready", "codes_1", "codes_2", "codes_rest", "c0_z1", "c0_z2", "c0_rest",
        "c0_in",
        "c2_mv", "c2_rstd", "c2_xn", "c2_nt", "c2_xf", "c2_nq", "c2_inv", "c2_relu", "c2_dots", "c2_diag", "c2_tx", "c2_lin", "c2_added", "c2_sim", "c2_y", "c2_sq", 
        "c3_mv", "c3_rstd", "c3_xn", "c3_xn2", "c3_nt", "c3_xm", "c3_t", "c3_t_read", "c3_t_kept", "c3_bmv", "c3_brstd", "c3_shift", "c3_sumsq", "c3_norm", "c3_inv", "c3_dots", "c3_relu", "c3_tr", "c3_sq", "c3_y", "c3_added", 
        "c1_mv", "c1_rstd", "c1_xn", "c1_nt", "c1_xf", "c1_qk", "c1_vals", "c1_part1", "c1_part2", "c1_part3", "c1_rest", "c1_selq", "c1_selk", "c1_qs", "c1_ks", "c1_v", "c1_v_read", "c1_s", "c1_max", "c1_m", "c1_mt", "c1_q2", "c1_st", "c1_p", "c1_o", "c1_em", "c1_on", "c1_ot", "c1_ot_read", "c1_y", "c1_added", "c0_xt", "c0_mv", "c0_rstd", "c0_xn", "c0_nt", "c0_xf", "c0_zp", "c0_z", "c0_read",
        "c0_scored", "ones_rows", "split_a", "split_r", "split_b", 
        "weights_t", "b2_split", "padded", "prepared", "out_t", "out_x", "out_y", "out_sent", "part_done", "apart",
        "dve_order", "pool_order"]


FfnSems = namedtuple("FfnSems", FFN_SEMS)
Sems = namedtuple("Sems", SEMS + ["c0_gathered", "ffn"])


class Memory:
    pass


def program(nc, d, out):
    with ExitStack() as ctx:
        m = Memory()

        def sb(name, shape, dt=F32):
            return ctx.enter_context(nc.sbuf_tensor(name, shape, dt))

        new = lambda name: ctx.enter_context(nc.semaphore(name))
        s = Sems(*[new(n) for n in SEMS],
                 c0_gathered=[new(f"c0_gathered{j}") for j in range(PT)],
                 ffn=[FfnSems(*[new(f"ffn{l}_{n}") for n in FFN_SEMS]) for l in range(2)] * 2)
        m.apart = s.apart
        m.ps = ctx.enter_context(nc.psum_tensor("ps", [P, 8, 512], F32))
        m.X = sb("X", [P, TILES, C])
        m.ident = sb("ident", [P, P])
        m.identb = sb("identb", [P, P], BF16)
        m.nat = sb("nat", [C, 8, C + 1])
        m.emb = sb("emb", [P, CODES // P, 2, C])
        m.rest_of_codes = sb("rest_of_codes", [P, CODES])
        m.norm_parts = sb("norm_parts", [3, CODES], BF16)
        m.proj0 = sb("proj0", [C + 1, 2 * C])
        m.minus_one = sb("minus_one", [P, C + 1])
        m.minus_half = sb("minus_half", [P, ST])
        m.xload = sb("xload", [P, PLACES])
        m.stats = sb("stats", [P, ST, 6])
        m.mv = sb("mv", [P, ST, 2])
        m.veps = sb("veps", [P, ST])
        m.rstd = sb("rstd", [P, ST])
        m.xc = sb("xc", [P, ST, C])
        m.xn = sb("xn", [P, ST, C])
        m.xf = sb("xf", [C + 1, 512])
        m.best = sb("best", [P, PT, 8])
        m.code = sb("code", [P, PT, 8], U32)
        m.zq = [sb(f"zq{j}", [P, C]) for j in range(PT)]
        m.wall = sb("wall", [P, WPAD + 8])
        m.w1 = sb("w1", [P, WPAD], BF16)
        m.w2 = sb("w2", [P, WPAD], BF16)
        m.w3 = sb("w3", [P, WPAD], BF16)
        m.gate_b = {l: sb(f"gate_b{l}", [P, FFN[l]["E"]]) for l in (0, 2, 3)}
        m.down = [sb(f"down{l}", [P, ffn_counts(l)[1]] + [2] * (l == 1) + [C]) for l in range(4)]
        m.b1nat = sb("b1nat", [B1ROWS, P])
        m.b1t = sb("b1t", [P, B1ROWS])
        m.b2 = sb("b2", [3, B2ROWS, C])
        m.b2p = sb("b2p", [3, B2ROWS, C], BF16)
        m.partsel = sb("partsel", [3, 4])
        m.ones3 = sb("ones3", [3, P], BF16)
        m.bn_in = sb("bn_in", [P, 3])
        m.mask = sb("mask", [P, MASK_COLS], BF16)
        m.padn = sb("padn", [P, 2 * HEADS])
        m.padmax = sb("padmax", [P, 2 * HEADS])
        m.iota = sb("iota", [P, 16])
        m.wqk = sb("wqk", [C + 1, 2 * C])
        m.wv = sb("wv", [C + 1, C])
        m.wpn = sb("wpn", [C + 1, C])
        m.wpp = sb("wpp", [C, C])
        m.w_l2 = sb("w_l2", [C + 1, C])
        m.w_l3 = sb("w_l3", [C, P])
        m.parts = sb("parts", [P, ST, 3, C], BF16)
        m.xa = sb("xa", [P, SPAN], BF16)
        m.xb = sb("xb", [P, SPAN], BF16)
        m.hid = m.wall[:, 0:2 * SPAN].rearrange("p (a n) -> p a n", a=2)
        m.silu = m.wall[:, 2 * SPAN:3 * SPAN].rearrange("p (a n) -> p a n", a=2)
        m.prod = m.wall[:, 3 * SPAN:4 * SPAN].rearrange("p (a t c) -> p a t c", a=2, t=ST)
        m.sel = m.wall[:, 4 * SPAN:4 * SPAN + 2 * 3 * BLOCKS * P // 2].bitcast(BF16).rearrange(
            "p (a k b r) -> p a k b r", a=2, k=3, b=BLOCKS)
        m.qkp = m.parts[:, :, :, :].rearrange("p t k c -> p (t k c)").rearrange("p (k n) -> p k n", k=3)
        m.qk_rest = m.xa[:, :].bitcast(F32)
        m.z_rest = m.parts[:, :, :, :].rearrange("p t k c -> p (t k c)")[:, 0:1024].bitcast(F32)
        m.normal = m.wall[:, 0:TILES * C].rearrange("p (t c) -> p t c", c=C)
        m.t = m.wall[:, TILES * C:TILES * C + PAIRS * 512].rearrange("p (g n) -> p g n", g=PAIRS)
        m.y = m.wall[:, 0:PAIRS * PLACES].rearrange("p (g n) -> p g n", g=PAIRS)
        m.xfp = sb("xfp", [C + 1, 512])
        m.qs = sb("qs", [P, BLOCKS, 512], BF16)
        m.ks = sb("ks", [P, BLOCKS, 512], BF16)
        m.q2 = sb("q2", [P, BLOCKS, PLACES], BF16)
        m.vals_next = sb("vals_next", [P, PT, C])
        m.vals = sb("vals", [P, PT, HEADS, HD + 1])
        m.maxr = sb("maxr", [P, PT, HEADS])
        m.maxp = sb("maxp", [P, PT, HEADS])
        m.maxes = sb("maxes", [P, PT, BLOCKS, P], BF16)
        m.maxparts = sb("maxparts", [P, 2, HEADS, 3], BF16)
        m.maxrest = sb("maxrest", [P, 2, HEADS])
        m.minus_rows = sb("minus_rows", [P, 1])
        m.pt = sb("pt", [P, PT, BANKS3])
        m.emax = sb("emax", [P, PT, HEADS])
        m.den = sb("den", [P, PT, HEADS])
        m.rden = sb("rden", [P, PT, HEADS])
        m.att = sb("att", [P, PT, C])
        m.ot1 = sb("ot1", [C + 1, 512])
        m.ot2 = sb("ot2", [C, 512])
        m.one = sb("one", [P, P])
        m.n2 = sb("n2", [P, PT])
        m.rn2 = sb("rn2", [P, PT])
        m.codes_a = m.ks[:, 0:2, :].rearrange("p a k -> p (a k)")
        m.codes_b = m.ks[:, 2:4, :].rearrange("p a k -> p (a k)")
        m.codes_c = m.q2[:, 0:4, :].rearrange("p a k -> p (a k)")
        m.codes_sq = m.pt[0:C, 0, 0:CODES]
        m.norms = m.pt[0:3, 3, 0:CODES]
        m.wrest = m.pt[:, 1, 0:WCHUNK]
        m.mask_in = m.pt[:, 2, 0:MASK_COLS]
        room = m.pt[:, :, :].rearrange("p t k -> p (t k)")
        m.diag = room[:, 0:PT * P].rearrange("p (t q) -> p t q", q=P)
        m.d2, m.inv, m.relu, m.relu2, m.sim = (
            room[:, k * 1024:(k + 1) * 1024].rearrange("p (im q) -> p im q", im=2) for k in range(5))
        m.sim3 = m.d2.rearrange("p im q -> p (im q)").rearrange("p (a im k n) -> p a im k n", a=2, im=2, k=2)
        m.sim = m.sim.rearrange("p im (k q) -> p im k q", k=2)
        m.tx = sb("tx", [P, PT, C])
        m.xn2 = sb("xn2", [P, PT, 2, C])
        m.xm = sb("xm", [P, 2, 4, C])
        m.tr = sb("tr", [P, 2, 2, C])
        m.inv3 = sb("inv3", [P, 2])
        m.inv_all = sb("inv_all", [P, IMAGES])
        m.sumsq = sb("sumsq", [P, IMAGES])
        m.bstats = sb("bstats", [P, PAIRS, 6])
        m.bmv = sb("bmv", [P, 2])
        m.bn_mean, m.bn_scale, m.bn_shift, m.brstd, m.bveps = (
            sb(name, [P, 1]) for name in ("bn_mean", "bn_scale", "bn_shift", "brstd", "bveps"))
        m.lg = sb("lg", [P, ST, 16])
        m.below = sb("below", [P, ST, 17])
        m.ex = sb("ex", [P, ST, 17])
        m.top = sb("top", [P, ST, 8])
        m.topi = sb("topi", [P, ST, 8], U32)
        m.topf = sb("topf", [P, ST, 2])
        m.hit = sb("hit", [P, 2, ST, 16])
        m.sums = sb("sums", [P, ST])
        m.rsum = sb("rsum", [P, ST])
        m.prob = sb("prob", [P, 2, ST])
        m.cw = sb("cw", [P, ST, 16])
        m.stage = sb("stage", [P, 2, 2, C])
        block = ctx.enter_context(nc.Block())

        @block.sync
        def _(sp):
            load_first(sp, nc, m, s, d)

            def pair(g):
                sp.wait_ge(s.c0_xt, g)
                sp.dma_start(m.xload[:, :], pair_of_images(d.x, g)).then_inc(s.c0_in, 16)

            load_rest(sp, nc, m, s, d, lambda: pair(1))
            with sp.Fori(2, PAIRS) as g:
                pair(g)
            out_sync(sp, nc, m, s, out)

        @block.tensor
        def _(pe):
            c0_pe(pe, nc, m, s)
            prepare_pe(pe, nc, m, s)
            barrier(pe, s, 1)
            ffn_pe(pe, nc, m, s, 0)
            barrier(pe, s, 2)
            c1_pe(pe, nc, m, s)
            barrier(pe, s, 3)
            ffn_pe(pe, nc, m, s, 1)
            barrier(pe, s, 4)
            c2_pe(pe, nc, m, s)
            barrier(pe, s, 5)
            ffn_pe(pe, nc, m, s, 2)
            barrier(pe, s, 6)
            c3_pe(pe, nc, m, s)
            barrier(pe, s, 7)
            ffn_pe(pe, nc, m, s, 3)
            barrier(pe, s, 8)
            out_pe(pe, nc, m, s)

        @block.scalar
        def _(act):
            c0_act(act, nc, m, s)
            prepare_act(act, nc, m, s)
            barrier(act, s, 1)
            ffn_act(act, nc, m, s, 0)
            barrier(act, s, 2)
            c1_act(act, nc, m, s)
            barrier(act, s, 3)
            ffn_act(act, nc, m, s, 1)
            barrier(act, s, 4)
            c2_act(act, nc, m, s)
            barrier(act, s, 5)
            ffn_act(act, nc, m, s, 2)
            barrier(act, s, 6)
            c3_act(act, nc, m, s)
            barrier(act, s, 7)
            ffn_act(act, nc, m, s, 3)
            barrier(act, s, 8)
            out_act(act, nc, m, s)

        @block.vector
        def _(dve):
            m.dve_order = Order(dve, s.dve_order)
            c0_dve(dve, nc, m, s)
            barrier(dve, s, 1)
            ffn_dve(dve, nc, m, s, 0)
            barrier(dve, s, 2)
            c1_dve(dve, nc, m, s)
            barrier(dve, s, 3)
            ffn_dve(dve, nc, m, s, 1)
            barrier(dve, s, 4)
            c2_dve(dve, nc, m, s)
            barrier(dve, s, 5)
            ffn_dve(dve, nc, m, s, 2)
            barrier(dve, s, 6)
            c3_dve(dve, nc, m, s)
            barrier(dve, s, 7)
            ffn_dve(dve, nc, m, s, 3)
            barrier(dve, s, 8)
            out_dve(dve, nc, m, s)

        @block.gpsimd
        def _(pool):
            m.pool_order = Order(pool, s.pool_order)
            c0_pool(pool, nc, m, s, d)
            barrier(pool, s, 1)
            ffn_pool(pool, nc, m, s, 0)
            barrier(pool, s, 2)
            c1_pool(pool, nc, m, s)
            barrier(pool, s, 3)
            ffn_pool(pool, nc, m, s, 1)
            barrier(pool, s, 4)
            c2_pool(pool, nc, m, s)
            barrier(pool, s, 5)
            ffn_pool(pool, nc, m, s, 2)
            barrier(pool, s, 6)
            c3_pool(pool, nc, m, s)
            barrier(pool, s, 7)
            ffn_pool(pool, nc, m, s, 3)
            barrier(pool, s, 8)


def attention_tables():
    mask = np.zeros((P, MASK_COLS), np.float32)
    padn = np.zeros((P, 2, HEADS), np.float32)
    for t in range(2):
        for r in range(P):
            for (ks, dil, heads), (kind, lo) in zip(RANGES, (("near", 0), ("rows", 1), ("all", 2))):
                y, x = place(kind, t, r)
                reach = ks // 2
                inside = 0
                for c in range(WIDTH[kind]):
                    ky, kx = key_place(kind, t, c)
                    dy, dx = ky - y, kx - x
                    sees = dy % dil == 0 and dx % dil == 0 and abs(dy) <= reach * dil and abs(dx) <= reach * dil
                    inside += sees
                    mask[r, t * MASK_TILE + MASK_AT[kind] + c] = not sees
                for h in heads:
                    padn[r, t, (0, 1, 2, 3, 7, 4, 5, 6).index(h)] = ks * ks - inside
    padmax = np.where(padn > 0, 0.0, -3e38).astype(np.float32)
    return mask, padn.reshape(P, -1), padmax.reshape(P, -1)


WIDTH = dict(near=160, rows=128, all=256)
MASK_AT = dict(near=0, all=160, rows=416)
MASK_TILE = 160 + 128 + 256
MASK_COLS = 2 * MASK_TILE


def place(kind, t, r):
    if kind == "rows":
        return 2 * (r // SIDE) + t, r % SIDE
    return (t * P + r) // SIDE, r % SIDE


def key_place(kind, t, c):
    if kind == "rows":
        return place(kind, t, c)
    if kind == "near":
        c += t * (PLACES - WIDTH["near"])
    return c // SIDE, c % SIDE


def constants():
    mask, padn, padmax = attention_tables()
    partsel = np.array([[0, 0, 0, 0], [1, 0, 0, 0], [1, 1, 0, 0]], np.float32)[:, :2].copy()
    minus_rows = np.zeros((P, 1), np.float32)
    for half in range(2):
        at = half * C + SPLIT_ROWS
        minus_rows[at:at + 3] = -1.0
    return dict(minus_rows=minus_rows, ident=np.eye(P, dtype=np.float32), mask_table=mask, padn=padn, padmax=padmax, partsel=partsel,
                iota=np.tile(np.arange(16, dtype=np.float32), (P, 1)))


INPUTS = [
    "x", "L0_conv_proj_w", "L0_conv_proj_b", "L0_conv_emb",
    "L0_ffn_gate_w", "L0_ffn_gate_b", "L0_ffn_W1", "L0_ffn_b1", "L0_ffn_W2", "L0_ffn_b2",
    "L1_conv_qkv_w0", "L1_conv_qkv_b0", "L1_conv_qkv_w1", "L1_conv_qkv_b1", "L1_conv_qkv_w2", "L1_conv_qkv_b2",
    "L1_conv_proj_w", "L1_conv_proj_b",
    "L1_ffn_router_w", "L1_ffn_w1", "L1_ffn_b1", "L1_ffn_w2", "L1_ffn_b2",
    "L2_conv_W", "L2_conv_bias", "L2_ffn_gate_w", "L2_ffn_gate_b", "L2_ffn_w1", "L2_ffn_w2", "L2_ffn_w3",
    "L3_conv_conv_w", "L3_conv_conv_b", "L3_conv_bn_gamma", "L3_conv_bn_beta",
    "L3_ffn_gate_w", "L3_ffn_gate_b", "L3_ffn_W1", "L3_ffn_b1", "L3_ffn_W2", "L3_ffn_b2"]


def kernel(**inputs):
    import concourse.bacc as bacc
    from concourse.bass_utils import run_bass_kernel_spmd

    nc = bacc.Bacc("TRN2", target_bir_lowering=False, num_devices=1)
    arrays, args = {}, {}
    for name, a in list({n: inputs[n] for n in INPUTS}.items()) + list(constants().items()):
        a = np.ascontiguousarray(a)
        arrays[f"in_{name}_dram"] = a
        args[name] = nc.dram_tensor(f"in_{name}_dram", a.shape, mybir.dt.from_np(a.dtype), kind="ExternalInput").ap()
    out = nc.dram_tensor("out_dram", (IMAGES, C, SIDE, SIDE), F32, kind="ExternalOutput").ap()
    program(nc, namedtuple("Inputs", list(args))(**args), out)
    r = run_bass_kernel_spmd(nc, [arrays], core_ids=[0])
    return r.results[0]["out_dram"]
```
